# Optimizing a Trainium2 kernel written in Bass

```python
import numpy as np
import jax
import jax.numpy as jnp

def _softmax(x, axis=-1):
    return jax.nn.softmax(x, axis=axis)

def _gelu(x):
    return jax.nn.gelu(x, approximate=True)

def _silu(x):
    return jax.nn.silu(x)

def _sigmoid(x):
    return jax.nn.sigmoid(x)

def _layernorm(x, axis=-1, eps=1e-05):
    m = jnp.mean(x, axis=axis, keepdims=True)
    v = jnp.var(x, axis=axis, keepdims=True)
    return (x - m) / jnp.sqrt(v + eps)

def _scatter_add(tgt, idx, src, axis=0):
    return tgt.at[idx].add(src)

def _segment_sum(src, seg, n):
    return jax.ops.segment_sum(src, seg, n)
kernel_name = 'mk_xattn_ffn_d2_seqx_r8_de5cae'

def setup_inputs(seed: int=0):
    np.random.seed(seed)
    _w = jnp.asarray

    def _rec_inputs():
        import jax
        import jax.numpy as jnp
        _rk = jax.random.key(seed)
        x = -0.0003929 + 0.9999 * jax.random.normal(jax.random.fold_in(_rk, 1), (4, 512, 128), jnp.float32)
        _lenS = 512 - jax.random.randint(jax.random.fold_in(_rk, 7), (4,), 0, max(1, 512 // 4) + 1, jnp.int32)
        _lenS2 = 32 - jax.random.randint(jax.random.fold_in(_rk, 8), (4,), 0, max(1, 32 // 4) + 1, jnp.int32)
        _ctx_768P = jax.random.normal(jax.random.fold_in(_rk, 11), (4, 16, 96), jnp.float32)
        _ctx_768c = jax.random.dirichlet(jax.random.fold_in(_rk, 511), 0.3 * jnp.ones((16,), jnp.float32), (4, 32))
        _ctx_768t = jnp.einsum('bsk,bkd->bsd', _ctx_768c, _ctx_768P)
        _ctx_768t = _ctx_768t * jax.lax.rsqrt(jnp.mean(jnp.square(_ctx_768t)) + 1e-12) * 0.953939
        ctx_768 = -7.36909e-05 + 0.999899 * (_ctx_768t + 0.3 * jax.random.normal(jax.random.fold_in(_rk, 611), (4, 32, 96), jnp.float32))
        return (x, ctx_768)
    x, ctx_768 = _rec_inputs()

    def _L0_xattn_setup():
        import jax, jax.numpy as jnp
        import numpy as np
        IMG_DIM, TXT_DIM, HID = (128, 96, 128)
        B, LQ, LK = (8, 256, 256)
        key = jax.random.key(seed)
        ks = jax.random.split(key, 8)
        s_img = 1.0 / np.sqrt(IMG_DIM)
        s_txt = 1.0 / np.sqrt(TXT_DIM)
        return {'image_features': jax.random.normal(ks[0], (B, LQ, IMG_DIM), jnp.float32), 'text_features': jax.random.normal(ks[1], (B, LK, TXT_DIM), jnp.float32), 'Wq': jax.random.uniform(ks[2], (IMG_DIM, HID), jnp.float32, -s_img, s_img), 'bq': jax.random.uniform(ks[3], (HID,), jnp.float32, -s_img, s_img), 'Wk': jax.random.uniform(ks[4], (TXT_DIM, HID), jnp.float32, -s_txt, s_txt), 'bk': jax.random.uniform(ks[5], (HID,), jnp.float32, -s_txt, s_txt), 'Wv': jax.random.uniform(ks[6], (TXT_DIM, HID), jnp.float32, -s_txt, s_txt), 'bv': jax.random.uniform(ks[7], (HID,), jnp.float32, -s_txt, s_txt)}
    _L0_xattn_all = _L0_xattn_setup()
    _L0_xattn_in = {k: v for k, v in _L0_xattn_all.items() if k in ('Wq', 'bq', 'Wk', 'bk', 'Wv', 'bv')}
    del _L0_xattn_all

    def _L0_ffn_setup():
        import jax, jax.numpy as jnp
        import numpy as np
        TOP_K = 2
        LN_EPS = 1e-05
        B, S, H, E, F = (2, 256, 128, 8, 512)

        def _layernorm(x, w, b):
            mu = jnp.mean(x, axis=-1, keepdims=True)
            var = jnp.mean(jnp.square(x - mu), axis=-1, keepdims=True)
            return (x - mu) * jax.lax.rsqrt(var + LN_EPS) * w + b
        key = jax.random.key(seed)
        ks = jax.random.split(key, 6)
        x = jax.random.normal(ks[0], (B, S, H), dtype=jnp.float32)
        Wg = jax.random.normal(ks[1], (H, E), dtype=jnp.float32) * 0.02
        alpha = jax.random.normal(ks[2], (E,), dtype=jnp.float32)
        ln_w = jnp.ones((E, H), dtype=jnp.float32)
        ln_b = jnp.zeros((E, H), dtype=jnp.float32)
        fc1_w = jax.random.normal(ks[3], (E, H, F), dtype=jnp.float32) * 0.02
        fc1_b = jnp.zeros((E, F), dtype=jnp.float32)
        fc2_w = jax.random.normal(ks[4], (E, F, H), dtype=jnp.float32) * 0.02
        fc2_b = jnp.zeros((E, H), dtype=jnp.float32)
        return {'x': x, 'Wg': Wg, 'alpha': alpha, 'ln_w': ln_w, 'ln_b': ln_b, 'fc1_w': fc1_w, 'fc1_b': fc1_b, 'fc2_w': fc2_w, 'fc2_b': fc2_b}
    _L0_ffn_all = _L0_ffn_setup()
    _L0_ffn_in = {k: v for k, v in _L0_ffn_all.items() if k in ('Wg', 'alpha', 'ln_w', 'ln_b', 'fc1_w', 'fc1_b', 'fc2_w', 'fc2_b')}
    del _L0_ffn_all

    def _L1_xattn_setup():
        import jax, jax.numpy as jnp
        import numpy as np
        NUM_HEADS = 16
        CLAMP = 10000.0
        key = jax.random.key(seed)
        ks = jax.random.split(key, 8)
        B, Nq, Nkv, Cq, Ckv = (4, 256, 256, 128, 96)
        s_q = 1.0 / np.sqrt(Cq)
        s_kv = 1.0 / np.sqrt(Ckv)
        return {'query': jax.random.normal(ks[0], (B, Nq, Cq), jnp.float32), 'key_value': jax.random.normal(ks[1], (B, Nkv, Ckv), jnp.float32), 'Wq': jax.random.normal(ks[2], (Cq, Cq), jnp.float32) * s_q, 'bq': jnp.zeros((Cq,), jnp.float32), 'Wk': jax.random.normal(ks[3], (Ckv, Cq), jnp.float32) * s_kv, 'bk': jnp.zeros((Cq,), jnp.float32), 'Wv': jax.random.normal(ks[4], (Ckv, Cq), jnp.float32) * s_kv, 'bv': jnp.zeros((Cq,), jnp.float32), 'Wo': jax.random.normal(ks[5], (Cq, Cq), jnp.float32) * s_q, 'bo': jnp.zeros((Cq,), jnp.float32)}
    _L1_xattn_all = _L1_xattn_setup()
    _L1_xattn_in = {k: v for k, v in _L1_xattn_all.items() if k in ('Wq', 'bq', 'Wk', 'bk', 'Wv', 'bv', 'Wo', 'bo')}
    del _L1_xattn_all

    def _L1_ffn_setup():
        import jax, jax.numpy as jnp
        import numpy as np
        B, T, D, E, H, K = (2, 256, 128, 8, 512, 2)
        key = jax.random.key(seed)
        ks = jax.random.split(key, 8)
        s = 0.02
        return {'x': jax.random.normal(ks[0], (B, T, D), jnp.float32), 'rw1': jax.random.normal(ks[1], (D, D), jnp.float32) * s, 'rb1': jnp.zeros((D,), jnp.float32), 'rw2': jax.random.normal(ks[2], (D, E), jnp.float32) * s, 'rb2': jnp.zeros((E,), jnp.float32), 'we1': jax.random.normal(ks[3], (E, D, H), jnp.float32) * s, 'be1': jnp.zeros((E, H), jnp.float32), 'we2': jax.random.normal(ks[4], (E, H, D), jnp.float32) * s, 'be2': jnp.zeros((E, D), jnp.float32)}
    _L1_ffn_all = _L1_ffn_setup()
    _L1_ffn_in = {k: v for k, v in _L1_ffn_all.items() if k in ('rw1', 'rb1', 'rw2', 'rb2', 'we1', 'be1', 'we2', 'be2')}
    del _L1_ffn_all
    return {'x': x, 'ctx_768': ctx_768, 'L0_xattn_Wq': _L0_xattn_in['Wq'], 'L0_xattn_bq': _L0_xattn_in['bq'], 'L0_xattn_Wk': _L0_xattn_in['Wk'], 'L0_xattn_bk': _L0_xattn_in['bk'], 'L0_xattn_Wv': _L0_xattn_in['Wv'], 'L0_xattn_bv': _L0_xattn_in['bv'], 'L0_ffn_Wg': _L0_ffn_in['Wg'], 'L0_ffn_alpha': _L0_ffn_in['alpha'], 'L0_ffn_ln_w': _L0_ffn_in['ln_w'], 'L0_ffn_ln_b': _L0_ffn_in['ln_b'], 'L0_ffn_fc1_w': _L0_ffn_in['fc1_w'], 'L0_ffn_fc1_b': _L0_ffn_in['fc1_b'], 'L0_ffn_fc2_w': _L0_ffn_in['fc2_w'], 'L0_ffn_fc2_b': _L0_ffn_in['fc2_b'], 'L1_xattn_Wq': _L1_xattn_in['Wq'], 'L1_xattn_bq': _L1_xattn_in['bq'], 'L1_xattn_Wk': _L1_xattn_in['Wk'], 'L1_xattn_bk': _L1_xattn_in['bk'], 'L1_xattn_Wv': _L1_xattn_in['Wv'], 'L1_xattn_bv': _L1_xattn_in['bv'], 'L1_xattn_Wo': _L1_xattn_in['Wo'], 'L1_xattn_bo': _L1_xattn_in['bo'], 'L1_ffn_rw1': _L1_ffn_in['rw1'], 'L1_ffn_rb1': _L1_ffn_in['rb1'], 'L1_ffn_rw2': _L1_ffn_in['rw2'], 'L1_ffn_rb2': _L1_ffn_in['rb2'], 'L1_ffn_we1': _L1_ffn_in['we1'], 'L1_ffn_be1': _L1_ffn_in['be1'], 'L1_ffn_we2': _L1_ffn_in['we2'], 'L1_ffn_be2': _L1_ffn_in['be2']}

def reference(x, ctx_768, L0_xattn_Wq, L0_xattn_bq, L0_xattn_Wk, L0_xattn_bk, L0_xattn_Wv, L0_xattn_bv, L0_ffn_Wg, L0_ffn_alpha, L0_ffn_ln_w, L0_ffn_ln_b, L0_ffn_fc1_w, L0_ffn_fc1_b, L0_ffn_fc2_w, L0_ffn_fc2_b, L1_xattn_Wq, L1_xattn_bq, L1_xattn_Wk, L1_xattn_bk, L1_xattn_Wv, L1_xattn_bv, L1_xattn_Wo, L1_xattn_bo, L1_ffn_rw1, L1_ffn_rb1, L1_ffn_rw2, L1_ffn_rb2, L1_ffn_we1, L1_ffn_be1, L1_ffn_we2, L1_ffn_be2):
    import jax
    import jax.numpy as jnp

    def _L0_xattn_ref(image_features, text_features, Wq, bq, Wk, bk, Wv, bv):
        import jax, jax.numpy as jnp
        import numpy as np
        IMG_DIM, TXT_DIM, HID = (128, 96, 128)
        B, LQ, LK = (8, 256, 256)
        query = jnp.einsum('bqi,ih->bqh', image_features, Wq) + bq
        key = jnp.einsum('bkt,th->bkh', text_features, Wk) + bk
        value = jnp.einsum('bkt,th->bkh', text_features, Wv) + bv
        scale = 1.0 / jnp.sqrt(jnp.asarray(HID, query.dtype))
        scores = jnp.einsum('bqh,bkh->bqk', query, key) * scale
        weights = jax.nn.softmax(scores, axis=-1)
        attended = jnp.einsum('bqk,bkh->bqh', weights, value)
        return attended

    def _L0_ffn_ref(x, Wg, alpha, ln_w, ln_b, fc1_w, fc1_b, fc2_w, fc2_b):
        import jax, jax.numpy as jnp
        import numpy as np
        TOP_K = 2
        LN_EPS = 1e-05
        B, S, H, E, F = (2, 256, 128, 8, 512)

        def _layernorm(x, w, b):
            mu = jnp.mean(x, axis=-1, keepdims=True)
            var = jnp.mean(jnp.square(x - mu), axis=-1, keepdims=True)
            return (x - mu) * jax.lax.rsqrt(var + LN_EPS) * w + b
        b, s, h = x.shape
        xf = x.reshape(-1, h)
        logits = xf @ Wg
        top_vals, top_idx = jax.lax.top_k(logits, TOP_K)
        gate_score = jax.nn.softmax(top_vals, axis=-1)
        one_hot = jax.nn.one_hot(top_idx, Wg.shape[1], dtype=xf.dtype)
        comb = jnp.einsum('tke,tk->te', one_hot, gate_score) * alpha
        out = jnp.zeros_like(xf)
        for e in range(Wg.shape[1]):
            hdn = _layernorm(xf, ln_w[e], ln_b[e])
            a = jax.nn.gelu(hdn @ fc1_w[e] + fc1_b[e], approximate=True)
            y = a @ fc2_w[e] + fc2_b[e]
            out = out + y * comb[:, e:e + 1]
        return out.reshape(b, s, h)

    def _L1_xattn_ref(query, key_value, Wq, bq, Wk, bk, Wv, bv, Wo, bo):
        import jax, jax.numpy as jnp
        import numpy as np
        NUM_HEADS = 16
        CLAMP = 10000.0
        B, Nq, Cq = query.shape
        Nkv = key_value.shape[1]
        H = NUM_HEADS
        D = Cq // H
        scale = D ** (-0.5)
        q = (query @ Wq + bq).reshape(B, Nq, H, D).transpose(0, 2, 1, 3)
        k = (key_value @ Wk + bk).reshape(B, Nkv, H, D).transpose(0, 2, 1, 3)
        v = (key_value @ Wv + bv).reshape(B, Nkv, H, D).transpose(0, 2, 1, 3)
        attn = jnp.einsum('bhqd,bhkd->bhqk', q, k) * scale
        attn = jnp.clip(attn, -CLAMP, CLAMP)
        attn = jax.nn.softmax(attn, axis=-1)
        attn = jnp.where(jnp.any(jnp.isnan(attn)), jnp.asarray(1.0 / Nkv, attn.dtype), attn)
        x = jnp.einsum('bhqk,bhkd->bqhd', attn, v).reshape(B, Nq, Cq)
        return x @ Wo + bo

    def _L1_ffn_ref(x, rw1, rb1, rw2, rb2, we1, be1, we2, be2):
        import jax, jax.numpy as jnp
        import numpy as np
        B, T, D, E, H, K = (2, 256, 128, 8, 512, 2)
        b, t, d = x.shape
        xt = x.reshape(b * t, d)
        n = xt.shape[0]
        logits = jax.nn.silu(xt @ rw1 + rb1) @ rw2 + rb2
        _, idx = jax.lax.top_k(logits, K)
        mask = jnp.zeros((n, E), bool).at[jnp.arange(n)[:, None], idx].set(True)
        w = jax.nn.softmax(jnp.where(mask, logits, -jnp.inf), axis=1)
        h = jax.nn.silu(jnp.einsum('nd,edh->enh', xt, we1) + be1[:, None, :])
        eo = jnp.einsum('enh,ehd->end', h, we2) + be2[:, None, :]
        y = xt + jnp.einsum('ne,end->nd', w, eo)
        return y.reshape(b, t, d)
    x = x + _L0_xattn_ref(_layernorm(x, axis=-1), ctx_768, L0_xattn_Wq, L0_xattn_bq, L0_xattn_Wk, L0_xattn_bk, L0_xattn_Wv, L0_xattn_bv)
    x = x + _L0_ffn_ref(_layernorm(x, axis=-1), L0_ffn_Wg, L0_ffn_alpha, L0_ffn_ln_w, L0_ffn_ln_b, L0_ffn_fc1_w, L0_ffn_fc1_b, L0_ffn_fc2_w, L0_ffn_fc2_b)
    x = x + _L1_xattn_ref(_layernorm(x, axis=-1), ctx_768, L1_xattn_Wq, L1_xattn_bq, L1_xattn_Wk, L1_xattn_bk, L1_xattn_Wv, L1_xattn_bv, L1_xattn_Wo, L1_xattn_bo)
    x = x + _L1_ffn_ref(_layernorm(x, axis=-1), L1_ffn_rw1, L1_ffn_rb1, L1_ffn_rw2, L1_ffn_rb2, L1_ffn_we1, L1_ffn_be1, L1_ffn_we2, L1_ffn_be2)
    return x

_drawn_inputs = setup_inputs


def setup_inputs(seed=0):
    import zlib

    import numpy as np

    out = dict(_drawn_inputs(seed))
    spreads = {'L0_ffn_ln_w': (1.0, 0.6),
     'L0_ffn_ln_b': (0.0, 0.8),
     'L0_ffn_fc1_b': (0.0, 0.622),
     'L0_ffn_fc2_b': (0.0, 0.1),
     'L1_xattn_bq': (0.0, 0.405),
     'L1_xattn_bk': (0.0, 0.8),
     'L1_xattn_bv': (0.0, 0.1),
     'L1_xattn_bo': (0.0, 0.1),
     'L1_ffn_rb1': (0.0, 0.8),
     'L1_ffn_rb2': (0.0, 0.1),
     'L1_ffn_be1': (0.0, 0.8),
     'L1_ffn_be2': (0.0, 0.1)}
    factors = {'L0_xattn_bq': 8.0,
     'L0_xattn_bk': 8.0,
     'L1_ffn_rw1': 8.0,
     'L1_ffn_rw2': 8.0,
     'L1_ffn_we1': 3.447,
     'L1_ffn_we2': 3.206}
    for name, (base, spread) in spreads.items():
        noise = np.random.default_rng([zlib.crc32(name.encode()), seed]).standard_normal(out[name].shape)
        drawn = base * np.exp(spread * noise) if base else spread * noise
        out[name] = jnp.asarray(drawn.astype(out[name].dtype))
    for name, factor in factors.items():
        out[name] = (out[name] * factor).astype(out[name].dtype)
    return out
```

```python
from contextlib import ExitStack

import concourse.bass as bass
from concourse import mybir

F32 = mybir.dt.float32
BF16 = mybir.dt.bfloat16
I32 = mybir.dt.int32
U32 = mybir.dt.uint32
ALU = mybir.AluOpType
ACT = mybir.ActivationFunctionType
AX = mybir.AxisListType

P = 128
BATCHES, SEQ, D = 4, 512, 128
TB = SEQ // P
NT = BATCHES * TB
TOKENS = BATCHES * SEQ
KEYS, CTX = 32, 96
HEADS = 16
HD = D // HEADS
GROUP = P // KEYS
E, F = 8, 512
FC = F // P
TOP = 2
EPS = 1e-5
CLAMP = 10000.0
BIG = 3.4e38
REGION = TOKENS + P
PAD_ROW = E * REGION
FFN_TILES = (TOP * TOKENS + E * (P - 1)) // P
MAP = FFN_TILES + 1
W_ROW = D + 4
AT_DEST, AT_GATE = D, D + 1
NOWHERE = 1 << 20
UNROLL = 4
LOOPS = (FFN_TILES - 2) // UNROLL
assert FFN_TILES == 39 and LOOPS == 9

R_B1, R_LNW = {0: 0, 1: E * FC}, 2 * E * FC
R_LNB = R_LNW + E
R_BQ, R_BK, R_RB1 = {0: R_LNB + E, 1: R_LNB + E + 1}, {0: R_LNB + E + 2, 1: R_LNB + E + 3}, R_LNB + E + 4
N_SMALL = R_RB1 + 1


def one(i):
    return bass.ds(i, 1)


def reached(j, n):
    return not isinstance(j, int) or j >= n


def build(nc, a, out, sent, contrib):
    with ExitStack() as ctx:
        def sb(name, shape, dt=F32):
            return ctx.enter_context(nc.sbuf_tensor(name, shape, dt))

        sems = {}

        def sem(name):
            if name not in sems:
                sems[name] = ctx.enter_context(nc.semaphore(name))
            return sems[name]

        bank = [ctx.enter_context(nc.psum_tensor(f"bank{i}", [P, 512], F32)) for i in range(8)]

        x_sb = sb("x_sb", [P, NT, D])
        ident = sb("ident", [P, P])
        ones_f = sb("ones_f", [P, P])
        ones_b = sb("ones_b", [P, P], BF16)
        earlier = sb("earlier", [P, P], BF16)
        head_mask = sb("head_mask", [P, HEADS])
        desc = sb("desc", [P, E])
        region_at = sb("region_at", [P, E])
        tile_no = sb("tile_no", [P, MAP])
        minus_half = sb("minus_half", [P, NT])
        zero_i = sb("zero_i", [P, 2], I32)
        carrier = sb("carrier", [P, 2])
        pool_carrier = sb("pool_carrier", [P, UNROLL, 2], I32)
        pad_tile = sb("pad_tile", [P, W_ROW])

        small_rows = sb("small_rows", [N_SMALL, P])
        col = sb("col", [P, N_SMALL])
        ctx_sb = sb("ctx_sb", [P, CTX])
        ctxT = sb("ctxT", [CTX, P])
        ctxT4 = sb("ctxT4", [CTX, BATCHES, GROUP, KEYS])
        wq = [sb(f"wq{l}", [D, D]) for l in range(2)]
        wk = [sb(f"wk{l}", [CTX, D]) for l in range(2)]
        wv = [sb(f"wv{l}", [CTX, D]) for l in range(2)]
        bv = [sb(f"bv{l}", [P, D]) for l in range(2)]
        wo = sb("wo", [D, D])
        bo = sb("bo", [1, TB, D])
        wg = sb("wg", [D, E])
        rw1 = sb("rw1", [D, D])
        rw2 = sb("rw2", [D, E])
        rb2 = sb("rb2", [P, E])
        alpha = sb("alpha", [P, E])
        w1 = [sb(f"w1_{l}", [D, E, F]) for l in range(2)]
        w2 = [sb(f"w2_{l}", [P, E, FC, D]) for l in range(2)]
        b1 = sb("b1", [P, E * FC])
        b2 = [sb(f"b2_{l}", [P, E, D]) for l in range(2)]

        kT = sb("kT", [D, 2, P])
        v_wide = sb("v_wide", [P, BATCHES, TB, D])
        k_wide = sb("k_wide", [P, BATCHES, HEADS, KEYS])
        v_head = sb("v_head", [P, BATCHES, HEADS, HD + 1])

        bn = sb("bn", [P, NT, 6])
        mv = sb("mv", [P, NT, 2])
        var_eps = sb("var_eps", [P, NT])
        rstd = sb("rstd", [P, NT])
        z_a = sb("z_a", [P, TB, D])
        zT_a = sb("zT_a", [P, SEQ])
        qT = sb("qT", [P, SEQ])
        top_score = sb("top_score", [P, TB])
        shifted = sb("shifted", [P, TB, KEYS])
        prob_sum = sb("prob_sum", [P, TB])
        prob_scale = sb("prob_scale", [P, TB])
        probsT = sb("probsT", [P, P])

        bn_r = sb("bn_r", [P, TB, 6])
        mv_r = sb("mv_r", [P, TB, 2])
        var_r = sb("var_r", [P, 2, TB])
        rstd_r = sb("rstd_r", [P, 2, TB])
        z_r = sb("z_r", [P, TB, D])
        zT_r = sb("zT_r", [P, SEQ])
        hidT = sb("hidT", [P, SEQ])
        logit = sb("logit", [P, TB, E])
        rest = sb("rest", [P, TB, E])
        best = sb("best", [P, TOP, TB])
        tied = sb("tied", [P, TB, E])
        key = sb("key", [P, TOP, TB])
        hot = sb("hot", [P, TOP, TB, E])
        picked = sb("picked", [P, TB, E], BF16)
        picked_now = sb("picked_now", [P, E])
        picked_before = sb("picked_before", [P, E], BF16)
        row_of = sb("row_of", [P, TB, E])
        spread = sb("spread", [P, TOP, TB, E])
        slot_f = sb("slot_f", [P, TOP, TB])
        slot = sb("slot", [P, BATCHES, TOP, TB], I32)
        gap = sb("gap", [P, TB])
        ratio = sb("ratio", [P, TB])
        total = sb("total", [P, TB])
        gate = sb("gate", [P, TOP, TB])
        alpha_hot = sb("alpha_hot", [P, TOP, TB, E])
        alpha_of = sb("alpha_of", [P, TOP, TB])
        row = sb("row", [P, NT, TOP, W_ROW])

        count = sb("count", [P, E])
        pad_at = sb("pad_at", [P, E], I32)
        count_up = sb("count_up", [P, E], I32)
        tiles_i = sb("tiles_i", [P, E], I32)
        tiles_f = sb("tiles_f", [P, E])
        tiles_end = sb("tiles_end", [P, E])
        passed = sb("passed", [P, MAP, E])
        expert_f = sb("expert_f", [P, MAP])
        first_f = sb("first_f", [P, MAP])
        expert = sb("expert", [P, MAP], I32)
        row_base = sb("row_base", [P, MAP], I32)

        xs = sb("xs", [P, UNROLL, W_ROW])
        meta = sb("meta", [P, UNROLL, 2])
        xT = sb("xT", [P, 2, P])
        w1_now = sb("w1_now", [P, 2, F])
        hid = sb("hid", [P, 2, F])
        y_raw = sb("y_raw", [P, 2, D])
        y_out = sb("y_out", [P, UNROLL, D])
        back = sb("back", [P, BATCHES, TOP, TB, D])

        max_all = sb("max_all", [P, NT, HEADS])
        max_clip = sb("max_clip", [P, NT, HEADS])
        nan_seen = sb("nan_seen", [P, NT])
        nan_junk = sb("nan_junk", [P, TB, F])
        nan_sum = sb("nan_sum", [P, 1])
        all_numbers = sb("all_numbers", [P, 1])
        qT_all = sb("qT_all", [P, BATCHES, SEQ])
        sc = sb("sc", [P, 2, HEADS, KEYS])
        pT = sb("pT", [P, 2, SEQ])
        head_scale = sb("head_scale", [P, HEADS])
        att = sb("att", [P, TB, D])
        attT = sb("attT", [P, TB, P])

        x_dram = a["x"].rearrange("b (t p) d -> p (b t) d", p=P)
        out_dram = out.rearrange("b (t p) d -> p (b t) d", p=P)
        w1_dram = [a["L0_ffn_fc1_w"], a["L1_ffn_we1"]]
        w2_dram = [a["L0_ffn_fc2_w"], a["L1_ffn_we2"]]
        b1_dram = [a["L0_ffn_fc1_b"], a["L1_ffn_be1"]]
        b2_dram = [a["L0_ffn_fc2_b"], a["L1_ffn_be2"]]
        SCALE = [float(D) ** -0.5, float(HD) ** -0.5]
        X_LOADED = 16
        N_ATTN = 5
        block = ctx.enter_context(nc.Block())

        def carry_wait(n):
            nc.vector.memset(carrier[:, n:n + 1], 0.0)

        def vec(ap):
            return ap.rearrange("(o n) -> o n", o=1)

        @block.sync
        def _(sp):
            small = [(R_B1[0], E * FC, b1_dram[0].rearrange("e (c p) -> (e c) p", p=P)),
                     (R_B1[1], E * FC, b1_dram[1].rearrange("e (c p) -> (e c) p", p=P)),
                     (R_LNW, E, a["L0_ffn_ln_w"]), (R_LNB, E, a["L0_ffn_ln_b"]),
                     (R_BQ[0], 1, vec(a["L0_xattn_bq"])), (R_BQ[1], 1, vec(a["L1_xattn_bq"])),
                     (R_BK[0], 1, vec(a["L0_xattn_bk"])), (R_BK[1], 1, vec(a["L1_xattn_bk"])),
                     (R_RB1, 1, vec(a["L1_ffn_rb1"]))]
            sp.dma_start(ctx_sb[:, :], a["ctx_768"].rearrange("b k c -> (b k) c")).then_inc(sem("ctx_loaded"), 16)
            sp.dma_start(x_sb[:, :, :], x_dram).then_inc(sem("x_loaded"), 16)
            for r, n, src in small:
                sp.dma_start(small_rows[r:r + n, :], src).then_inc(sem("small_loaded"), 16)
            for l in range(2):
                sp.dma_start(wk[l][:, :], a[f"L{l}_xattn_Wk"]).then_inc(sem("attn_loaded"), 16)
                sp.dma_start(wv[l][:, :], a[f"L{l}_xattn_Wv"]).then_inc(sem("attn_loaded"), 16)
                sp.dma_start(wq[l][:, :], a[f"L{l}_xattn_Wq"]).then_inc(sem("attn_loaded"), 16)
                sp.dma_start(bv[l][:, :], a[f"L{l}_xattn_bv"].partition_broadcast(P)).then_inc(sem("attn_loaded"), 16)
            sp.dma_start(wg[:, :], a["L0_ffn_Wg"]).then_inc(sem("router_loaded"), 16)
            sp.dma_start(alpha[:, :], a["L0_ffn_alpha"].partition_broadcast(P)).then_inc(sem("router_loaded"), 16)
            sp.dma_start(rw1[:, :], a["L1_ffn_rw1"]).then_inc(sem("router_loaded"), 16)
            sp.dma_start(rw2[:, :], a["L1_ffn_rw2"]).then_inc(sem("router_loaded"), 16)
            sp.dma_start(rb2[:, :], a["L1_ffn_rb2"].partition_broadcast(P)).then_inc(sem("router_loaded"), 16)
            sp.dma_start(wo[:, :], a["L1_xattn_Wo"]).then_inc(sem("router_loaded"), 16)
            for t in range(TB):
                sp.dma_start(bo[:, t, :], vec(a["L1_xattn_bo"])).then_inc(sem("router_loaded"), 16)
            for l in range(2):
                sp.dma_start(w1[l][:, :, :], w1_dram[l].rearrange("e d f -> d e f")).then_inc(sem(f"w_loaded{l}"), 16)
                sp.dma_start(w2[l][:, :, :, :], w2_dram[l].rearrange("e (c p) d -> p e c d", p=P)).then_inc(sem(f"w_loaded{l}"), 16)
                sp.dma_start(b2[l][:, :, :], b2_dram[l].rearrange("e d -> (e d)").partition_broadcast(P).rearrange("p (e d) -> p e d", e=E)).then_inc(sem(f"w_loaded{l}"), 16)
            sp.wait_ge(sem("pad_tile_ready"), 2)
            for l in range(2):
                sp.dma_start(sent[l][PAD_ROW:PAD_ROW + P, :], pad_tile[:, :]).then_inc(sem(f"pad_written{l}"), 16)

            for l in range(2):
                sp.wait_ge(sem(f"map_ready{l}"), 1)
                for e in range(E):
                    r = sp.value_load(pad_at[0:1, e:e + 1], min_val=0, max_val=PAD_ROW - P)
                    sp.dma_start(sent[l][bass.ds(r, P), :], pad_tile[:, :]).then_inc(sem(f"pad_written{l}"), 16)
                sp.wait_ge(sem(f"pad_written{l}"), 16 * (E + 1))
                sp.wait_ge(sem(f"rows_sent{l}"), 16 * TOP * NT)

                def load(i, c):
                    j = UNROLL * i + c
                    if reached(j, UNROLL):
                        sp.wait_ge(sem(f"x_turned{l}"), j - UNROLL + 1)
                        sp.wait_ge(sem(f"meta_ready{l}"), j - UNROLL + 1)
                    r = sp.value_load(row_base[0:1, one(j)], min_val=0, max_val=PAD_ROW)
                    sp.dma_start(xs[:, c % UNROLL, :], sent[l][bass.ds(r, P), :]).then_inc(sem(f"xs_loaded{l}_{c % UNROLL}"), 16)

                for c in range(UNROLL):
                    load(0, c)
                with sp.Fori(1, LOOPS) as i:
                    for c in range(UNROLL):
                        load(i, c)
                for j in range(UNROLL * LOOPS, FFN_TILES):
                    load(j // UNROLL, j % UNROLL)

                for u in range(UNROLL):
                    sp.wait_ge(sem(f"y_sent{l}_{u}"), 16 * len(range(u, FFN_TILES, UNROLL)))
                for b in range(BATCHES):
                    for k in range(TOP):
                        src = contrib[l][k * TOKENS + b * SEQ:k * TOKENS + (b + 1) * SEQ, :]
                        sp.dma_start(back[:, b, k, :, :], src.rearrange("(t p) d -> p t d", p=P)).then_inc(sem(f"back{l}_{b}"), 16)
            for b in range(BATCHES):
                sp.wait_ge(sem("added1"), 2 * (b + 1))
                sp.dma_start(out_dram[:, TB * b:TB * (b + 1), :], x_sb[:, TB * b:TB * (b + 1), :]).then_inc(sem("stored"), 16)
            sp.wait_ge(sem("stored"), 16 * BATCHES)

        @block.gpsimd
        def _(pool):
            g = nc.gpsimd
            g.memset(ident[:, :], 0.0).then_inc(sem("const_step"), 1)
            g.memset(minus_half[:, :], -0.5)
            g.memset(zero_i[:, :], 0)
            g.memset(ones_f[:, :], 1.0)
            g.memset(ones_b[:, :], 1.0)
            g.memset(earlier[:, :], 1.0)
            g.memset(head_mask[:, :], 1.0)
            g.memset(pad_tile[:, :], 0.0).then_inc(sem("const_step"), 1)
            pool.wait_ge(sem("const_step"), 2)
            g.affine_select(out=ident[:, :], in_=ident[:, :], compare_op=ALU.not_equal, fill=1.0, base=0,
                            pattern=[[-1, P]], channel_multiplier=1).then_inc(sem("ident_ready"), 1)
            g.affine_select(out=earlier[:, :], in_=earlier[:, :], compare_op=ALU.is_gt, fill=0.0, base=0,
                            pattern=[[1, P]], channel_multiplier=-1)
            g.iota(pad_tile[:, AT_DEST:AT_DEST + 1].bitcast(I32), pattern=[[0, 1]], base=NOWHERE,
                   channel_multiplier=0).then_inc(sem("pad_tile_ready"), 2)
            g.affine_select(out=head_mask[:, :], in_=head_mask[:, :], compare_op=ALU.is_ge, fill=0.0, base=0,
                            pattern=[[-HD, HEADS]], channel_multiplier=1).then_inc(sem("const_step"), 1)
            pool.wait_ge(sem("const_step"), 3)
            g.affine_select(out=head_mask[:, :], in_=head_mask[:, :], compare_op=ALU.is_ge, fill=0.0, base=HD - 1,
                            pattern=[[HD, HEADS]], channel_multiplier=-1)
            g.iota(desc[:, :], pattern=[[-1, E]], base=E, channel_multiplier=0, allow_small_or_imprecise_dtypes=True)
            g.iota(region_at[:, :], pattern=[[REGION, E]], base=0, channel_multiplier=0, allow_small_or_imprecise_dtypes=True)
            g.iota(tile_no[:, :], pattern=[[1, MAP]], base=0, channel_multiplier=0, allow_small_or_imprecise_dtypes=True)
            g.memset(row[:, :, :, :], 0.0).then_inc(sem("const_step"), 1)
            pool.wait_ge(sem("const_step"), 4)
            for k in range(TOP):
                g.iota(row[:, :, k, AT_DEST:AT_DEST + 1].bitcast(I32), pattern=[[P, NT], [0, 1]], base=k * TOKENS,
                       channel_multiplier=1).then_inc(sem("consts_ready"), 1)

            last_place = pool.to_reg(TOP * TOKENS - 1)

            def scatter_ffn(l):
                def copy_meta(i, c):
                    j, s = UNROLL * i + c, c % UNROLL
                    pool.wait_ge(sem(f"xs_loaded{l}_{s}"), 16 * (i + c // UNROLL + 1))
                    if reached(j, UNROLL):
                        pool.wait_ge(sem(f"y_gated{l}"), j - UNROLL + 1)
                        pool.wait_ge(sem(f"y_sent{l}_{s}"), 16 * (i + c // UNROLL))
                    g.tensor_tensor(meta[:, s, :].bitcast(I32), xs[:, s, AT_DEST:AT_DEST + 2].bitcast(I32), zero_i[:, :], ALU.add)\
                        .then_inc(sem(f"meta_ready{l}"), 1)

                def send(i, c):
                    j, s = UNROLL * i + c, c % UNROLL
                    pool.wait_ge(sem(f"meta_ready{l}"), j + 1)
                    pool.wait_ge(sem(f"y_gated{l}"), j + 1)
                    g.tensor_tensor(pool_carrier[:, s, :], zero_i[:, :], zero_i[:, :], ALU.add)
                    pool.indirect_dma_start(
                        out=contrib[l], out_offset=bass.IndirectOffsetOnAxis(ap=meta[:, s, 0:1].bitcast(I32), axis=0),
                        in_=y_out[:, s, :], in_offset=None, bounds_check=last_place, oob_is_err=False)\
                        .then_inc(sem(f"y_sent{l}_{s}"), 16)

                def body(i, c):
                    j = UNROLL * i + c
                    if not isinstance(j, int) or j + 1 < FFN_TILES:
                        copy_meta(i, c + 1)
                    send(i, c - 1)

                copy_meta(0, 0)
                copy_meta(0, 1)
                for j in range(1, UNROLL + 1):
                    body(0, j)
                with pool.Fori(1, LOOPS) as i:
                    for c in range(1, UNROLL + 1):
                        body(i, c)
                for j in range(UNROLL * LOOPS + 1, FFN_TILES + 1):
                    body(LOOPS, j - UNROLL * LOOPS)

            def power(n, into, base):
                pool.wait_ge(sem(f"var_ready_{n}"), base)
                g.tensor_tensor(into, {"a": var_eps[:, :], "r": var_r[:, :, :]}[n[0]],
                                {"a": minus_half[:, :], "r": minus_half[:, 0:2 * TB].rearrange("p (k t) -> p k t", k=2)}[n[0]],
                                ALU.pow).then_inc(sem(f"rstd_ready_{n}"), 1)

            for l in range(2):
                power(f"a{l}", rstd[:, :], 1)
                for b in range(BATCHES):
                    power(f"r{l}", rstd_r[:, :, :], b + 1)
                    pool.wait_ge(sem(f"slots_ready{l}"), b + 1)
                    pool.wait_ge(sem(f"rows_ready{l}"), b + 1)
                    for t in range(TB):
                        for k in range(TOP):
                            pool.indirect_dma_start(
                                out=sent[l], out_offset=bass.IndirectOffsetOnAxis(ap=slot[:, b, k, t:t + 1], axis=0),
                                in_=row[:, TB * b + t, k, :], in_offset=None).then_inc(sem(f"rows_sent{l}"), 16)
                scatter_ffn(l)

        @block.tensor
        def _(pe):
            mm = nc.tensor.matmul

            def setup():
                pe.wait_ge(sem("ident_ready"), 1)
                pe.wait_ge(sem("consts_ready"), 2)
                pe.wait_ge(sem("small_loaded"), 16 * 9)
                nc.tensor.transpose(bank[0][:, 0:N_SMALL], small_rows[:, :], ident[0:N_SMALL, 0:N_SMALL]).then_inc(sem("cols_turned"), 1)
                pe.wait_ge(sem("ctx_loaded"), 16)
                nc.tensor.transpose(bank[1][0:CTX, 0:P], ctx_sb[:, :], ident[:, :]).then_inc(sem("ctx_turned"), 1)
                pe.wait_ge(sem("ctxT_ready"), 2)
                pe.wait_ge(sem("attn_loaded"), 16 * 8)
                for l in range(2):
                    m = mm(bank[2][:, P * l:P * (l + 1)], wk[l][:, :], ctxT[:, :], start=True, stop=True)
                m.then_inc(sem("k_ready"), 1)
                for l in range(2):
                    for b in range(BATCHES):
                        m = mm(bank[3 + l][:, D * b:D * (b + 1)], ctxT4[:, b, :, :].rearrange("c g k -> c (g k)"),
                               wv[l][:, :], start=True, stop=True)
                    m.then_inc(sem("v_ready"), 1)

            def turn(n, b, src, dst, ready):
                pe.wait_ge(sem(ready), b + 1)
                for t in range(TB):
                    m = nc.tensor.transpose(dst[:, P * t:P * (t + 1)], src[:, t, :], ident[:, :])
                m.then_inc(sem(n), 1)

            def project_q(l, b):
                pe.wait_ge(sem(f"zT_copied_a{l}"), b + 1)
                mm(bank[1][:, :], wq[l][:, :], zT_a[:, :], start=True, stop=True).then_inc(sem(f"q_done{l}"), 1)

            def attention0(b):
                turn("z_turned_a0", b, z_a, bank[0], "z_ready_a0")
                project_q(0, b)
                pe.wait_ge(sem("qT_copied0"), b + 1)
                for t in range(TB):
                    m = mm(bank[2][:, KEYS * t:KEYS * (t + 1)], qT[:, P * t:P * (t + 1)], kT[:, 0, bass.ds(KEYS * b, KEYS)],
                           start=True, stop=True)
                m.then_inc(sem("scores_done0"), 1)
                pe.wait_ge(sem("probs_ready0"), b + 1)
                nc.tensor.transpose(bank[3][:, 0:P], shifted[:, :, :].rearrange("p t k -> p (t k)"), ident[:, :])\
                    .then_inc(sem("probs_turned0"), 1)
                pe.wait_ge(sem("probsT_copied0"), b + 1)
                mm(bank[4][:, :], probsT[:, :], v_wide[:, one(b), :, :].rearrange("p o t d -> p (o t d)"),
                   start=True, stop=True).then_inc(sem("att_done0"), 1)

            def routing(l, b):
                turn(f"z_turned_r{l}", b, z_r, bank[5], f"z_ready_r{l}")
                pe.wait_ge(sem(f"zT_copied_r{l}"), b + 1)
                feat, w = zT_r, wg
                if l == 1:
                    mm(bank[5][:, :], rw1[:, :], zT_r[:, :], start=True, stop=True).then_inc(sem("router_hidden"), 1)
                    pe.wait_ge(sem("router_silu"), b + 1)
                    feat, w = hidT, rw2
                for t in range(TB):
                    m = mm(bank[6][:, E * t:E * (t + 1)], feat[:, P * t:P * (t + 1)], w[:, :], start=True, stop=True)
                m.then_inc(sem(f"logits_done{l}"), 1)
                pe.wait_ge(sem(f"picked_ready{l}"), b + 1)
                rank = bank[6][:, 64:64 + TB * E]
                chosen = picked[:, :, :].rearrange("p t e -> p (t e)")
                mm(rank, earlier[:, :], chosen, start=True, stop=False)
                for s in range(1, TB):
                    mm(rank[:, E * s:], ones_b[:, :], chosen[:, 0:E * (TB - s)], start=False, stop=False)
                mm(rank.rearrange("p (t e) -> p t e", e=E), ones_b[:, :], picked_before[:, :].unsqueeze(1).broadcast_to([P, TB, E]),
                   start=False, stop=True).then_inc(sem(f"rank_done{l}"), 1)

            def count_experts(l):
                pe.wait_ge(sem(f"picked_summed{l}"), BATCHES)
                mm(bank[6][:, 0:E], ones_b[:, :], picked_before[:, :], start=True, stop=True).then_inc(sem(f"counts_done{l}"), 1)

            def fold_norm_bias():
                pe.wait_ge(sem("w_loaded0"), 16 * 3)
                for n in range(E * FC):
                    m = mm(bank[7][:, n:n + 1], w1[0][:, n // FC, P * (n % FC):P * (n % FC + 1)],
                           col[:, R_LNB + n // FC:R_LNB + n // FC + 1], start=True, stop=True)
                m.then_inc(sem("norm_bias_done"), 1)

            def ffn(l):
                def turn_rows(i, c):
                    j, s = UNROLL * i + c, c % UNROLL
                    pe.wait_ge(sem(f"xs_loaded{l}_{s}"), 16 * (i + c // UNROLL + 1))
                    if reached(j, 2):
                        pe.wait_ge(sem(f"xT_ready{l}"), j - 1)
                    nc.tensor.transpose(bank[c % 2][:, 0:P], xs[:, s, 0:D], ident[:, :]).then_inc(sem(f"x_turned{l}"), 1)

                def up(i, c):
                    j, h = UNROLL * i + c, c % 2
                    pe.wait_ge(sem(f"xT_ready{l}"), j + 1)
                    pe.wait_ge(sem(f"w1_ready{l}"), j + 1)
                    if reached(j, 2):
                        pe.wait_ge(sem(f"hid_biased{l}"), j - 1)
                    for f in range(FC):
                        m = mm(bank[2 + h][:, P * f:P * (f + 1)], w1_now[:, h, P * f:P * (f + 1)], xT[:, h, :],
                               start=True, stop=True)
                    m.then_inc(sem(f"up_done{l}"), 1)

                def down(i, c):
                    j, h = UNROLL * i + c, c % 2
                    e = pe.value_load(expert[0:1, one(j)], min_val=0, max_val=E - 1)
                    pe.wait_ge(sem(f"hid_ready{l}"), j + 1)
                    if reached(j, 2):
                        pe.wait_ge(sem(f"y_biased{l}"), j - 1)
                    for f in range(FC):
                        m = mm(bank[4 + h][:, 0:D], hid[:, h, P * f:P * (f + 1)],
                               w2[l][:, one(e), f, :].rearrange("p o d -> p (o d)"), start=(f == 0), stop=(f == FC - 1))
                    m.then_inc(sem(f"down_done{l}"), 1)

                def body(i, c):
                    j = UNROLL * i + c
                    if not isinstance(j, int) or j + 1 < FFN_TILES:
                        turn_rows(i, c + 1)
                    if not isinstance(j, int) or j < FFN_TILES:
                        up(i, c)
                    if reached(j, 1):
                        down(i, c - 1)

                turn_rows(0, 0)
                for j in range(UNROLL + 1):
                    body(0, j)
                with pe.Fori(1, LOOPS) as i:
                    for c in range(1, UNROLL + 1):
                        body(i, c)
                for j in range(UNROLL * LOOPS + 1, FFN_TILES + 1):
                    body(LOOPS, j - UNROLL * LOOPS)

            def score_heads(i, b, t, wait_sem, value):
                pe.wait_ge(sem(wait_sem), value)
                mm(bank[2 + t % 2][:, :], qT[:, P * t:P * (t + 1)], k_wide[:, one(b), :, :].rearrange("p o h k -> p (o h k)"),
                   start=True, stop=True).then_inc(sem(i), 1)

            def prepass1(b):
                turn("z_turned_a1", b, z_a, bank[0], "z_ready_a1")
                project_q(1, b)
                pe.wait_ge(sem("qT_copied1"), b + 1)
                for t in range(TB):
                    if t >= 2:
                        pe.wait_ge(sem("pre_max_read"), TB * b + t - 1)
                        pe.wait_ge(sem("pre_nan_read"), TB * b + t - 1)
                    mm(bank[2 + t % 2][:, :], qT[:, P * t:P * (t + 1)],
                       k_wide[:, one(b), :, :].rearrange("p o h k -> p (o h k)"), start=True, stop=True)\
                        .then_inc(sem("pre_scores"), 1)

            def attention1(b):
                pe.wait_ge(sem("q_again"), b + 1)
                for t in range(TB):
                    n = TB * b + t
                    if t >= 2:
                        pe.wait_ge(sem("shift_done1"), n - 1)
                    mm(bank[2 + t % 2][:, :], qT[:, P * t:P * (t + 1)],
                       k_wide[:, one(b), :, :].rearrange("p o h k -> p (o h k)"), start=True, stop=True)\
                        .then_inc(sem("scores_done1"), 1)
                    if t >= 1:
                        weigh(b, t - 1)
                weigh(b, TB - 1)
                pe.wait_ge(sem("att_ready1"), TB * (b + 1))
                for t in range(TB):
                    m = nc.tensor.transpose(bank[4][:, P * t:P * (t + 1)], att[:, t, :], ident[:, :])
                m.then_inc(sem("att_turned1"), 1)
                pe.wait_ge(sem("attT_copied1"), b + 1)
                mm(bank[4][:, :], ones_f[0:1, :], bo[:, :, :].rearrange("o t d -> o (t d)"), start=True, stop=False)
                for t in range(TB):
                    m = mm(bank[4][:, D * t:D * (t + 1)], attT[:, t, :], wo[:, :], start=False, stop=(t == TB - 1))
                m.then_inc(sem("att_done1"), 1)

            def weigh(b, t):
                n = TB * b + t
                pe.wait_ge(sem("exp_done1"), n + 1)
                for c in range(TB):
                    m = nc.tensor.transpose(bank[t % 2][:, P * c:P * (c + 1)],
                                            sc[:, t % 2, GROUP * c:GROUP * (c + 1), :].rearrange("p h k -> p (h k)"), ident[:, :])
                m.then_inc(sem("p_turned1"), 1)
                pe.wait_ge(sem("pT_copied1"), n + 1)
                if t >= 1:
                    pe.wait_ge(sem("att_ready1"), n)
                w = GROUP * (HD + 1)
                for c in range(TB):
                    m = mm(bank[7][:, w * c:w * (c + 1)], pT[:, t % 2, P * c:P * (c + 1)],
                           v_head[:, one(b), GROUP * c:GROUP * (c + 1), :].rearrange("p o h d -> p (o h d)"), start=True, stop=True)
                m.then_inc(sem("weighed1"), 1)

            setup()
            pe.wait_ge(sem("setup_read"), 1)
            pe.wait_ge(sem("router_loaded"), 16 * 10)
            with pe.Fori(0, BATCHES) as b:
                attention0(b)
                routing(0, b)
            count_experts(0)
            fold_norm_bias()
            ffn(0)
            with pe.Fori(0, BATCHES) as b:
                prepass1(b)
            pe.wait_ge(sem("pre_nan_read"), NT)
            mm(bank[4][:, 0:NT], ones_f[:, :], nan_seen[:, :], start=True, stop=True).then_inc(sem("nan_summed"), 1)
            with pe.Fori(0, BATCHES) as b:
                attention1(b)
                routing(1, b)
            count_experts(1)
            pe.wait_ge(sem("w_loaded1"), 16 * 3)
            ffn(1)

        @block.scalar
        def _(act):
            s = nc.scalar

            def copy_zT(n, b, dst, src):
                act.wait_ge(sem(f"z_turned_{n}"), b + 1)
                s.copy(dst[:, :], src[:, :]).then_inc(sem(f"zT_copied_{n}"), 1)

            def add_bq(l, b):
                act.wait_ge(sem(f"q_done{l}"), b + 1)
                s.activation(qT[:, :], bank[1][:, :], ACT.Identity, bias=col[:, R_BQ[l]:R_BQ[l] + 1]).then_inc(sem(f"qT_copied{l}"), 1)

            def attention0(b):
                copy_zT("a0", b, zT_a, bank[0])
                add_bq(0, b)
                act.wait_ge(sem("shifted0"), b + 1)
                s.activation(shifted[:, :, :], shifted[:, :, :], ACT.Exp).then_inc(sem("exp_done0"), 1)
                act.wait_ge(sem("probs_turned0"), b + 1)
                s.copy(probsT[:, :], bank[3][:, 0:P]).then_inc(sem("probsT_copied0"), 1)

            def routing(l, b):
                copy_zT(f"r{l}", b, zT_r, bank[5])
                if l == 1:
                    act.wait_ge(sem("router_hidden"), b + 1)
                    s.activation(hidT[:, :], bank[5][:, :], ACT.Silu, bias=col[:, R_RB1:R_RB1 + 1]).then_inc(sem("router_silu"), 1)
                act.wait_ge(sem(f"gap_ready{l}"), b + 1)
                s.activation(ratio[:, :], gap[:, :], ACT.Exp).then_inc(sem(f"ratio_ready{l}"), 1)

            def scale_w1():
                act.wait_ge(sem("norm_bias_done"), 1)
                for e in range(E):
                    m = s.activation(w1[0][:, e, :], w1[0][:, e, :], ACT.Copy, scale=col[:, R_LNW + e:R_LNW + e + 1])
                m.then_inc(sem("w1_scaled"), 1)

            def ffn(l):
                func = [ACT.Gelu_apprx_tanh, ACT.Silu][l]

                def copy_xT(i, c):
                    j, h = UNROLL * i + c, c % 2
                    act.wait_ge(sem(f"x_turned{l}"), j + 1)
                    if reached(j, 2):
                        act.wait_ge(sem(f"up_done{l}"), j - 1)
                    s.copy(xT[:, h, :], bank[h][:, 0:P]).then_inc(sem(f"xT_ready{l}"), 1)

                def activate(i, c):
                    j, h = UNROLL * i + c, c % 2
                    act.wait_ge(sem(f"hid_biased{l}"), j + 1)
                    s.activation(hid[:, h, :], hid[:, h, :], func).then_inc(sem(f"hid_ready{l}"), 1)

                def apply_gate(i, c):
                    j, q = UNROLL * i + c, c % UNROLL
                    act.wait_ge(sem(f"y_biased{l}"), j + 1)
                    act.wait_ge(sem(f"meta_ready{l}"), j + 1)
                    if reached(j, UNROLL):
                        act.wait_ge(sem(f"y_sent{l}_{q}"), 16 * (i + c // UNROLL))
                    s.activation(y_out[:, q, :], y_raw[:, c % 2, :], ACT.Copy, scale=meta[:, q, 1:2]).then_inc(sem(f"y_gated{l}"), 1)

                def body(i, c):
                    j = UNROLL * i + c
                    if not isinstance(j, int) or j + 1 < FFN_TILES:
                        copy_xT(i, c + 1)
                    if not isinstance(j, int) or j < FFN_TILES:
                        activate(i, c)
                    if reached(j, 1):
                        apply_gate(i, c - 1)

                copy_xT(0, 0)
                for j in range(UNROLL + 1):
                    body(0, j)
                with act.Fori(1, LOOPS) as i:
                    for c in range(1, UNROLL + 1):
                        body(i, c)
                for j in range(UNROLL * LOOPS + 1, FFN_TILES + 1):
                    body(LOOPS, j - UNROLL * LOOPS)

            def prepass1(b):
                copy_zT("a1", b, zT_a, bank[0])
                add_bq(1, b)
                act.wait_ge(sem("qT_copied1"), b + 1)
                s.copy(qT_all[:, one(b), :], qT[:, :].unsqueeze(1))
                for t in range(TB):
                    act.wait_ge(sem("pre_scores"), TB * b + t + 1)
                    act.wait_ge(sem("pre_max_read"), TB * b + t + 1)
                    s.activation(nan_junk[:, t, :], bank[2 + t % 2][:, :], ACT.Tanh, accum_out=nan_seen[:, one(TB * b + t)])\
                        .then_inc(sem("pre_nan_read"), 1)

            def attention1(b):
                s.copy(qT[:, :].unsqueeze(1), qT_all[:, one(b), :]).then_inc(sem("q_again"), 1)
                for t in range(TB):
                    n = TB * b + t
                    act.wait_ge(sem("shift_done1"), n + 1)
                    s.activation(sc[:, t % 2, :, :], sc[:, t % 2, :, :], ACT.Exp).then_inc(sem("exp_done1"), 1)
                    act.wait_ge(sem("p_turned1"), n + 1)
                    s.copy(pT[:, t % 2, :], bank[t % 2][:, :]).then_inc(sem("pT_copied1"), 1)
                act.wait_ge(sem("att_turned1"), b + 1)
                s.copy(attT[:, :, :].rearrange("p t q -> p (t q)"), bank[4][:, :]).then_inc(sem("attT_copied1"), 1)

            with act.Fori(0, BATCHES) as b:
                attention0(b)
                routing(0, b)
            scale_w1()
            ffn(0)
            with act.Fori(0, BATCHES) as b:
                prepass1(b)
            act.wait_ge(sem("pre_nan_read"), NT)
            with act.Fori(0, BATCHES) as b:
                attention1(b)
                routing(1, b)
            ffn(1)

        @block.vector
        def _(dve):
            v = nc.vector

            def setup():
                v.memset(v_wide[:, :, :, :], 0.0)
                v.memset(v_head[:, :, :, :], 0.0).then_inc(sem("v_cleared"), 1)
                dve.wait_ge(sem("cols_turned"), 1)
                v.tensor_copy(col[:, :], bank[0][:, 0:N_SMALL]).then_inc(sem("cols_ready"), 1)
                dve.wait_ge(sem("ctx_turned"), 1)
                v.tensor_copy(ctxT[:, :], bank[1][0:CTX, 0:P]).then_inc(sem("ctxT_ready"), 1)
                v.tensor_copy(ctxT4[:, :, :, :], bank[1][0:CTX, 0:P].rearrange("c (b k) -> c b k", b=BATCHES)
                              .unsqueeze(2).broadcast_to([CTX, BATCHES, GROUP, KEYS])).then_inc(sem("ctxT_ready"), 1)
                dve.wait_ge(sem("k_ready"), 1)
                dve.wait_ge(sem("cols_ready"), 1)
                for l in range(2):
                    m = v.tensor_scalar(kT[:, l, :], bank[2][:, P * l:P * (l + 1)], col[:, R_BK[l]:R_BK[l] + 1], SCALE[l], ALU.add, ALU.mult)
                m.then_inc(sem("kT_ready"), 1)
                dve.wait_ge(sem("v_ready"), 2)
                dve.wait_ge(sem("v_cleared"), 1)
                dve.wait_ge(sem("kT_ready"), 1)
                for r in range(GROUP):
                    p = slice(KEYS * r, KEYS * (r + 1))
                    v.tensor_tensor(v_wide[p, :, r, :], bank[3][p, :].rearrange("p (b d) -> p b d", b=BATCHES),
                                    bv[0][p, :].unsqueeze(1).broadcast_to([KEYS, BATCHES, D]), ALU.add)
                    for b in range(BATCHES):
                        v.tensor_tensor(v_head[p, b, r::GROUP, 0:HD],
                                        bank[4][p, D * b:D * (b + 1)].rearrange("p (h d) -> p h d", d=HD)[:, r::GROUP, :],
                                        bv[1][p, :].rearrange("p (h d) -> p h d", d=HD)[:, r::GROUP, :], ALU.add)
                    v.memset(v_head[p, :, r::GROUP, HD:HD + 1].rearrange("p b h o -> p b (h o)"), 1.0)
                for b in range(BATCHES):
                    m = v.tensor_tensor(k_wide[:, b, :, :], kT[:, 1, KEYS * b:KEYS * (b + 1)].unsqueeze(1).broadcast_to([P, HEADS, KEYS]),
                                        head_mask[:, :].unsqueeze(2).broadcast_to([P, HEADS, KEYS]), ALU.mult)
                m.then_inc(sem("setup_read"), 1)

            def norm_all(l):
                for t in range(NT):
                    m = v.bn_stats(bn[:, t, :], x_sb[:, t, :])
                m.then_inc(sem(f"stats{l}"), 1)
                dve.wait_ge(sem(f"stats{l}"), 1)
                for t in range(NT):
                    m = v.bn_aggr(mv[:, t, :], bn[:, t, :])
                m.then_inc(sem(f"stats{l}"), 1)
                dve.wait_ge(sem(f"stats{l}"), 2)
                v.tensor_scalar(var_eps[:, :], mv[:, :, 1], EPS, None, ALU.add).then_inc(sem(f"var_ready_a{l}"), 1)

            def normalise_a(l, b):
                for t in range(TB):
                    n = TB * b + t
                    m = v.tensor_scalar(z_a[:, t, :], x_sb[:, one(n), :].rearrange("p o d -> p (o d)"),
                                        mv[:, one(n), 0:1].rearrange("p o d -> p (o d)"), rstd[:, one(n)], ALU.subtract, ALU.mult)
                m.then_inc(sem(f"z_ready_a{l}"), 1)

            def attention0(b):
                normalise_a(0, b)
                dve.wait_ge(sem("scores_done0"), b + 1)
                scores = bank[2][:, 0:TB * KEYS].rearrange("p (t k) -> p t k", k=KEYS)
                v.tensor_reduce(top_score[:, :], scores, AX.X, ALU.max).then_inc(sem("soft_step0"), 1)
                dve.wait_ge(sem("soft_step0"), 4 * b + 1)
                v.tensor_tensor(shifted[:, :, :], scores, top_score[:, :].unsqueeze(2).broadcast_to([P, TB, KEYS]),
                                ALU.subtract).then_inc(sem("shifted0"), 1)
                dve.wait_ge(sem("exp_done0"), b + 1)
                v.tensor_reduce(prob_sum[:, :], shifted[:, :, :], AX.X, ALU.add).then_inc(sem("soft_step0"), 1)
                dve.wait_ge(sem("soft_step0"), 4 * b + 2)
                v.reciprocal(prob_scale[:, :], prob_sum[:, :]).then_inc(sem("soft_step0"), 1)
                dve.wait_ge(sem("soft_step0"), 4 * b + 3)
                v.tensor_tensor(shifted[:, :, :], shifted[:, :, :], prob_scale[:, :].unsqueeze(2).broadcast_to([P, TB, KEYS]),
                                ALU.mult).then_inc(sem("probs_ready0"), 1)
                dve.wait_ge(sem("att_done0"), b + 1)
                add_to_x(b, bank[4], "soft_step0")
                dve.wait_ge(sem("soft_step0"), 4 * b + 4)
                carry_wait(0)

            def add_to_x(b, src, done):
                mine = x_sb[:, bass.ds(TB * b, TB), :]
                v.tensor_tensor(mine, mine, src[:, :].rearrange("p (t d) -> p t d", t=TB), ALU.add).then_inc(sem(done), 1)

            def routing(l, b):
                STEPS = 23
                step, at = sem(f"route_step{l}"), STEPS * b
                bc_e = [P, TB, E]
                for t in range(TB):
                    m = v.bn_stats(bn_r[:, t, :], x_sb[:, one(TB * b + t), :].rearrange("p o d -> p (o d)"))
                m.then_inc(step, 1)
                dve.wait_ge(step, at + 1)
                carry_wait(1)
                for t in range(TB):
                    m = v.bn_aggr(mv_r[:, t, :], bn_r[:, t, :])
                m.then_inc(step, 1)
                dve.wait_ge(step, at + 2)
                v.tensor_scalar(var_r[:, 0, :], mv_r[:, :, 1], EPS, None, ALU.add)
                v.tensor_scalar(var_r[:, 1, :], mv_r[:, :, 1], 1.0 + EPS, EPS * EPS, ALU.mult, ALU.add).then_inc(sem(f"var_ready_r{l}"), 1)
                dve.wait_ge(sem(f"rstd_ready_r{l}"), b + 1)
                if l == 1:
                    dve.wait_ge(sem("rows_sent0"), 16 * TOP * NT)
                for t in range(TB):
                    n = TB * b + t
                    xt = x_sb[:, one(n), :]
                    m = v.tensor_scalar(z_r[:, t, :], xt.rearrange("p o d -> p (o d)"), mv_r[:, t, 0:1], rstd_r[:, 0, t:t + 1],
                                        ALU.subtract, ALU.mult)
                m.then_inc(sem(f"z_ready_r{l}"), 1)
                for t in range(TB):
                    n = TB * b + t
                    xt = x_sb[:, one(n), :]
                    m = v.tensor_scalar(row[:, one(n), :, 0:D].rearrange("p o k d -> p (o k) d"), xt.broadcast_to([P, TOP, D]),
                                        mv_r[:, t, 0:1], rstd_r[:, 1 - l, t:t + 1], ALU.subtract, ALU.mult)
                m.then_inc(step, 1)
                if l == 1:
                    mine = x_sb[:, bass.ds(TB * b, TB), :]
                    dve.wait_ge(step, at + 3)
                    dve.wait_ge(sem("z_ready_r1"), b + 1)
                    v.tensor_tensor(mine, mine, z_r[:, :, :], ALU.add)
                dve.wait_ge(sem(f"logits_done{l}"), b + 1)
                lg = bank[6][:, 0:TB * E].rearrange("p (t e) -> p t e", e=E)
                if l == 0:
                    v.tensor_copy(logit[:, :, :], lg).then_inc(step, 1)
                else:
                    v.tensor_tensor(logit[:, :, :], lg, rb2[:, :].unsqueeze(1).broadcast_to(bc_e), ALU.add).then_inc(step, 1)
                dve.wait_ge(step, at + 4)
                src, n = logit, 4
                for k in range(TOP):
                    v.tensor_reduce(best[:, k, :], src[:, :, :], AX.X, ALU.max).then_inc(step, 1)
                    dve.wait_ge(step, at + n + 1)
                    v.tensor_tensor(tied[:, :, :], src[:, :, :], best[:, k, :].unsqueeze(2).broadcast_to(bc_e), ALU.is_equal).then_inc(step, 1)
                    dve.wait_ge(step, at + n + 2)
                    v.tensor_tensor(tied[:, :, :], tied[:, :, :], desc[:, :].unsqueeze(1).broadcast_to(bc_e), ALU.mult).then_inc(step, 1)
                    dve.wait_ge(step, at + n + 3)
                    v.tensor_reduce(key[:, k, :], tied[:, :, :], AX.X, ALU.max).then_inc(step, 1)
                    dve.wait_ge(step, at + n + 4)
                    v.tensor_tensor(hot[:, k, :, :], desc[:, :].unsqueeze(1).broadcast_to(bc_e),
                                    key[:, k, :].unsqueeze(2).broadcast_to(bc_e), ALU.is_equal).then_inc(step, 1)
                    dve.wait_ge(step, at + n + 5)
                    n += 5
                    if k == 0:
                        v.scalar_tensor_tensor(out=rest[:, :, :], in0=hot[:, 0, :, :], scalar=-BIG, in1=logit[:, :, :],
                                               op0=ALU.mult, op1=ALU.add).then_inc(step, 1)
                        dve.wait_ge(step, at + n + 1)
                        src, n = rest, n + 1
                v.tensor_tensor(picked[:, :, :], hot[:, 0, :, :], hot[:, 1, :, :], ALU.add).then_inc(sem(f"picked_ready{l}"), 1)
                v.tensor_tensor(gap[:, :], best[:, 1, :], best[:, 0, :], ALU.subtract).then_inc(sem(f"gap_ready{l}"), 1)
                if l == 0:
                    v.tensor_tensor(alpha_hot[:, :, :, :].rearrange("p k t e -> p (k t) e"), hot[:, :, :, :].rearrange("p k t e -> p (k t) e"),
                                    alpha[:, :].unsqueeze(1).broadcast_to([P, TOP * TB, E]), ALU.mult).then_inc(step, 1)
                    dve.wait_ge(step, at + 16)
                    v.tensor_reduce(alpha_of[:, :, :], alpha_hot[:, :, :, :], AX.X, ALU.add).then_inc(step, 1)
                else:
                    v.memset(alpha_of[:, :, :], 1.0).then_inc(step, 2)
                dve.wait_ge(sem(f"rank_done{l}"), b + 1)
                v.tensor_tensor(row_of[:, :, :], bank[6][:, 64:64 + TB * E].rearrange("p (t e) -> p t e", e=E),
                                region_at[:, :].unsqueeze(1).broadcast_to(bc_e), ALU.add).then_inc(step, 1)
                dve.wait_ge(step, at + 18)
                v.tensor_tensor(spread[:, :, :, :], hot[:, :, :, :], row_of[:, :, :].unsqueeze(1).broadcast_to([P, TOP, TB, E]),
                                ALU.mult).then_inc(step, 1)
                dve.wait_ge(step, at + 19)
                v.tensor_reduce(slot_f[:, :, :], spread[:, :, :, :], AX.X, ALU.add).then_inc(step, 1)
                dve.wait_ge(step, at + 20)
                v.tensor_copy(slot[:, one(b), :, :].rearrange("p o k t -> p (o k) t"), slot_f[:, :, :]).then_inc(sem(f"slots_ready{l}"), 1)
                v.tensor_reduce(picked_now[:, :], picked[:, :, :].rearrange("p t e -> p e t"), AX.X, ALU.add).then_inc(step, 1)
                dve.wait_ge(step, at + 21)
                v.tensor_tensor(picked_before[:, :], picked_before[:, :], picked_now[:, :], ALU.add).then_inc(sem(f"picked_summed{l}"), 1)
                dve.wait_ge(sem(f"ratio_ready{l}"), b + 1)
                v.tensor_scalar(total[:, :], ratio[:, :], 1.0, None, ALU.add).then_inc(step, 1)
                dve.wait_ge(step, at + 22)
                v.reciprocal(gate[:, 0, :], total[:, :]).then_inc(step, 1)
                dve.wait_ge(step, at + 23)
                v.tensor_tensor(gate[:, 1, :], gate[:, 0, :], ratio[:, :], ALU.mult).then_inc(sem(f"gates{l}"), 1)
                dve.wait_ge(sem(f"gates{l}"), b + 1)
                v.tensor_tensor(row[:, bass.ds(TB * b, TB), :, AT_GATE], gate[:, :, :].rearrange("p k t -> p t k"),
                                alpha_of[:, :, :].rearrange("p k t -> p t k"), ALU.mult).then_inc(sem(f"rows_ready{l}"), 1)

            def map_tiles(l):
                step = sem(f"map_step{l}")
                n = [0]

                def then_wait(m):
                    n[0] += 1
                    m.then_inc(step, 1)
                    dve.wait_ge(step, n[0])

                by_tile = [P, MAP, E]
                dve.wait_ge(sem(f"counts_done{l}"), 1)
                then_wait(v.tensor_copy(count[:, :], bank[6][:, 0:E]))
                v.tensor_tensor(pad_at[:, :], count[:, :], region_at[:, :], ALU.add)
                then_wait(v.tensor_scalar(count_up[:, :], count[:, :], float(P - 1), None, ALU.add))
                then_wait(v.tensor_scalar(tiles_i[:, :], count_up[:, :], 7, None, ALU.arith_shift_right))
                then_wait(v.tensor_copy(tiles_f[:, :], tiles_i[:, :]))
                then_wait(v.tensor_tensor_scan(tiles_end[:, :], ones_f[:, 0:E], tiles_f[:, :], 0.0, ALU.mult, ALU.add))
                then_wait(v.tensor_tensor(passed[:, :, :], tiles_end[:, :].unsqueeze(1).broadcast_to(by_tile),
                                          tile_no[:, :].unsqueeze(2).broadcast_to(by_tile), ALU.is_le))
                then_wait(v.tensor_reduce(expert_f[:, :], passed[:, :, :], AX.X, ALU.add))
                then_wait(v.tensor_tensor(passed[:, :, :], passed[:, :, :], tiles_f[:, :].unsqueeze(1).broadcast_to(by_tile), ALU.mult))
                then_wait(v.tensor_reduce(first_f[:, :], passed[:, :, :], AX.X, ALU.add))
                then_wait(v.tensor_tensor(first_f[:, :], tile_no[:, :], first_f[:, :], ALU.subtract))
                then_wait(v.scalar_tensor_tensor(out=first_f[:, :], in0=expert_f[:, :], scalar=float(REGION // P), in1=first_f[:, :],
                                                 op0=ALU.mult, op1=ALU.add))
                v.tensor_scalar(row_base[:, :], first_f[:, :], float(P), float(PAD_ROW), ALU.mult, ALU.min)
                v.tensor_scalar(expert[:, :], expert_f[:, :], float(E - 1), None, ALU.min).then_inc(sem(f"map_ready{l}"), 1)
                dve.wait_ge(sem(f"map_ready{l}"), 1)

            def ffn(l):
                bias1 = (b1 if l == 0 else col[:, R_B1[1]:R_B1[1] + E * FC])

                def index(i, c):
                    return dve.value_load(expert[0:1, one(UNROLL * i + c)], min_val=0, max_val=E - 1)

                def stage_w1(i, c):
                    j, h = UNROLL * i + c, c % 2
                    e = index(i, c)
                    if reached(j, 2):
                        dve.wait_ge(sem(f"up_done{l}"), j - 1)
                    v.tensor_copy(w1_now[:, h, :], w1[l][:, one(e), :].rearrange("p o f -> p (o f)")).then_inc(sem(f"w1_ready{l}"), 1)

                def add_b1(i, c):
                    j, h = UNROLL * i + c, c % 2
                    e = index(i, c)
                    dve.wait_ge(sem(f"up_done{l}"), j + 1)
                    if reached(j, 2):
                        dve.wait_ge(sem(f"down_done{l}"), j - 1)
                    v.tensor_tensor(hid[:, h, :].rearrange("p (f q) -> p f q", f=FC), bank[2 + h][:, :].rearrange("p (f q) -> p f q", f=FC),
                                    bias1[:, bass.ds(e * FC, FC)].unsqueeze(2).broadcast_to([P, FC, P]), ALU.add)\
                        .then_inc(sem(f"hid_biased{l}"), 1)

                def add_b2(i, c):
                    j, h = UNROLL * i + c, c % 2
                    e = index(i, c)
                    dve.wait_ge(sem(f"down_done{l}"), j + 1)
                    if reached(j, 2):
                        dve.wait_ge(sem(f"y_gated{l}"), j - 1)
                    v.tensor_tensor(y_raw[:, h, :], bank[4 + h][:, 0:D], b2[l][:, one(e), :].rearrange("p o d -> p (o d)"), ALU.add)\
                        .then_inc(sem(f"y_biased{l}"), 1)

                def body(i, c):
                    j = UNROLL * i + c
                    if not isinstance(j, int) or j + 1 < FFN_TILES:
                        stage_w1(i, c + 1)
                    if not isinstance(j, int) or j < FFN_TILES:
                        add_b1(i, c)
                    if reached(j, 1):
                        add_b2(i, c - 1)

                stage_w1(0, 0)
                for j in range(UNROLL + 1):
                    body(0, j)
                with dve.Fori(1, LOOPS) as i:
                    for c in range(1, UNROLL + 1):
                        body(i, c)
                for j in range(UNROLL * LOOPS + 1, FFN_TILES + 1):
                    body(LOOPS, j - UNROLL * LOOPS)

            def add_back(l, b):
                mine = x_sb[:, TB * b:TB * (b + 1), :]
                dve.wait_ge(sem(f"back{l}_{b}"), 16 * TOP)
                v.tensor_tensor(mine, mine, back[:, b, 0, :, :], ALU.add).then_inc(sem(f"added{l}"), 1)
                dve.wait_ge(sem(f"added{l}"), 2 * b + 1)
                v.tensor_tensor(mine, mine, back[:, b, 1, :, :], ALU.add).then_inc(sem(f"added{l}"), 1)

            def prepass1(b):
                normalise_a(1, b)
                for t in range(TB):
                    n = TB * b + t
                    dve.wait_ge(sem("pre_scores"), n + 1)
                    v.tensor_reduce(max_all[:, one(n), :].rearrange("p o h -> p (o h)"), bank[2 + t % 2][:, :].rearrange("p (h k) -> p h k", k=KEYS),
                                    AX.X, ALU.max).then_inc(sem("pre_max_read"), 1)

            def nan_guard():
                dve.wait_ge(sem("pre_max_read"), NT)
                v.tensor_scalar(max_clip[:, :, :], max_all[:, :, :], -CLAMP, CLAMP, ALU.max, ALU.min)
                dve.wait_ge(sem("nan_summed"), 1)
                v.tensor_reduce(nan_sum[:, :], bank[4][:, 0:NT], AX.X, ALU.add).then_inc(sem("guard_step"), 1)
                dve.wait_ge(sem("guard_step"), 1)
                v.tensor_tensor(all_numbers[:, :], nan_sum[:, :], nan_sum[:, :], ALU.is_equal).then_inc(sem("guard_step"), 1)
                dve.wait_ge(sem("guard_step"), 2)

            def attention1(b):
                for t in range(TB):
                    n, h = TB * b + t, t % 2
                    dve.wait_ge(sem("scores_done1"), n + 1)
                    if t >= 2:
                        dve.wait_ge(sem("p_turned1"), n - 1)
                    v.scalar_tensor_tensor(out=sc[:, h, :, :], in0=bank[2 + h][:, :].rearrange("p (h k) -> p h k", k=KEYS), scalar=-CLAMP,
                                           in1=max_clip[:, one(n), :].rearrange("p o h -> p (o h)").unsqueeze(2).broadcast_to([P, HEADS, KEYS]),
                                           op0=ALU.max, op1=ALU.subtract).then_inc(sem("clip_step1"), 1)
                    dve.wait_ge(sem("clip_step1"), n + 1)
                    v.tensor_scalar(sc[:, h, :, :], sc[:, h, :, :], 0.0, all_numbers[:, 0:1], ALU.min, ALU.mult).then_inc(sem("shift_done1"), 1)
                    if t >= 1:
                        divide(b, t - 1)
                divide(b, TB - 1)
                dve.wait_ge(sem("att_done1"), b + 1)
                add_to_x(b, bank[4], "x_mid1")
                dve.wait_ge(sem("x_mid1"), b + 1)
                carry_wait(0)

            def divide(b, t):
                n = TB * b + t
                dve.wait_ge(sem("weighed1"), n + 1)
                got = bank[7][:, 0:HEADS * (HD + 1)].rearrange("p (h d) -> p h d", d=HD + 1)
                v.reciprocal(head_scale[:, :], got[:, :, HD]).then_inc(sem("head_step"), 1)
                dve.wait_ge(sem("head_step"), n + 1)
                v.tensor_tensor(att[:, t, :].rearrange("p (h d) -> p h d", d=HD), got[:, :, 0:HD],
                                head_scale[:, :].unsqueeze(2).broadcast_to([P, HEADS, HD]), ALU.mult).then_inc(sem("att_ready1"), 1)

            setup()
            dve.wait_ge(sem("x_loaded"), 16)
            dve.wait_ge(sem("setup_read"), 1)
            dve.wait_ge(sem("router_loaded"), 16 * 10)
            norm_all(0)
            v.memset(picked_before[:, :], 0.0)
            dve.wait_ge(sem("rstd_ready_a0"), 1)
            with dve.Fori(0, BATCHES) as b:
                attention0(b)
                routing(0, b)
            map_tiles(0)
            dve.wait_ge(sem("norm_bias_done"), 1)
            v.tensor_tensor(b1[:, :], bank[7][:, 0:E * FC], col[:, R_B1[0]:R_B1[0] + E * FC], ALU.add).then_inc(sem("b1_ready"), 1)
            dve.wait_ge(sem("b1_ready"), 1)
            dve.wait_ge(sem("w1_scaled"), 1)
            ffn(0)
            for b in range(BATCHES):
                add_back(0, b)
            dve.wait_ge(sem("added0"), 2 * BATCHES)
            norm_all(1)
            v.memset(picked_before[:, :], 0.0)
            dve.wait_ge(sem("rstd_ready_a1"), 1)
            with dve.Fori(0, BATCHES) as b:
                prepass1(b)
            nan_guard()
            with dve.Fori(0, BATCHES) as b:
                attention1(b)
                routing(1, b)
            map_tiles(1)
            dve.wait_ge(sem("w_loaded1"), 16 * 3)
            ffn(1)
            for b in range(BATCHES):
                add_back(1, b)


_INS = ['x', 'ctx_768', 'L0_xattn_Wq', 'L0_xattn_bq', 'L0_xattn_Wk', 'L0_xattn_bk', 'L0_xattn_Wv', 'L0_xattn_bv',
        'L0_ffn_Wg', 'L0_ffn_alpha', 'L0_ffn_ln_w', 'L0_ffn_ln_b', 'L0_ffn_fc1_w', 'L0_ffn_fc1_b', 'L0_ffn_fc2_w',
        'L0_ffn_fc2_b', 'L1_xattn_Wq', 'L1_xattn_bq', 'L1_xattn_Wk', 'L1_xattn_bk', 'L1_xattn_Wv', 'L1_xattn_bv',
        'L1_xattn_Wo', 'L1_xattn_bo', 'L1_ffn_rw1', 'L1_ffn_rb1', 'L1_ffn_rw2', 'L1_ffn_rb2', 'L1_ffn_we1',
        'L1_ffn_be1', 'L1_ffn_we2', 'L1_ffn_be2']


def kernel(**inputs):
    import numpy as _np
    import concourse.bacc as _bacc
    from concourse import mybir as _mybir
    from concourse.bass_utils import run_bass_kernel_spmd as _run

    nc = _bacc.Bacc("TRN2", target_bir_lowering=False, num_devices=1)
    arrays, aps = {}, {}
    for name in _INS:
        arr = _np.ascontiguousarray(inputs[name])
        arrays[f"in_{name}"] = arr
        aps[name] = nc.dram_tensor(f"in_{name}", arr.shape, _mybir.dt.from_np(arr.dtype), kind="ExternalInput").ap()
    out = nc.dram_tensor("out_0", (BATCHES, SEQ, D), F32, kind="ExternalOutput").ap()
    sent = [nc.dram_tensor(f"sent{l}", (PAD_ROW + P, W_ROW), F32, kind="Internal").ap() for l in range(2)]
    contrib = [nc.dram_tensor(f"contrib{l}", (TOP * TOKENS, D), F32, kind="Internal").ap() for l in range(2)]
    build(nc, aps, out, sent, contrib)
    r = _run(nc, [arrays], core_ids=[0])
    return r.results[0]["out_0"]
```

```python
from contextlib import ExitStack

import concourse.bass as bass
from concourse import mybir

F32 = mybir.dt.float32
BF16 = mybir.dt.bfloat16
I32 = mybir.dt.int32
U32 = mybir.dt.uint32
ALU = mybir.AluOpType
ACT = mybir.ActivationFunctionType
AX = mybir.AxisListType

P = 128
BATCHES, SEQ, D = 4, 512, 128
TB = SEQ // P
NT = BATCHES * TB
TOKENS = BATCHES * SEQ
KEYS, CTX = 32, 96
HEADS = 16
HD = D // HEADS
GROUP = P // KEYS
E, F = 8, 512
FC = F // P
TOP = 2
EPS = 1e-5
CLAMP = 10000.0
BIG = 3.4e38
REGION = TOKENS + P
PAD_ROW = E * REGION
FFN_TILES = (TOP * TOKENS + E * (P - 1)) // P
MAP = FFN_TILES + 1
W_ROW = D + 4
AT_DEST, AT_GATE = D, D + 1
NOWHERE = 1 << 20
UNROLL = 4
LOOPS = (FFN_TILES - 2) // UNROLL
assert FFN_TILES == 39 and LOOPS == 9

R_B1, R_LNW = {0: 0, 1: E * FC}, 2 * E * FC
R_LNB = R_LNW + E
R_BQ, R_BK, R_RB1 = {0: R_LNB + E, 1: R_LNB + E + 1}, {0: R_LNB + E + 2, 1: R_LNB + E + 3}, R_LNB + E + 4
R_BV = R_RB1 + 1
N_SMALL = R_BV + 1

AT_B1, AT_B2 = F, F + FC
W_TABLE = F + FC + D
STAGED = 4


def one(i):
    return bass.ds(i, 1)


def reached(j, n):
    return not isinstance(j, int) or j >= n


def build(nc, a, out, sent, contrib):
    with ExitStack() as ctx:
        def sb(name, shape, dt=F32):
            return ctx.enter_context(nc.sbuf_tensor(name, shape, dt))

        sems = {}

        def sem(name):
            if name not in sems:
                sems[name] = ctx.enter_context(nc.semaphore(name))
            return sems[name]

        bank = [ctx.enter_context(nc.psum_tensor(f"bank{i}", [P, 512], F32)) for i in range(8)]

        x_sb = sb("x_sb", [P, NT, D])
        ident = sb("ident", [P, P])
        ones_f = sb("ones_f", [P, P])
        ones_b = sb("ones_b", [P, P], BF16)
        earlier = sb("earlier", [P, P], BF16)
        head_mask = sb("head_mask", [P, HEADS])
        desc = sb("desc", [P, E])
        region_at = sb("region_at", [P, E])
        tile_no = sb("tile_no", [P, MAP])
        minus_half = sb("minus_half", [P, NT])
        zero_i = sb("zero_i", [P, 2], I32)
        pool_carrier = sb("pool_carrier", [P, UNROLL, 2], I32)
        pad_tile = sb("pad_tile", [P, W_ROW])

        small_rows = sb("small_rows", [N_SMALL, P])
        col = sb("col", [P, N_SMALL])
        ctx_sb = sb("ctx_sb", [P, CTX])
        ctxT = sb("ctxT", [CTX, P])
        ctxT4 = sb("ctxT4", [CTX, BATCHES, GROUP, KEYS])
        wq = [sb(f"wq{l}", [D, D]) for l in range(2)]
        wk = [sb(f"wk{l}", [CTX, D]) for l in range(2)]
        wv = [sb(f"wv{l}", [CTX, D]) for l in range(2)]
        wo = sb("wo", [D, D])
        bias_row = sb("bias_row", [1, 3, D])
        wg = sb("wg", [D, E])
        rw1 = sb("rw1", [D, D])
        rw2 = sb("rw2", [D, E])
        rb2 = sb("rb2", [P, E])
        alpha = sb("alpha", [P, E])
        table = [sb(f"table{l}", [P, E, W_TABLE]) for l in range(2)]
        w2 = [sb(f"w2_{l}", [P, E, FC, D]) for l in range(2)]

        kT = sb("kT", [D, 2, P])
        v_wide = sb("v_wide", [P, BATCHES, TB, D])
        k_wide = sb("k_wide", [P, BATCHES, HEADS, KEYS])
        v_head = sb("v_head", [P, BATCHES, HEADS, HD + 1])
        ctx_mean = sb("ctx_mean", [CTX, BATCHES])
        v_mean = sb("v_mean", [D, BATCHES])
        even_row = sb("even_row", [1, BATCHES, D])
        out_bias = sb("out_bias", [1, BATCHES, D])

        bn = sb("bn", [P, NT, 6])
        mv = sb("mv", [P, NT, 2])
        var_eps = sb("var_eps", [P, NT])
        rstd = sb("rstd", [P, NT])
        z_a = sb("z_a", [P, TB, D])
        zT_a = sb("zT_a", [P, SEQ])
        qT = sb("qT", [P, 2, SEQ])
        top_score = sb("top_score", [P, TB])
        shifted = sb("shifted", [P, TB, KEYS])
        prob_sum = sb("prob_sum", [P, TB])
        prob_scale = sb("prob_scale", [P, TB])
        probsT = sb("probsT", [P, P])

        bn_r = sb("bn_r", [P, TB, 6])
        mv_r = sb("mv_r", [P, TB, 2])
        var_r = sb("var_r", [P, BATCHES, 2, TB])
        rstd_r = sb("rstd_r", [P, BATCHES, 2, TB])
        shift_r = sb("shift_r", [P, BATCHES, TB])
        z_r = sb("z_r", [P, TB, D])
        zT_r = sb("zT_r", [P, SEQ])
        hidT = sb("hidT", [P, SEQ])
        logit = sb("logit", [P, TB, E])
        rest = sb("rest", [P, TB, E])
        best = sb("best", [P, TOP, TB])
        tied = sb("tied", [P, TB, E])
        key = sb("key", [P, TOP, TB])
        hot = sb("hot", [P, TOP, TB, E])
        picked = sb("picked", [P, TB, E], BF16)
        picked_now = sb("picked_now", [P, E])
        picked_before = sb("picked_before", [P, E], BF16)
        row_of = sb("row_of", [P, TB, E])
        spread = sb("spread", [P, TOP, TB, E])
        slot_f = sb("slot_f", [P, TOP, TB])
        slot = sb("slot", [P, BATCHES, TOP, TB], I32)
        gap = sb("gap", [P, TB])
        ratio = sb("ratio", [P, TB])
        total = sb("total", [P, TB])
        gate = sb("gate", [P, TOP, TB])
        alpha_hot = sb("alpha_hot", [P, TOP, TB, E])
        alpha_of = sb("alpha_of", [P, TOP, TB])
        row = sb("row", [P, NT, TOP, W_ROW])

        count = sb("count", [P, E])
        pad_at = sb("pad_at", [P, E], I32)
        count_up = sb("count_up", [P, E], I32)
        tiles_i = sb("tiles_i", [P, E], I32)
        tiles_f = sb("tiles_f", [P, E])
        tiles_end = sb("tiles_end", [P, E])
        passed = sb("passed", [P, MAP, E])
        expert_f = sb("expert_f", [P, MAP])
        first_f = sb("first_f", [P, MAP])
        expert = sb("expert", [P, MAP], I32)
        row_base = sb("row_base", [P, MAP], I32)

        xs = sb("xs", [P, UNROLL, W_ROW])
        meta = sb("meta", [P, UNROLL, 2])
        xT = sb("xT", [P, 2, P])
        staged = sb("staged", [P, STAGED, W_TABLE])
        hid = sb("hid", [P, 2, F])
        y_raw = sb("y_raw", [P, 2, D])
        y_out = sb("y_out", [P, UNROLL, D])
        back = sb("back", [P, BATCHES, TOP, TB, D])

        max_all = sb("max_all", [P, NT, HEADS])
        max_clip = sb("max_clip", [P, NT, HEADS])
        nan_seen = sb("nan_seen", [P, NT])
        nan_junk = sb("nan_junk", [P, 2, HEADS * KEYS], BF16)
        nan_sum = sb("nan_sum", [P, 1])
        all_numbers = sb("all_numbers", [P, 1])
        keep_bits = sb("keep_bits", [P, 1], I32)
        guard = sb("guard", [P, 1])
        sc = sb("sc", [P, 2, HEADS, KEYS])
        pT = sb("pT", [P, 2, SEQ])
        head_scale = sb("head_scale", [P, 2, HEADS])
        att = sb("att", [P, 2, TB, D])
        attT = back[:, :, 0, :, :]

        x_dram = a["x"].rearrange("b (t p) d -> p (b t) d", p=P)
        out_dram = out.rearrange("b (t p) d -> p (b t) d", p=P)
        w1_dram = [a["L0_ffn_fc1_w"], a["L1_ffn_we1"]]
        w2_dram = [a["L0_ffn_fc2_w"], a["L1_ffn_we2"]]
        b1_dram = [a["L0_ffn_fc1_b"], a["L1_ffn_be1"]]
        b2_dram = [a["L0_ffn_fc2_b"], a["L1_ffn_be2"]]
        SCALE = [float(D) ** -0.5, float(HD) ** -0.5]
        N_SMALL_DMAS, N_BIAS_DMAS = 10, 3
        SCALED_BY = (0, 3, 6, E)
        WEIGHED = (7, 1)
        block = ctx.enter_context(nc.Block())

        def steps(*stages):
            for step in range(BATCHES + max(lag for _, lag in stages)):
                for stage, lag in stages:
                    if 0 <= step - lag < BATCHES:
                        stage(step - lag)

        def nth(l, b):
            return l * BATCHES + b + 1

        def loads_before(l, u):
            return l * len(range(u, FFN_TILES, UNROLL))

        def vec(ap):
            return ap.rearrange("(o n) -> o n", o=1)

        @block.sync
        def _(sp):
            sp.dma_start(ctx_sb[:, :], a["ctx_768"].rearrange("b k c -> (b k) c")).then_inc(sem("ctx_loaded"), 16)
            sp.dma_start(x_sb[:, 0:TB, :], x_dram[:, 0:TB, :]).then_inc(sem("x_first"), 16)
            sp.dma_start(wk[0][:, :], a["L0_xattn_Wk"]).then_inc(sem("attn_loaded0"), 16)
            sp.dma_start(wv[0][:, :], a["L0_xattn_Wv"]).then_inc(sem("attn_loaded0"), 16)
            sp.dma_start(wq[0][:, :], a["L0_xattn_Wq"]).then_inc(sem("attn_loaded0"), 16)
            sp.dma_start(x_sb[:, TB:, :], x_dram[:, TB:, :]).then_inc(sem("x_rest"), 16)
            sp.dma_start(wg[:, :], a["L0_ffn_Wg"]).then_inc(sem("router_loaded0"), 16)
            sp.dma_start(alpha[:, :], a["L0_ffn_alpha"].partition_broadcast(P)).then_inc(sem("router_loaded0"), 16)
            sp.dma_start(wk[1][:, :], a["L1_xattn_Wk"]).then_inc(sem("attn_loaded1"), 16)
            sp.dma_start(wv[1][:, :], a["L1_xattn_Wv"]).then_inc(sem("attn_loaded1"), 16)
            sp.dma_start(wq[1][:, :], a["L1_xattn_Wq"]).then_inc(sem("attn_loaded1"), 16)
            sp.dma_start(wo[:, :], a["L1_xattn_Wo"]).then_inc(sem("attn_loaded1"), 16)
            for l in range(2):
                sp.dma_start(table[l][:, :, 0:F], w1_dram[l].rearrange("e d f -> d e f")).then_inc(sem(f"w1_loaded{l}"), 16)
                sp.dma_start(w2[l][:, :, :, :], w2_dram[l].rearrange("e (c p) d -> p e c d", p=P)).then_inc(sem(f"w2_loaded{l}"), 16)
                sp.dma_start(table[l][:, :, AT_B2:], b2_dram[l].rearrange("e d -> (e d)").partition_broadcast(P).rearrange("p (e d) -> p e d", e=E))\
                    .then_inc(sem(f"w2_loaded{l}"), 16)
            sp.dma_start(rw1[:, :], a["L1_ffn_rw1"]).then_inc(sem("router_loaded1"), 16)
            sp.dma_start(rw2[:, :], a["L1_ffn_rw2"]).then_inc(sem("router_loaded1"), 16)
            sp.dma_start(rb2[:, :], a["L1_ffn_rb2"].partition_broadcast(P)).then_inc(sem("router_loaded1"), 16)
            sp.wait_ge(sem("pad_tile_ready"), 2)
            for l in range(2):
                sp.dma_start(sent[l][PAD_ROW:PAD_ROW + P, :], pad_tile[:, :]).then_inc(sem("pad_written"), 16)

            for l in range(2):
                sp.wait_ge(sem("pad_known"), l + 1)
                for e in range(E):
                    r = sp.value_load(pad_at[0:1, e:e + 1], min_val=0, max_val=PAD_ROW - P)
                    sp.dma_start(sent[l][bass.ds(r, P), :], pad_tile[:, :]).then_inc(sem("pad_written"), 16)
                sp.wait_ge(sem("map_ready"), l + 1)
                sp.wait_ge(sem("pad_written"), 16 * (2 + E * (l + 1)))
                sp.wait_ge(sem("rows_sent"), 16 * TOP * NT * (l + 1))

                before = l * FFN_TILES

                def load(i, c):
                    j = UNROLL * i + c
                    if reached(j, UNROLL):
                        sp.wait_ge(sem("x_turned"), before + j - UNROLL + 1)
                        sp.wait_ge(sem("meta_ready"), before + j - UNROLL + 1)
                    r = sp.value_load(row_base[0:1, one(j)], min_val=0, max_val=PAD_ROW)
                    sp.dma_start(xs[:, c % UNROLL, :], sent[l][bass.ds(r, P), :]).then_inc(sem(f"xs_loaded_{c % UNROLL}"), 16)

                for c in range(UNROLL):
                    load(0, c)
                with sp.Fori(1, LOOPS) as i:
                    for c in range(UNROLL):
                        load(i, c)
                for j in range(UNROLL * LOOPS, FFN_TILES):
                    load(j // UNROLL, j % UNROLL)

                for u in range(UNROLL):
                    sp.wait_ge(sem(f"y_sent_{u}"), 16 * loads_before(l + 1, u))
                for b in range(BATCHES):
                    src = contrib[l][b * SEQ:(b + 1) * SEQ, :]
                    sp.dma_start(back[:, b, 0, :, :], src.rearrange("(t p) d -> p t d", p=P)).then_inc(sem(f"back_{b}"), 16)
            for b in range(BATCHES):
                sp.wait_ge(sem("added"), 2 * nth(1, b))
                sp.dma_start(out_dram[:, TB * b:TB * (b + 1), :], x_sb[:, TB * b:TB * (b + 1), :]).then_inc(sem("stored"), 16)
            sp.wait_ge(sem("stored"), 16 * BATCHES)

        @block.gpsimd
        def _(pool):
            g = nc.gpsimd

            def power_a(order, n0, n1):
                pool.wait_ge(sem("var_ready_a"), order)
                g.tensor_tensor(rstd[:, n0:n1], var_eps[:, n0:n1], minus_half[:, 0:n1 - n0], ALU.pow).then_inc(sem("rstd_ready_a"), 1)

            def power_r(l, b):
                k = TOP if l == 0 else 1
                pool.wait_ge(sem("var_ready_r"), nth(l, b))
                g.tensor_tensor(rstd_r[:, b, 0:k, :], var_r[:, b, 0:k, :], minus_half[:, 0:k * TB].rearrange("p (k t) -> p k t", k=k),
                                ALU.pow).then_inc(sem("rstd_ready_r"), 1)

            g.memset(ident[:, :], 0.0).then_inc(sem("const_step"), 1)
            pool.wait_ge(sem("const_step"), 1)
            g.affine_select(out=ident[:, :], in_=ident[:, :], compare_op=ALU.not_equal, fill=1.0, base=0,
                            pattern=[[-1, P]], channel_multiplier=1).then_inc(sem("ident_ready"), 1)
            g.memset(ones_f[:, :], 1.0)
            g.memset(v_wide[:, :, :, :], 0.0).then_inc(sem("v_cleared"), 1)
            g.memset(minus_half[:, :], -0.5).then_inc(sem("const_step"), 1)
            pool.wait_ge(sem("const_step"), 2)
            power_a(1, 0, TB)
            g.memset(ones_b[:, :], 1.0)
            g.memset(earlier[:, :], 1.0)
            g.memset(head_mask[:, :], 1.0)
            g.memset(zero_i[:, :], 0)
            g.memset(row[:, :, :, D:], 0.0)
            g.memset(v_head[:, :, :, :], 0.0).then_inc(sem("v_cleared"), 1)
            g.memset(pad_tile[:, :], 0.0).then_inc(sem("const_step"), 1)
            pool.wait_ge(sem("const_step"), 3)
            g.iota(desc[:, :], pattern=[[-1, E]], base=E, channel_multiplier=0, allow_small_or_imprecise_dtypes=True)
            g.iota(region_at[:, :], pattern=[[REGION, E]], base=0, channel_multiplier=0, allow_small_or_imprecise_dtypes=True)
            g.iota(tile_no[:, :], pattern=[[1, MAP]], base=0, channel_multiplier=0, allow_small_or_imprecise_dtypes=True)
            power_a(2, TB, NT)
            g.affine_select(out=earlier[:, :], in_=earlier[:, :], compare_op=ALU.is_gt, fill=0.0, base=0,
                            pattern=[[1, P]], channel_multiplier=-1).then_inc(sem("consts_ready"), 1)
            g.iota(pad_tile[:, AT_DEST:AT_DEST + 1].bitcast(I32), pattern=[[0, 1]], base=NOWHERE,
                   channel_multiplier=0).then_inc(sem("pad_tile_ready"), 2)
            for k in range(TOP):
                g.iota(row[:, :, k, AT_DEST:AT_DEST + 1].bitcast(I32), pattern=[[P, NT], [0, 1]], base=k * TOKENS,
                       channel_multiplier=1)
            g.affine_select(out=head_mask[:, :], in_=head_mask[:, :], compare_op=ALU.is_ge, fill=0.0, base=0,
                            pattern=[[-HD, HEADS]], channel_multiplier=1).then_inc(sem("const_step"), 1)
            pool.wait_ge(sem("const_step"), 4)
            g.affine_select(out=head_mask[:, :], in_=head_mask[:, :], compare_op=ALU.is_ge, fill=0.0, base=HD - 1,
                            pattern=[[HD, HEADS]], channel_multiplier=-1).then_inc(sem("const_step"), 1)
            pool.wait_ge(sem("const_step"), 5)
            power_r(0, 0)
            pool.wait_ge(sem("kT_ready"), 2)
            for b in range(BATCHES):
                m = g.tensor_tensor(k_wide[:, b, :, :], kT[:, 1, KEYS * b:KEYS * (b + 1)].unsqueeze(1).broadcast_to([P, HEADS, KEYS]),
                                    head_mask[:, :].unsqueeze(2).broadcast_to([P, HEADS, KEYS]), ALU.mult)
            m.then_inc(sem("k_wide_ready"), 1)

            last_place = pool.to_reg(TOP * TOKENS - 1)

            def scatter_ffn(l):
                before = l * FFN_TILES
                def copy_meta(i, c):
                    j, s = UNROLL * i + c, c % UNROLL
                    pool.wait_ge(sem(f"xs_loaded_{s}"), 16 * (loads_before(l, s) + i + c // UNROLL + 1))
                    if reached(j, UNROLL):
                        pool.wait_ge(sem("y_gated"), before + j - UNROLL + 1)
                        pool.wait_ge(sem(f"y_sent_{s}"), 16 * (loads_before(l, s) + i + c // UNROLL))
                    g.tensor_tensor(meta[:, s, :].bitcast(I32), xs[:, s, AT_DEST:AT_DEST + 2].bitcast(I32), zero_i[:, :], ALU.add)\
                        .then_inc(sem("meta_ready"), 1)

                def send(i, c):
                    j, s = UNROLL * i + c, c % UNROLL
                    pool.wait_ge(sem("meta_ready"), before + j + 1)
                    pool.wait_ge(sem("y_gated"), before + j + 1)
                    g.tensor_tensor(pool_carrier[:, s, :], zero_i[:, :], zero_i[:, :], ALU.add)
                    pool.indirect_dma_start(
                        out=contrib[l], out_offset=bass.IndirectOffsetOnAxis(ap=meta[:, s, 0:1].bitcast(I32), axis=0),
                        in_=y_out[:, s, :], in_offset=None, bounds_check=last_place, oob_is_err=False)\
                        .then_inc(sem(f"y_sent_{s}"), 16)

                def body(i, c):
                    j = UNROLL * i + c
                    if not isinstance(j, int) or j + 1 < FFN_TILES:
                        copy_meta(i, c + 1)
                    send(i, c - 1)

                copy_meta(0, 0)
                copy_meta(0, 1)
                for j in range(1, UNROLL + 1):
                    body(0, j)
                with pool.Fori(1, LOOPS) as i:
                    for c in range(1, UNROLL + 1):
                        body(i, c)
                for j in range(UNROLL * LOOPS + 1, FFN_TILES + 1):
                    body(LOOPS, j - UNROLL * LOOPS)

            def scatter_rows(l, b, t0, t1):
                pool.wait_ge(sem("slots_ready"), nth(l, b))
                pool.wait_ge(sem("rows_copied"), nth(l, b))
                pool.wait_ge(sem("rows_gated"), nth(l, b))
                for t in range(t0, t1):
                    for k in range(TOP):
                        pool.indirect_dma_start(
                            out=sent[l], out_offset=bass.IndirectOffsetOnAxis(ap=slot[:, b, k, t:t + 1], axis=0),
                            in_=row[:, TB * b + t, k, :], in_offset=None).then_inc(sem("rows_sent"), 16)

            for l in range(2):
                if l == 1:
                    for b in range(BATCHES):
                        power_a(2 + b + 1, TB * b, TB * (b + 1))
                    power_r(1, 0)
                power_r(l, 1)
                for b in range(BATCHES):
                    scatter_rows(l, b, 0, TB - 1)
                    if b + 2 < BATCHES:
                        power_r(l, b + 2)
                    scatter_rows(l, b, TB - 1, TB)
                scatter_ffn(l)

        @block.tensor
        def _(pe):
            mm = nc.tensor.matmul

            def keys(l, dst):
                mm(dst[:, 0:P], wk[l][:, :], ctxT[:, :], start=True, stop=True).then_inc(sem("k_ready"), 1)

            def values(l, dst):
                mm(dst[:, :].rearrange("p (b d) -> p b d", b=BATCHES), ones_f[0:1, :],
                   bias_row[0:1, l:l + 1, :].broadcast_to([1, BATCHES, D]), start=True, stop=False)
                for b in range(BATCHES):
                    m = mm(dst[:, D * b:D * (b + 1)], ctxT4[:, b, :, :].rearrange("c g k -> c (g k)"),
                           wv[l][:, :], start=False, stop=(b == BATCHES - 1))
                m.then_inc(sem("v_ready"), 1)

            def setup():
                pe.wait_ge(sem("ident_ready"), 1)
                pe.wait_ge(sem("ctx_loaded"), 16)
                nc.tensor.transpose(bank[1][0:CTX, 0:P], ctx_sb[:, :], ident[:, :]).then_inc(sem("ctx_turned"), 1)
                pe.wait_ge(sem("small_loaded"), 16 * N_SMALL_DMAS)
                nc.tensor.transpose(bank[0][:, 0:N_SMALL], small_rows[:, :], ident[0:N_SMALL, 0:N_SMALL]).then_inc(sem("cols_turned"), 1)
                pe.wait_ge(sem("ctxT_ready"), 2)
                pe.wait_ge(sem("v_cleared"), 1)
                pe.wait_ge(sem("bias_loaded"), 16 * N_BIAS_DMAS)
                pe.wait_ge(sem("attn_loaded0"), 16 * 3)
                keys(0, bank[2])
                values(0, bank[3])
                pe.wait_ge(sem("cols_ready"), 1)

            def turn(n, l, b, src, dst):
                pe.wait_ge(sem(f"z_ready_{n}"), nth(l, b))
                for t in range(TB):
                    m = nc.tensor.transpose(dst[:, P * t:P * (t + 1)], src[:, t, :], ident[:, :])
                m.then_inc(sem(f"z_turned_{n}"), 1)

            def turn_a0(b):
                turn("a", 0, b, z_a, bank[0])

            def project_q0(b):
                pe.wait_ge(sem("zT_copied_a"), nth(0, b))
                mm(bank[1][:, :], wq[0][:, :], zT_a[:, :], start=True, stop=True).then_inc(sem("q_done"), 1)

            def scores0(b):
                pe.wait_ge(sem("qT_copied"), nth(0, b))
                pe.wait_ge(sem("kT_ready"), 1)
                for t in range(TB):
                    m = mm(bank[2][:, KEYS * t:KEYS * (t + 1)], qT[:, b % 2, P * t:P * (t + 1)], kT[:, 0, KEYS * b:KEYS * (b + 1)],
                           start=True, stop=True)
                m.then_inc(sem("scores_done0"), 1)

            def turn_probs0(b):
                if b == 0:
                    pe.wait_ge(sem("v_wide_ready"), 1)
                pe.wait_ge(sem("probs_ready0"), b + 1)
                nc.tensor.transpose(bank[3][:, 0:P], shifted[:, :, :].rearrange("p t k -> p (t k)"), ident[:, :])\
                    .then_inc(sem("probs_turned0"), 1)

            def attend0(b):
                pe.wait_ge(sem("probsT_copied0"), b + 1)
                mm(bank[4][:, :], probsT[:, :], v_wide[:, b, :, :].rearrange("p t d -> p (t d)"), start=True, stop=True)\
                    .then_inc(sem("att_done"), 1)

            def turn_r(l, b):
                turn("r", l, b, z_r, bank[5])

            def logits(l, b):
                pe.wait_ge(sem("zT_copied_r"), nth(l, b))
                if l == 0:
                    pe.wait_ge(sem("router_loaded0"), 16 * 2)
                feat, w = zT_r, wg
                if l == 1:
                    mm(bank[0][:, :], rw1[:, :], zT_r[:, :], start=True, stop=True).then_inc(sem("router_hidden"), 1)
                    pe.wait_ge(sem("router_silu"), b + 1)
                    feat, w = hidT, rw2
                for t in range(TB):
                    m = mm(bank[6][:, E * t:E * (t + 1)], feat[:, P * t:P * (t + 1)], w[:, :], start=True, stop=True)
                m.then_inc(sem("logits_done"), 1)

            def rank(l, b):
                pe.wait_ge(sem("picked_ready"), nth(l, b))
                pe.wait_ge(sem("consts_ready"), 1)
                rank = bank[6][:, 64:64 + TB * E]
                chosen = picked[:, :, :].rearrange("p t e -> p (t e)")
                mm(rank, earlier[:, :], chosen, start=True, stop=False)
                for s in range(1, TB):
                    mm(rank[:, E * s:], ones_b[:, :], chosen[:, 0:E * (TB - s)], start=False, stop=False)
                mm(rank.rearrange("p (t e) -> p t e", e=E), ones_b[:, :], picked_before[:, :].unsqueeze(1).broadcast_to([P, TB, E]),
                   start=False, stop=True).then_inc(sem("rank_done"), 1)

            def count_experts(l):
                pe.wait_ge(sem("picked_summed"), nth(l, BATCHES - 1))
                pe.wait_ge(sem("rank_read"), nth(l, BATCHES - 1))
                mm(bank[6][:, 0:E], ones_b[:, :], picked_before[:, :], start=True, stop=True).then_inc(sem("counts_done"), 1)

            def prepare(b):
                if b == 0:
                    pe.wait_ge(sem("attn_loaded1"), 16 * 4)
                    pe.wait_ge(sem("ctx_mean_ready"), 1)
                    mm(bank[7][:, P:P + BATCHES], wv[1][:, :], ctx_mean[:, :], start=True, stop=True)
                    keys(1, bank[7])
                if b == 1:
                    pe.wait_ge(sem("w1_loaded0"), 16)
                    pe.wait_ge(sem("v_mean_ready"), 1)
                    for n in range(E * FC):
                        m = mm(bank[7][:, n:n + 1], table[0][:, n // FC, P * (n % FC):P * (n % FC + 1)],
                               col[:, R_LNB + n // FC:R_LNB + n // FC + 1], start=True, stop=True)
                    m.then_inc(sem("norm_bias_done"), 1)
                if b == 2:
                    pe.wait_ge(sem("b1_ready"), 1)
                    values(1, bank[7])
                if b == 3:
                    pe.wait_ge(sem("v_head_ready"), 2)
                    for n in range(BATCHES):
                        m = mm(bank[7][0:1, D * n:D * (n + 1)], v_mean[:, n:n + 1], wo[:, :], start=True, stop=True)
                    m.then_inc(sem("even_row_done"), 1)

            def ffn(l):
                before = l * FFN_TILES
                def turn_rows(i, c):
                    j, s = UNROLL * i + c, c % UNROLL
                    pe.wait_ge(sem(f"xs_loaded_{s}"), 16 * (loads_before(l, s) + i + c // UNROLL + 1))
                    if reached(j, 2):
                        pe.wait_ge(sem("xT_ready"), before + j - 1)
                    nc.tensor.transpose(bank[c % 2][:, 0:P], xs[:, s, 0:D], ident[:, :]).then_inc(sem("x_turned"), 1)

                def up(i, c):
                    j, h = UNROLL * i + c, c % 2
                    pe.wait_ge(sem("xT_ready"), before + j + 1)
                    pe.wait_ge(sem("staged"), before + j + 1)
                    if reached(j, 2):
                        pe.wait_ge(sem("hid_biased"), before + j - 1)
                    for f in range(FC):
                        m = mm(bank[2 + h][:, P * f:P * (f + 1)], staged[:, c % STAGED, P * f:P * (f + 1)], xT[:, h, :],
                               start=True, stop=True)
                    m.then_inc(sem("up_done"), 1)

                def down(i, c):
                    j, h = UNROLL * i + c, c % 2
                    e = pe.value_load(expert[0:1, one(j)], min_val=0, max_val=E - 1)
                    pe.wait_ge(sem("hid_ready"), before + j + 1)
                    if reached(j, 2):
                        pe.wait_ge(sem("y_biased"), before + j - 1)
                    for f in range(FC):
                        m = mm(bank[4 + h][:, 0:D], hid[:, h, P * f:P * (f + 1)],
                               w2[l][:, one(e), f, :].rearrange("p o d -> p (o d)"), start=(f == 0), stop=(f == FC - 1))
                    m.then_inc(sem("down_done"), 1)

                def body(i, c):
                    j = UNROLL * i + c
                    if not isinstance(j, int) or j + 1 < FFN_TILES:
                        turn_rows(i, c + 1)
                    if not isinstance(j, int) or j < FFN_TILES:
                        up(i, c)
                    if reached(j, 1):
                        down(i, c - 1)

                turn_rows(0, 0)
                for j in range(UNROLL + 1):
                    body(0, j)
                with pe.Fori(1, LOOPS) as i:
                    for c in range(1, UNROLL + 1):
                        body(i, c)
                for j in range(UNROLL * LOOPS + 1, FFN_TILES + 1):
                    body(LOOPS, j - UNROLL * LOOPS)

            def turn_a1(b):
                turn("a", 1, b, z_a, bank[0])

            def project_q1(b):
                pe.wait_ge(sem("zT_copied_a"), nth(1, b))
                mm(bank[0][:, :], wq[1][:, :], zT_a[:, :], start=True, stop=True).then_inc(sem("q_done"), 1)

            def scores1(n):
                b, t = divmod(n, TB)
                if n >= 2:
                    pe.wait_ge(sem("nan_seen"), n - 1)
                pe.wait_ge(sem("qT_copied"), nth(1, b))
                pe.wait_ge(sem("k_wide_ready"), 1)
                mm(bank[2 + n % 2][:, :], qT[:, b % 2, P * t:P * (t + 1)], k_wide[:, b, :, :].rearrange("p h k -> p (h k)"),
                   start=True, stop=True).then_inc(sem("scores_done1"), 1)

            def turn_probs1(n):
                pe.wait_ge(sem("exp_done1"), n + 1)
                for c in range(TB):
                    m = nc.tensor.transpose(bank[4 + n % 2][:, P * c:P * (c + 1)],
                                            sc[:, n % 2, GROUP * c:GROUP * (c + 1), :].rearrange("p h k -> p (h k)"), ident[:, :])
                m.then_inc(sem("p_turned1"), 1)

            def weigh(n):
                pe.wait_ge(sem("pT_copied1"), n + 1)
                if n >= 2:
                    pe.wait_ge(sem("att_ready1"), n - 1)
                w = GROUP * (HD + 1)
                for c in range(TB):
                    m = mm(bank[WEIGHED[n % 2]][:, w * c:w * (c + 1)], pT[:, n % 2, P * c:P * (c + 1)],
                           v_head[:, n // TB, GROUP * c:GROUP * (c + 1), :].rearrange("p h d -> p (h d)"), start=True, stop=True)
                m.then_inc(sem("weighed1"), 1)

            def turn_att1(b):
                pe.wait_ge(sem("att_ready1"), TB * (b + 1))
                if b >= 1:
                    pe.wait_ge(sem("attT_copied1"), b)
                for t in range(TB):
                    m = nc.tensor.transpose(bank[6][:, P * t:P * (t + 1)], att[:, b % 2, t, :], ident[:, :])
                m.then_inc(sem("att_turned1"), 1)

            def attention1():
                pe.wait_ge(sem("v_head_ready"), 2)
                turn_a1(0)
                project_q1(0)
                scores1(0)
                scores1(1)
                for n in range(NT):
                    b, t = divmod(n, TB)
                    if n + 2 < NT:
                        scores1(n + 2)
                    turn_probs1(n)
                    weigh(n)
                    if t == 0 and b + 1 < BATCHES:
                        turn_a1(b + 1)
                    if t == 1 and b + 1 < BATCHES:
                        project_q1(b + 1)
                    if t == 2 and b >= 1:
                        turn_att1(b - 1)
                pe.wait_ge(sem("nan_seen"), NT)
                mm(bank[0][:, 0:NT], ones_f[:, :], nan_seen[:, :], start=True, stop=True).then_inc(sem("nan_summed"), 1)
                turn_att1(BATCHES - 1)

            def output1(b):
                pe.wait_ge(sem("out_bias_ready"), 1)
                pe.wait_ge(sem("att_kept1"), b + 1)
                out = bank[4 - b % 2]
                mm(out[:, :].rearrange("p (t d) -> p t d", t=TB), ones_f[0:1, :], out_bias[0:1, b:b + 1, :].broadcast_to([1, TB, D]),
                   start=True, stop=False)
                for t in range(TB):
                    m = mm(out[:, D * t:D * (t + 1)], attT[:, b, t, :], wo[:, :], start=False, stop=(t == TB - 1))
                m.then_inc(sem("att_done"), 1)

            setup()
            steps((lambda b: turn_r(0, b), 2), (turn_a0, 0), (lambda b: logits(0, b), 2), (project_q0, 0), (turn_probs0, 1),
                  (scores0, 0), (attend0, 1), (lambda b: rank(0, b), 2), (prepare, 1))
            count_experts(0)
            pe.wait_ge(sem("w2_loaded0"), 16 * 2)
            ffn(0)
            attention1()
            pe.wait_ge(sem("router_loaded1"), 16 * 3)
            steps((lambda b: turn_r(1, b), 1), (output1, 0), (lambda b: logits(1, b), 1), (lambda b: rank(1, b), 1))
            count_experts(1)
            pe.wait_ge(sem("w2_loaded1"), 16 * 2)
            ffn(1)

        @block.scalar
        def _(act):
            s = nc.scalar
            small = [(R_BK[0], 1, vec(a["L0_xattn_bk"])), (R_BK[1], 1, vec(a["L1_xattn_bk"])),
                     (R_BQ[0], 1, vec(a["L0_xattn_bq"])), (R_BQ[1], 1, vec(a["L1_xattn_bq"])),
                     (R_BV, 1, vec(a["L1_xattn_bv"])), (R_RB1, 1, vec(a["L1_ffn_rb1"])),
                     (R_LNW, E, a["L0_ffn_ln_w"]), (R_LNB, E, a["L0_ffn_ln_b"]),
                     (R_B1[0], E * FC, b1_dram[0].rearrange("e (c p) -> (e c) p", p=P)),
                     (R_B1[1], E * FC, b1_dram[1].rearrange("e (c p) -> (e c) p", p=P))]
            for r, n, src in small:
                act.dma_start(small_rows[r:r + n, :], src).then_inc(sem("small_loaded"), 16)
            for n, name in enumerate(["L0_xattn_bv", "L1_xattn_bv", "L1_xattn_bo"]):
                act.dma_start(bias_row[0:1, n, :], vec(a[name])).then_inc(sem("bias_loaded"), 16)

            def spread_v_wide():
                act.wait_ge(sem("v_cleared"), 1)
                act.wait_ge(sem("v_ready"), 1)
                for r in range(GROUP):
                    p = slice(KEYS * r, KEYS * (r + 1))
                    m = s.copy(v_wide[p, :, r, :], bank[3][p, :].rearrange("p (b d) -> p b d", b=BATCHES))
                m.then_inc(sem("v_wide_ready"), 1)

            def prepare(b):
                if b == 1:
                    act.wait_ge(sem("norm_bias_done"), 1)
                if b >= 1:
                    for e in range(SCALED_BY[b - 1], SCALED_BY[b]):
                        s.activation(table[0][:, e, 0:F], table[0][:, e, 0:F], ACT.Copy, scale=col[:, R_LNW + e:R_LNW + e + 1])\
                            .then_inc(sem("w1_scaled"), 1)
                if b == 2:
                    act.wait_ge(sem("v_cleared"), 2)
                    act.wait_ge(sem("v_ready"), 2)
                    for r in range(GROUP):
                        p = slice(KEYS * r, KEYS * (r + 1))
                        m = s.copy(v_head[p, :, r::GROUP, 0:HD], bank[7][p, :].rearrange("p (b h d) -> p b h d", b=BATCHES, d=HD)[:, :, r::GROUP, :])
                    m.then_inc(sem("v_head_ready"), 1)

            def copy_zT(n, l, b, dst, src):
                act.wait_ge(sem(f"z_turned_{n}"), nth(l, b))
                s.copy(dst[:, :], src[:, :]).then_inc(sem(f"zT_copied_{n}"), 1)

            def add_bq(l, b):
                act.wait_ge(sem("q_done"), nth(l, b))
                s.activation(qT[:, b % 2, :], bank[1 - l][:, :], ACT.Identity, bias=col[:, R_BQ[l]:R_BQ[l] + 1]).then_inc(sem("qT_copied"), 1)

            def exp0(b):
                act.wait_ge(sem("shifted0"), b + 1)
                s.activation(shifted[:, :, :], shifted[:, :, :], ACT.Exp).then_inc(sem("exp_done0"), 1)

            def copy_probsT0(b):
                act.wait_ge(sem("probs_turned0"), b + 1)
                s.copy(probsT[:, :], bank[3][:, 0:P]).then_inc(sem("probsT_copied0"), 1)

            def copy_rows(l, b):
                act.wait_ge(sem("z_ready_r"), nth(l, b))
                for t in range(TB):
                    n = TB * b + t
                    if l == 0:
                        m = s.activation(row[:, n, :, 0:D], x_sb[:, n:n + 1, :].broadcast_to([P, TOP, D]), ACT.Identity,
                                         bias=shift_r[:, b, t:t + 1], scale=rstd_r[:, b, 1, t:t + 1])
                    else:
                        m = s.copy(row[:, n, :, 0:D], z_r[:, t:t + 1, :].broadcast_to([P, TOP, D]))
                m.then_inc(sem("rows_copied"), 1)

            def silu1(b):
                act.wait_ge(sem("router_hidden"), b + 1)
                s.activation(hidT[:, :], bank[0][:, :], ACT.Silu, bias=col[:, R_RB1:R_RB1 + 1]).then_inc(sem("router_silu"), 1)

            def ratio_of(l, b):
                act.wait_ge(sem("gap_ready"), nth(l, b))
                s.activation(ratio[:, :], gap[:, :], ACT.Exp).then_inc(sem("ratio_ready"), 1)

            def ffn(l):
                before = l * FFN_TILES
                func = [ACT.Gelu_apprx_tanh, ACT.Silu][l]

                def copy_xT(i, c):
                    j, h = UNROLL * i + c, c % 2
                    act.wait_ge(sem("x_turned"), before + j + 1)
                    if reached(j, 2):
                        act.wait_ge(sem("up_done"), before + j - 1)
                    s.copy(xT[:, h, :], bank[h][:, 0:P]).then_inc(sem("xT_ready"), 1)

                def activate(i, c):
                    j, h = UNROLL * i + c, c % 2
                    act.wait_ge(sem("hid_biased"), before + j + 1)
                    s.activation(hid[:, h, :], hid[:, h, :], func).then_inc(sem("hid_ready"), 1)

                def apply_gate(i, c):
                    j, q = UNROLL * i + c, c % UNROLL
                    act.wait_ge(sem("y_biased"), before + j + 1)
                    act.wait_ge(sem("meta_ready"), before + j + 1)
                    if reached(j, UNROLL):
                        act.wait_ge(sem(f"y_sent_{q}"), 16 * (loads_before(l, q) + i + c // UNROLL))
                    s.activation(y_out[:, q, :], y_raw[:, c % 2, :], ACT.Copy, scale=meta[:, q, 1:2]).then_inc(sem("y_gated"), 1)

                def body(i, c):
                    j = UNROLL * i + c
                    if not isinstance(j, int) or j + 1 < FFN_TILES:
                        copy_xT(i, c + 1)
                    if not isinstance(j, int) or j < FFN_TILES:
                        activate(i, c)
                    if reached(j, 1):
                        apply_gate(i, c - 1)

                copy_xT(0, 0)
                for j in range(UNROLL + 1):
                    body(0, j)
                with act.Fori(1, LOOPS) as i:
                    for c in range(1, UNROLL + 1):
                        body(i, c)
                for j in range(UNROLL * LOOPS + 1, FFN_TILES + 1):
                    body(LOOPS, j - UNROLL * LOOPS)

            def load_back(l):
                for u in range(UNROLL):
                    act.wait_ge(sem(f"y_sent_{u}"), 16 * loads_before(l + 1, u))
                for b in range(BATCHES):
                    src = contrib[l][TOKENS + b * SEQ:TOKENS + (b + 1) * SEQ, :]
                    act.dma_start(back[:, b, 1, :, :], src.rearrange("(t p) d -> p t d", p=P)).then_inc(sem(f"back_{b}"), 16)

            def find_nan(n):
                act.wait_ge(sem("clipped1"), n + 1)
                if n >= 2:
                    act.wait_ge(sem("nan_seen"), n - 1)
                s.activation(nan_junk[:, n % 2, :], bank[2 + n % 2][:, :], ACT.Tanh, accum_out=nan_seen[:, n:n + 1])\
                    .then_inc(sem("nan_seen"), 1)

            def copy_attT(b):
                act.wait_ge(sem("att_turned1"), b + 1)
                s.copy(attT[:, b, :, :].rearrange("p t q -> p (t q)"), bank[6][:, :]).then_inc(sem("attT_copied1"), 1)

            def attention1():
                copy_zT("a", 1, 0, zT_a, bank[0])
                add_bq(1, 0)
                for n in range(NT):
                    b, t = divmod(n, TB)
                    find_nan(n)
                    act.wait_ge(sem("shift_done1"), n + 1)
                    s.activation(sc[:, n % 2, :, :], sc[:, n % 2, :, :], ACT.Exp).then_inc(sem("exp_done1"), 1)
                    act.wait_ge(sem("p_turned1"), n + 1)
                    s.copy(pT[:, n % 2, :], bank[4 + n % 2][:, :]).then_inc(sem("pT_copied1"), 1)
                    if t == 0 and b + 1 < BATCHES:
                        copy_zT("a", 1, b + 1, zT_a, bank[0])
                    if t == 1 and b + 1 < BATCHES:
                        add_bq(1, b + 1)
                    if t == 2 and b >= 1:
                        copy_attT(b - 1)
                copy_attT(BATCHES - 1)

            act.wait_ge(sem("cols_ready"), 1)
            spread_v_wide()
            steps((lambda b: copy_zT("r", 0, b, zT_r, bank[5]), 2), (lambda b: copy_zT("a", 0, b, zT_a, bank[0]), 0),
                  (lambda b: add_bq(0, b), 0), (copy_probsT0, 1), (lambda b: copy_rows(0, b), 2), (lambda b: ratio_of(0, b), 2),
                  (exp0, 0), (prepare, 1))
            ffn(0)
            load_back(0)
            attention1()
            steps((lambda b: copy_zT("r", 1, b, zT_r, bank[5]), 1), (silu1, 1), (lambda b: copy_rows(1, b), 1),
                  (lambda b: ratio_of(1, b), 1))
            ffn(1)
            load_back(1)

        @block.vector
        def _(dve):
            v = nc.vector

            dve_steps = [0]

            def then_wait(m):
                dve_steps[0] += 1
                m.then_inc(sem("dve_step"), 1)
                dve.wait_ge(sem("dve_step"), dve_steps[0])

            def per_tile(ap, n):
                return ap.unsqueeze(2).broadcast_to([P, TB, n])

            def stats_a(l, n0, n1):
                for n in range(n0, n1):
                    m = v.bn_stats(bn[:, n, :], x_sb[:, n, :])
                then_wait(m)
                for n in range(n0, n1):
                    m = v.bn_aggr(mv[:, n, :], bn[:, n, :])
                then_wait(m)
                v.tensor_scalar(var_eps[:, n0:n1], mv[:, n0:n1, 1], EPS, None, ALU.add).then_inc(sem("var_ready_a"), 1)

            def normalise_a(l, b, powers):
                dve.wait_ge(sem("rstd_ready_a"), powers)
                for t in range(TB):
                    n = TB * b + t
                    m = v.tensor_scalar(z_a[:, t, :], x_sb[:, n, :], mv[:, n, 0:1], rstd[:, n:n + 1], ALU.subtract, ALU.mult)
                m.then_inc(sem("z_ready_a"), 1)

            def setup():
                dve.wait_ge(sem("ctx_turned"), 1)
                v.tensor_copy(ctxT[:, :], bank[1][0:CTX, 0:P]).then_inc(sem("ctxT_ready"), 1)
                v.tensor_copy(ctxT4[:, :, :, :], bank[1][0:CTX, 0:P].rearrange("c (b k) -> c b k", b=BATCHES)
                              .unsqueeze(2).broadcast_to([CTX, BATCHES, GROUP, KEYS])).then_inc(sem("ctxT_ready"), 1)
                dve.wait_ge(sem("x_first"), 16)
                stats_a(0, 0, TB)
                dve.wait_ge(sem("ctxT_ready"), 2)
                then_wait(v.tensor_reduce(ctx_mean[:, :], ctxT[:, :].rearrange("c (b k) -> c b k", b=BATCHES), AX.X, ALU.add))
                v.tensor_scalar(ctx_mean[:, :], ctx_mean[:, :], 1.0 / KEYS, None, ALU.mult).then_inc(sem("ctx_mean_ready"), 1)
                dve.wait_ge(sem("cols_turned"), 1)
                v.tensor_copy(col[:, :], bank[0][:, 0:N_SMALL]).then_inc(sem("cols_ready"), 1)
                dve.wait_ge(sem("k_ready"), 1)
                dve.wait_ge(sem("cols_ready"), 1)
                v.tensor_scalar(kT[:, 0, :], bank[2][:, 0:P], col[:, R_BK[0]:R_BK[0] + 1], SCALE[0], ALU.add, ALU.mult)\
                    .then_inc(sem("kT_ready"), 1)
                normalise_a(0, 0, 1)
                dve.wait_ge(sem("x_rest"), 16)
                stats_a(0, TB, NT)

            def prepare(b):
                if b == 0:
                    dve.wait_ge(sem("k_ready"), 2)
                    v.tensor_scalar(kT[:, 1, :], bank[7][:, 0:P], col[:, R_BK[1]:R_BK[1] + 1], SCALE[1], ALU.add, ALU.mult)\
                        .then_inc(sem("kT_ready"), 1)
                    v.tensor_scalar(v_mean[:, :], bank[7][:, P:P + BATCHES], col[:, R_BV:R_BV + 1], None, ALU.add)\
                        .then_inc(sem("v_mean_ready"), 1)
                    dve.wait_ge(sem("v_cleared"), 2)
                    for r in range(GROUP):
                        m = v.memset(v_head[KEYS * r:KEYS * (r + 1), :, r::GROUP, HD:HD + 1].rearrange("p b h o -> p b (h o)"), 1.0)
                    m.then_inc(sem("v_head_ready"), 1)
                if b == 1:
                    dve.wait_ge(sem("norm_bias_done"), 1)
                    v.tensor_copy(table[1][:, :, AT_B1:AT_B2], col[:, R_B1[1]:R_B1[1] + E * FC].rearrange("p (e c) -> p e c", e=E))
                    v.tensor_tensor(table[0][:, :, AT_B1:AT_B2], bank[7][:, 0:E * FC].rearrange("p (e c) -> p e c", e=E),
                                    col[:, R_B1[0]:R_B1[0] + E * FC].rearrange("p (e c) -> p e c", e=E), ALU.add).then_inc(sem("b1_ready"), 1)
                if b == 3:
                    dve.wait_ge(sem("even_row_done"), 1)
                    v.tensor_copy(even_row[:, :, :], bank[7][0:1, :].rearrange("o (b d) -> o b d", b=BATCHES)).then_inc(sem("even_row_ready"), 1)

            def shift_scores0(b):
                dve.wait_ge(sem("scores_done0"), b + 1)
                scores = bank[2][:, 0:TB * KEYS].rearrange("p (t k) -> p t k", k=KEYS)
                then_wait(v.tensor_reduce(top_score[:, :], scores, AX.X, ALU.max))
                v.tensor_tensor(shifted[:, :, :], scores, per_tile(top_score[:, :], KEYS), ALU.subtract).then_inc(sem("shifted0"), 1)

            def normalise_probs0(b):
                dve.wait_ge(sem("exp_done0"), b + 1)
                then_wait(v.tensor_reduce(prob_sum[:, :], shifted[:, :, :], AX.X, ALU.add))
                then_wait(v.reciprocal(prob_scale[:, :], prob_sum[:, :]))
                v.tensor_tensor(shifted[:, :, :], shifted[:, :, :], per_tile(prob_scale[:, :], KEYS), ALU.mult).then_inc(sem("probs_ready0"), 1)

            def add_attention(l, b):
                mine = x_sb[:, TB * b:TB * (b + 1), :]
                dve.wait_ge(sem("att_done"), nth(l, b))
                src = bank[4] if l == 0 else bank[4 - b % 2]
                then_wait(v.tensor_tensor(mine, mine, src[:, :].rearrange("p (t d) -> p t d", t=TB), ALU.add))
                for t in range(TB):
                    m = v.bn_stats(bn_r[:, t, :], x_sb[:, TB * b + t, :])
                then_wait(m)
                for t in range(TB):
                    m = v.bn_aggr(mv_r[:, t, :], bn_r[:, t, :])
                then_wait(m)
                m = v.tensor_scalar(var_r[:, b, 0, :], mv_r[:, :, 1], EPS, None, ALU.add)
                if l == 0:
                    m = v.tensor_scalar(var_r[:, b, 1, :], mv_r[:, :, 1], 1.0 + EPS, EPS * EPS, ALU.mult, ALU.add)
                m.then_inc(sem("var_ready_r"), 1)

            def normalise_r(l, b):
                dve.wait_ge(sem("rstd_ready_r"), nth(l, b))
                if l == 0:
                    v.scalar_tensor_tensor(out=shift_r[:, b, :], in0=mv_r[:, :, 0], scalar=-1.0, in1=rstd_r[:, b, 1, :],
                                           op0=ALU.mult, op1=ALU.mult)
                elif b >= 1:
                    dve.wait_ge(sem("rows_copied"), nth(1, b - 1))
                for t in range(TB):
                    m = v.tensor_scalar(z_r[:, t, :], x_sb[:, TB * b + t, :], mv_r[:, t, 0:1], rstd_r[:, b, 0, t:t + 1],
                                        ALU.subtract, ALU.mult)
                m.then_inc(sem("z_ready_r"), 1)

            def add_normalised1(b):
                mine = x_sb[:, TB * b:TB * (b + 1), :]
                dve.wait_ge(sem("z_ready_r"), nth(1, b))
                v.tensor_tensor(mine, mine, z_r[:, :, :], ALU.add).then_inc(sem("z_added1"), 1)

            def pick(l, b):
                bc_e = [P, TB, E]
                dve.wait_ge(sem("logits_done"), nth(l, b))
                lg = bank[6][:, 0:TB * E].rearrange("p (t e) -> p t e", e=E)
                if l == 0:
                    then_wait(v.tensor_copy(logit[:, :, :], lg))
                else:
                    then_wait(v.tensor_tensor(logit[:, :, :], lg, rb2[:, :].unsqueeze(1).broadcast_to(bc_e), ALU.add))
                by_e = desc[:, :].unsqueeze(1).broadcast_to(bc_e)
                src = logit
                for k in range(TOP):
                    then_wait(v.tensor_reduce(best[:, k, :], src[:, :, :], AX.X, ALU.max))
                    then_wait(v.tensor_tensor(tied[:, :, :], src[:, :, :], per_tile(best[:, k, :], E), ALU.is_equal))
                    then_wait(v.tensor_tensor(tied[:, :, :], tied[:, :, :], by_e, ALU.mult))
                    then_wait(v.tensor_reduce(key[:, k, :], tied[:, :, :], AX.X, ALU.max))
                    then_wait(v.tensor_tensor(hot[:, k, :, :], by_e, per_tile(key[:, k, :], E), ALU.is_equal))
                    if k == 0:
                        then_wait(v.scalar_tensor_tensor(out=rest[:, :, :], in0=hot[:, 0, :, :], scalar=-BIG, in1=logit[:, :, :],
                                                         op0=ALU.mult, op1=ALU.add))
                        src = rest
                v.tensor_tensor(picked[:, :, :], hot[:, 0, :, :], hot[:, 1, :, :], ALU.add).then_inc(sem("picked_ready"), 1)
                v.tensor_tensor(gap[:, :], best[:, 1, :], best[:, 0, :], ALU.subtract).then_inc(sem("gap_ready"), 1)

            def place(l, b):
                alphas = alpha[:, :].unsqueeze(1).broadcast_to([P, TOP * TB, E])
                if l == 0:
                    v.tensor_tensor(alpha_hot[:, :, :, :].rearrange("p k t e -> p (k t) e"), hot[:, :, :, :].rearrange("p k t e -> p (k t) e"),
                                    alphas, ALU.mult).then_inc(sem("alpha_step"), 1)
                dve.wait_ge(sem("picked_ready"), nth(l, b))
                then_wait(v.tensor_reduce(picked_now[:, :], picked[:, :, :].rearrange("p t e -> p e t"), AX.X, ALU.add))
                dve.wait_ge(sem("rank_done"), nth(l, b))
                v.tensor_tensor(row_of[:, :, :], bank[6][:, 64:64 + TB * E].rearrange("p (t e) -> p t e", e=E),
                                region_at[:, :].unsqueeze(1).broadcast_to([P, TB, E]), ALU.add).then_inc(sem("rank_read"), 1)
                v.tensor_tensor(picked_before[:, :], picked_before[:, :], picked_now[:, :], ALU.add).then_inc(sem("picked_summed"), 1)
                dve.wait_ge(sem("rank_read"), nth(l, b))
                m = v.tensor_tensor(spread[:, :, :, :], hot[:, :, :, :], row_of[:, :, :].unsqueeze(1).broadcast_to([P, TOP, TB, E]), ALU.mult)
                dve.wait_ge(sem("ratio_ready"), nth(l, b))
                then_wait(v.tensor_scalar(total[:, :], ratio[:, :], 1.0, None, ALU.add))
                v.reciprocal(gate[:, 0, :], total[:, :]).then_inc(sem("gates"), 1)
                then_wait(v.tensor_reduce(slot_f[:, :, :], spread[:, :, :, :], AX.X, ALU.add))
                v.tensor_copy(slot[:, b, :, :], slot_f[:, :, :]).then_inc(sem("slots_ready"), 1)
                dve.wait_ge(sem("gates"), 2 * nth(l, b) - 2 + 1)
                v.tensor_tensor(gate[:, 1, :], gate[:, 0, :], ratio[:, :], ALU.mult).then_inc(sem("gates"), 1)
                out = row[:, TB * b:TB * (b + 1), :, AT_GATE]
                if l == 0:
                    dve.wait_ge(sem("alpha_step"), 2 * b + 1)
                    v.tensor_reduce(alpha_of[:, :, :], alpha_hot[:, :, :, :], AX.X, ALU.add).then_inc(sem("alpha_step"), 1)
                    dve.wait_ge(sem("alpha_step"), 2 * b + 2)
                dve.wait_ge(sem("gates"), 2 * nth(l, b) - 2 + 2)
                if l == 0:
                    v.tensor_tensor(out, gate[:, :, :].rearrange("p k t -> p t k"), alpha_of[:, :, :].rearrange("p k t -> p t k"), ALU.mult)\
                        .then_inc(sem("rows_gated"), 1)
                else:
                    v.tensor_copy(out, gate[:, :, :].rearrange("p k t -> p t k")).then_inc(sem("rows_gated"), 1)

            def map_tiles(l):
                by_tile = [P, MAP, E]
                dve.wait_ge(sem("counts_done"), l + 1)
                then_wait(v.tensor_copy(count[:, :], bank[6][:, 0:E]))
                v.tensor_tensor(pad_at[:, :], count[:, :], region_at[:, :], ALU.add).then_inc(sem("pad_known"), 1)
                then_wait(v.tensor_scalar(count_up[:, :], count[:, :], float(P - 1), None, ALU.add))
                then_wait(v.tensor_scalar(tiles_i[:, :], count_up[:, :], 7, None, ALU.arith_shift_right))
                then_wait(v.tensor_copy(tiles_f[:, :], tiles_i[:, :]))
                then_wait(v.tensor_tensor_scan(tiles_end[:, :], ones_f[:, 0:E], tiles_f[:, :], 0.0, ALU.mult, ALU.add))
                then_wait(v.tensor_tensor(passed[:, :, :], tiles_end[:, :].unsqueeze(1).broadcast_to(by_tile),
                                          tile_no[:, :].unsqueeze(2).broadcast_to(by_tile), ALU.is_le))
                then_wait(v.tensor_reduce(expert_f[:, :], passed[:, :, :], AX.X, ALU.add))
                then_wait(v.tensor_tensor(passed[:, :, :], passed[:, :, :], tiles_f[:, :].unsqueeze(1).broadcast_to(by_tile), ALU.mult))
                then_wait(v.tensor_reduce(first_f[:, :], passed[:, :, :], AX.X, ALU.add))
                then_wait(v.tensor_tensor(first_f[:, :], tile_no[:, :], first_f[:, :], ALU.subtract))
                then_wait(v.scalar_tensor_tensor(out=first_f[:, :], in0=expert_f[:, :], scalar=float(REGION // P), in1=first_f[:, :],
                                                 op0=ALU.mult, op1=ALU.add))
                v.tensor_scalar(row_base[:, :], first_f[:, :], float(P), float(PAD_ROW), ALU.mult, ALU.min)
                v.tensor_scalar(expert[:, :], expert_f[:, :], float(E - 1), None, ALU.min).then_inc(sem("map_ready"), 1)
                dve.wait_ge(sem("map_ready"), l + 1)

            def ffn(l):
                before = l * FFN_TILES
                def stage(i, c):
                    j = UNROLL * i + c
                    e = dve.value_load(expert[0:1, one(UNROLL * i + c)], min_val=0, max_val=E - 1)
                    if reached(j, STAGED):
                        dve.wait_ge(sem("y_biased"), before + j - STAGED + 1)
                    v.tensor_copy(staged[:, c % STAGED, :], table[l][:, one(e), :].rearrange("p o f -> p (o f)")).then_inc(sem("staged"), 1)

                def add_b1(i, c):
                    j, h = UNROLL * i + c, c % 2
                    dve.wait_ge(sem("up_done"), before + j + 1)
                    dve.wait_ge(sem("staged"), before + j + 1)
                    if reached(j, 2):
                        dve.wait_ge(sem("down_done"), before + j - 1)
                    v.tensor_tensor(hid[:, h, :].rearrange("p (f q) -> p f q", f=FC), bank[2 + h][:, :].rearrange("p (f q) -> p f q", f=FC),
                                    staged[:, c % STAGED, AT_B1:AT_B2].unsqueeze(2).broadcast_to([P, FC, P]), ALU.add)\
                        .then_inc(sem("hid_biased"), 1)

                def add_b2(i, c):
                    j, h = UNROLL * i + c, c % 2
                    dve.wait_ge(sem("down_done"), before + j + 1)
                    if reached(j, 2):
                        dve.wait_ge(sem("y_gated"), before + j - 1)
                    v.tensor_tensor(y_raw[:, h, :], bank[4 + h][:, 0:D], staged[:, c % STAGED, AT_B2:], ALU.add)\
                        .then_inc(sem("y_biased"), 1)

                def body(i, c):
                    j = UNROLL * i + c
                    if not isinstance(j, int) or j < FFN_TILES:
                        add_b1(i, c)
                    if not isinstance(j, int) or j + 2 < FFN_TILES:
                        stage(i, c + 2)
                    if reached(j, 1):
                        add_b2(i, c - 1)

                stage(0, 0)
                stage(0, 1)
                for j in range(UNROLL + 1):
                    body(0, j)
                with dve.Fori(1, LOOPS) as i:
                    for c in range(1, UNROLL + 1):
                        body(i, c)
                for j in range(UNROLL * LOOPS + 1, FFN_TILES + 1):
                    body(LOOPS, j - UNROLL * LOOPS)

            def add_back(l, b):
                mine = x_sb[:, TB * b:TB * (b + 1), :]
                dve.wait_ge(sem(f"back_{b}"), 16 * TOP * (l + 1))
                v.tensor_tensor(mine, mine, back[:, b, 0, :, :], ALU.add).then_inc(sem("added"), 1)
                dve.wait_ge(sem("added"), 2 * nth(l, b) - 1)
                v.tensor_tensor(mine, mine, back[:, b, 1, :, :], ALU.add).then_inc(sem("added"), 1)

            def attention1():
                for n in range(NT + 2):
                    h = n % 2
                    b, t = divmod(n, TB)
                    if n < NT:
                        scores = bank[2 + h][:, :].rearrange("p (h k) -> p h k", k=KEYS)
                        dve.wait_ge(sem("scores_done1"), n + 1)
                        if t == 0 and b + 1 < BATCHES:
                            normalise_a(1, b + 1, 2 + b + 2)
                        then_wait(v.tensor_reduce(max_all[:, n, :], scores, AX.X, ALU.max))
                        then_wait(v.tensor_scalar(max_clip[:, n, :], max_all[:, n, :], -CLAMP, CLAMP, ALU.max, ALU.min))
                        if n >= 2:
                            dve.wait_ge(sem("p_turned1"), n - 1)
                        v.scalar_tensor_tensor(out=sc[:, h, :, :], in0=scores, scalar=-CLAMP,
                                               in1=max_clip[:, n, :].unsqueeze(2).broadcast_to([P, HEADS, KEYS]), op0=ALU.max, op1=ALU.subtract)\
                            .then_inc(sem("clipped1"), 1)
                        dve.wait_ge(sem("clipped1"), n + 1)
                        v.tensor_scalar(sc[:, h, :, :], sc[:, h, :, :], 0.0, None, ALU.min).then_inc(sem("shift_done1"), 1)
                    if n >= 2:
                        divide(n - 2)
                    if n == NT:
                        guard_against_nan()

            def divide(n):
                dve.wait_ge(sem("weighed1"), n + 1)
                got = bank[WEIGHED[n % 2]][:, 0:HEADS * (HD + 1)].rearrange("p (h d) -> p h d", d=HD + 1)
                then_wait(v.reciprocal(head_scale[:, n % 2, :], got[:, :, HD]))
                v.tensor_tensor(att[:, n // TB % 2, n % TB, :].rearrange("p (h d) -> p h d", d=HD), got[:, :, 0:HD],
                                head_scale[:, n % 2, :].unsqueeze(2).broadcast_to([P, HEADS, HD]), ALU.mult).then_inc(sem("att_ready1"), 1)

            def guard_against_nan():
                dve.wait_ge(sem("nan_summed"), 1)
                then_wait(v.tensor_reduce(nan_sum[:, :], bank[0][:, 0:NT], AX.X, ALU.add))
                then_wait(v.tensor_tensor(all_numbers[:, :], nan_sum[:, :], nan_sum[:, :], ALU.is_equal))
                v.tensor_scalar(keep_bits[:, :], all_numbers[:, :], -1.0, None, ALU.mult)
                then_wait(v.tensor_scalar(guard[:, :], all_numbers[:, :], -1.0, 1.0, ALU.mult, ALU.add))
                dve.wait_ge(sem("even_row_ready"), 1)
                v.scalar_tensor_tensor(out=out_bias[:, :, :], in0=even_row[:, :, :], scalar=guard[0:1, 0:1],
                                       in1=bias_row[0:1, 2:3, :].broadcast_to([1, BATCHES, D]), op0=ALU.mult, op1=ALU.add)\
                    .then_inc(sem("out_bias_ready"), 1)

            def keep_att1(b):
                dve.wait_ge(sem("attT_copied1"), b + 1)
                mine = attT[:, b, :, :].rearrange("p t q -> p (t q)").bitcast(I32)
                v.tensor_tensor(mine, mine, keep_bits[:, :].broadcast_to([P, SEQ]), ALU.bitwise_and).then_inc(sem("att_kept1"), 1)

            setup()
            v.memset(picked_before[:, :], 0.0)
            dve.wait_ge(sem("router_loaded0"), 16 * 2)
            steps((lambda b: normalise_r(0, b), 2), (lambda b: normalise_a(0, b, 2) if b else None, 0), (normalise_probs0, 1),
                  (lambda b: pick(0, b), 2), (lambda b: add_attention(0, b), 1), (shift_scores0, 0), (lambda b: place(0, b), 2),
                  (prepare, 1))
            map_tiles(0)
            dve.wait_ge(sem("b1_ready"), 1)
            dve.wait_ge(sem("w1_scaled"), E)
            dve.wait_ge(sem("w2_loaded0"), 16 * 2)
            ffn(0)
            for b in range(BATCHES):
                add_back(0, b)
                dve.wait_ge(sem("added"), 2 * nth(0, b))
                stats_a(1, TB * b, TB * (b + 1))
                if b == 1:
                    normalise_a(1, 0, 2 + 1)
            v.memset(picked_before[:, :], 0.0)
            attention1()
            dve.wait_ge(sem("router_loaded1"), 16 * 3)
            keep_att1(0)
            steps((lambda b: normalise_r(1, b), 1), (lambda b: keep_att1(b + 1) if b + 1 < BATCHES else None, 0),
                  (lambda b: add_attention(1, b), 0), (add_normalised1, 1), (lambda b: pick(1, b), 1), (lambda b: place(1, b), 1))
            map_tiles(1)
            dve.wait_ge(sem("w1_loaded1"), 16)
            dve.wait_ge(sem("w2_loaded1"), 16 * 2)
            ffn(1)
            for b in range(BATCHES):
                add_back(1, b)



_INS = ['x', 'ctx_768', 'L0_xattn_Wq', 'L0_xattn_bq', 'L0_xattn_Wk', 'L0_xattn_bk', 'L0_xattn_Wv', 'L0_xattn_bv',
        'L0_ffn_Wg', 'L0_ffn_alpha', 'L0_ffn_ln_w', 'L0_ffn_ln_b', 'L0_ffn_fc1_w', 'L0_ffn_fc1_b', 'L0_ffn_fc2_w',
        'L0_ffn_fc2_b', 'L1_xattn_Wq', 'L1_xattn_bq', 'L1_xattn_Wk', 'L1_xattn_bk', 'L1_xattn_Wv', 'L1_xattn_bv',
        'L1_xattn_Wo', 'L1_xattn_bo', 'L1_ffn_rw1', 'L1_ffn_rb1', 'L1_ffn_rw2', 'L1_ffn_rb2', 'L1_ffn_we1',
        'L1_ffn_be1', 'L1_ffn_we2', 'L1_ffn_be2']


def kernel(**inputs):
    import numpy as _np
    import concourse.bacc as _bacc
    from concourse import mybir as _mybir
    from concourse.bass_utils import run_bass_kernel_spmd as _run

    nc = _bacc.Bacc("TRN2", target_bir_lowering=False, num_devices=1)
    arrays, aps = {}, {}
    for name in _INS:
        arr = _np.ascontiguousarray(inputs[name])
        arrays[f"in_{name}"] = arr
        aps[name] = nc.dram_tensor(f"in_{name}", arr.shape, _mybir.dt.from_np(arr.dtype), kind="ExternalInput").ap()
    out = nc.dram_tensor("out_0", (BATCHES, SEQ, D), F32, kind="ExternalOutput").ap()
    sent = [nc.dram_tensor(f"sent{l}", (PAD_ROW + P, W_ROW), F32, kind="Internal").ap() for l in range(2)]
    contrib = [nc.dram_tensor(f"contrib{l}", (TOP * TOKENS, D), F32, kind="Internal").ap() for l in range(2)]
    build(nc, aps, out, sent, contrib)
    r = _run(nc, [arrays], core_ids=[0])
    return r.results[0]["out_0"]
```

```python
from contextlib import ExitStack

import concourse.bass as bass
from concourse import mybir

F32 = mybir.dt.float32
BF16 = mybir.dt.bfloat16
I32 = mybir.dt.int32
U32 = mybir.dt.uint32
ALU = mybir.AluOpType
ACT = mybir.ActivationFunctionType
AX = mybir.AxisListType

P = 128
BATCHES, SEQ, D = 4, 512, 128
TB = SEQ // P
NT = BATCHES * TB
TOKENS = BATCHES * SEQ
KEYS, CTX = 32, 96
HEADS = 16
HD = D // HEADS
GROUP = P // KEYS
E, F = 8, 512
FC = F // P
TOP = 2
EPS = 1e-5
CLAMP = 10000.0
BIG = 3.4e38
REGION = TOKENS + P
PAD_ROW = E * REGION
FFN_TILES = (TOP * TOKENS + E * (P - 1)) // P
MAP = FFN_TILES + 1
W_ROW = D + 4
AT_DEST, AT_GATE = D, D + 1
NOWHERE = 1 << 20
UNROLL = 4
LOOPS = (FFN_TILES - 2) // UNROLL
assert FFN_TILES == 39 and LOOPS == 9

R_B1, R_LNW = {0: 0, 1: E * FC}, 2 * E * FC
R_LNB = R_LNW + E
R_RB1 = R_LNB + E
R_BV = R_RB1 + 1
R_BQ, R_BK = {1: R_BV + 1}, {1: R_BV + 2}
N_SMALL = R_BV + 3
R_BK[0], R_BQ[0] = N_SMALL, N_SMALL + 1
N_FIRST = 2

AT_B1, AT_B2, AT_NORM = F, F + FC, F + FC + D
W_TABLE = [AT_NORM + 2, AT_NORM]
STAGED = 4


def one(i):
    return bass.ds(i, 1)


def reached(j, n):
    return not isinstance(j, int) or j >= n


def build(nc, a, out, sent, contrib):
    with ExitStack() as ctx:
        def sb(name, shape, dt=F32):
            return ctx.enter_context(nc.sbuf_tensor(name, shape, dt))

        sems = {}

        def sem(name):
            if name not in sems:
                sems[name] = ctx.enter_context(nc.semaphore(name))
            return sems[name]

        bank = [ctx.enter_context(nc.psum_tensor(f"bank{i}", [P, 512], F32)) for i in range(8)]

        x_sb = sb("x_sb", [P, NT, D])
        ident = sb("ident", [P, P])
        ones_f = sb("ones_f", [P, P])
        ones_b = sb("ones_b", [P, P], BF16)
        earlier = sb("earlier", [P, P], BF16)
        head_mask = sb("head_mask", [P, HEADS])
        desc = sb("desc", [P, E])
        region_at = sb("region_at", [P, E])
        tile_no = sb("tile_no", [P, MAP])
        minus_half = sb("minus_half", [P, NT])
        zero_i = sb("zero_i", [P, 2], I32)
        pool_carrier = sb("pool_carrier", [P, UNROLL, 2], I32)
        pad_tile = sb("pad_tile", [P, W_ROW])

        small_rows = sb("small_rows", [N_SMALL, P])
        nothing = sb("nothing", [P, P], BF16)
        act_start = sb("act_start", [P, 1])
        first_rows = sb("first_rows", [N_FIRST, P])
        col = sb("col", [P, N_SMALL + N_FIRST])
        ctx_sb = sb("ctx_sb", [P, CTX])
        ctxT = sb("ctxT", [CTX, P])
        ctxT4 = sb("ctxT4", [CTX, BATCHES, GROUP, KEYS])
        wq = [sb(f"wq{l}", [D, D]) for l in range(2)]
        wk = [sb(f"wk{l}", [CTX, D]) for l in range(2)]
        wv = [sb(f"wv{l}", [CTX, D]) for l in range(2)]
        wo = sb("wo", [D, D])
        bias_row = sb("bias_row", [1, 3, D])
        wg = sb("wg", [D, E])
        rw1 = sb("rw1", [D, D])
        rw2 = sb("rw2", [D, E])
        rb2 = sb("rb2", [P, E])
        alpha = sb("alpha", [P, E])
        table = [sb(f"table{l}", [P, E, W_TABLE[l]]) for l in range(2)]
        w2 = [sb(f"w2_{l}", [P, E, FC, D]) for l in range(2)]

        kT = sb("kT", [D, 2, P])
        v_wide = sb("v_wide", [P, BATCHES, TB, D])
        k_wide = sb("k_wide", [P, BATCHES, HEADS, KEYS])
        v_head = sb("v_head", [P, BATCHES, HEADS, HD + 1])
        ctx_mean = sb("ctx_mean", [CTX, BATCHES])
        v_mean = sb("v_mean", [D, BATCHES])
        even_row = sb("even_row", [1, BATCHES, D])
        out_bias = sb("out_bias", [1, BATCHES, D])

        bn = sb("bn", [P, NT, 6])
        mv = sb("mv", [P, NT, 2])
        var_eps = sb("var_eps", [P, NT])
        rstd = sb("rstd", [P, NT])
        shift_a = sb("shift_a", [P, NT])
        z_a = sb("z_a", [P, TB, D])
        zT_a = sb("zT_a", [P, SEQ])
        qT = sb("qT", [P, 2, SEQ])
        top_score = sb("top_score", [P, TB])
        shifted = sb("shifted", [P, TB, KEYS])
        prob_sum = sb("prob_sum", [P, TB])
        prob_scale = sb("prob_scale", [P, TB])
        probsT = sb("probsT", [P, P])

        bn_r = sb("bn_r", [P, TB, 6])
        mv_r = sb("mv_r", [P, BATCHES, TB, 2])
        var_r = sb("var_r", [P, BATCHES, 2, TB])
        rstd_r = sb("rstd_r", [P, BATCHES, 2, TB])
        shift_r = sb("shift_r", [P, BATCHES, TB])
        z_r = sb("z_r", [P, 2, TB, D])
        zT_r = sb("zT_r", [P, SEQ])
        hidT = sb("hidT", [P, SEQ])
        logit = sb("logit", [P, TB, E])
        rest = sb("rest", [P, TB, E])
        best = sb("best", [P, TOP, TB])
        tied = sb("tied", [P, TB, E])
        key = sb("key", [P, TOP, TB])
        hot = sb("hot", [P, TOP, TB, E])
        picked = sb("picked", [P, TB, E], BF16)
        picked_now = sb("picked_now", [P, E])
        picked_before = sb("picked_before", [P, E], BF16)
        row_of = sb("row_of", [P, TB, E])
        spread = sb("spread", [P, TOP, TB, E])
        slot_f = sb("slot_f", [P, TOP, TB])
        slot = sb("slot", [P, BATCHES, TOP, TB], I32)
        gap = sb("gap", [P, TB])
        ratio = sb("ratio", [P, TB])
        total = sb("total", [P, TB])
        gate = sb("gate", [P, TOP, TB])
        alpha_hot = sb("alpha_hot", [P, TOP, TB, E])
        alpha_of = sb("alpha_of", [P, TOP, TB])
        row = sb("row", [P, NT, TOP, W_ROW])

        count = sb("count", [P, E])
        pad_at = sb("pad_at", [P, E], I32)
        count_up = sb("count_up", [P, E], I32)
        tiles_i = sb("tiles_i", [P, E], I32)
        tiles_f = sb("tiles_f", [P, E])
        tiles_end = sb("tiles_end", [P, E])
        passed = sb("passed", [P, MAP, E])
        expert_f = sb("expert_f", [P, MAP])
        first_f = sb("first_f", [P, MAP])
        expert = sb("expert", [P, MAP], I32)
        row_base = sb("row_base", [P, MAP], I32)

        xs = sb("xs", [P, UNROLL, W_ROW])
        meta = sb("meta", [P, UNROLL, 2])
        xT = sb("xT", [P, 2, P])
        staged = sb("staged", [P, STAGED, W_TABLE[0]])
        hid = sb("hid", [P, 2, F])
        y_raw = sb("y_raw", [P, 2, D])
        y_out = sb("y_out", [P, UNROLL, D])
        back = sb("back", [P, BATCHES, TOP, TB, D])

        max_all = sb("max_all", [P, NT, HEADS])
        max_clip = sb("max_clip", [P, NT, HEADS])
        nan_seen = sb("nan_seen", [P, NT])
        nan_junk = sb("nan_junk", [P, 2, HEADS * KEYS], BF16)
        nan_sum = sb("nan_sum", [P, 1])
        all_numbers = sb("all_numbers", [P, 1])
        keep_bits = sb("keep_bits", [P, 1], I32)
        guard = sb("guard", [P, 1])
        sc = sb("sc", [P, 2, HEADS, KEYS])
        pT = sb("pT", [P, 2, SEQ])
        head_scale = sb("head_scale", [P, 2, HEADS])
        att = sb("att", [P, 2, TB, D])
        attT = back[:, :, 0, :, :]

        x_dram = a["x"].rearrange("b (t p) d -> p (b t) d", p=P)
        out_dram = out.rearrange("b (t p) d -> p (b t) d", p=P)
        w1_dram = [a["L0_ffn_fc1_w"], a["L1_ffn_we1"]]
        w2_dram = [a["L0_ffn_fc2_w"], a["L1_ffn_we2"]]
        b1_dram = [a["L0_ffn_fc1_b"], a["L1_ffn_be1"]]
        b2_dram = [a["L0_ffn_fc2_b"], a["L1_ffn_be2"]]
        SCALE = [float(D) ** -0.5, float(HD) ** -0.5]
        N_SMALL_DMAS = 10
        LOGITS = (6, 7)
        WEIGHED = (7, 1)
        block = ctx.enter_context(nc.Block())

        def steps(*stages):
            for step in range(BATCHES + max(lag for _, lag in stages)):
                for stage, lag in stages:
                    if 0 <= step - lag < BATCHES:
                        stage(step - lag)

        def nth(l, b):
            return l * BATCHES + b + 1

        def loads_before(l, u):
            return l * len(range(u, FFN_TILES, UNROLL))

        def vec(ap):
            return ap.rearrange("(o n) -> o n", o=1)

        @block.sync
        def _(sp):
            sp.dma_start(ctx_sb[:, :], a["ctx_768"].rearrange("b k c -> (b k) c")).then_inc(sem("ctx_loaded"), 16)
            sp.dma_start(x_sb[:, 0:TB, :], x_dram[:, 0:TB, :]).then_inc(sem("x_first"), 16)
            sp.dma_start(wk[0][:, :], a["L0_xattn_Wk"]).then_inc(sem("attn_loaded0"), 16)
            sp.dma_start(wq[0][:, :], a["L0_xattn_Wq"]).then_inc(sem("attn_loaded0"), 16)
            sp.dma_start(wv[0][:, :], a["L0_xattn_Wv"]).then_inc(sem("attn_loaded0"), 16)
            sp.dma_start(x_sb[:, TB:, :], x_dram[:, TB:, :]).then_inc(sem("x_rest"), 16)
            sp.dma_start(wg[:, :], a["L0_ffn_Wg"]).then_inc(sem("router_loaded0"), 16)
            sp.dma_start(alpha[:, :], a["L0_ffn_alpha"].partition_broadcast(P)).then_inc(sem("router_loaded0"), 16)
            small = [(R_BK[1], 1, vec(a["L1_xattn_bk"])), (R_BQ[1], 1, vec(a["L1_xattn_bq"])),
                     (R_BV, 1, vec(a["L1_xattn_bv"])), (R_RB1, 1, vec(a["L1_ffn_rb1"])),
                     (R_LNW, E, a["L0_ffn_ln_w"]), (R_LNB, E, a["L0_ffn_ln_b"]),
                     (R_B1[0], E * FC, b1_dram[0].rearrange("e (c p) -> (e c) p", p=P)),
                     (R_B1[1], E * FC, b1_dram[1].rearrange("e (c p) -> (e c) p", p=P))]
            for r, n, src in small:
                sp.dma_start(small_rows[r:r + n, :], src).then_inc(sem("small_loaded"), 16)
            for n, name in enumerate(["L1_xattn_bv", "L1_xattn_bo"]):
                sp.dma_start(bias_row[0:1, 1 + n, :], vec(a[name])).then_inc(sem("small_loaded"), 16)
            for n, name in enumerate(["Wk", "Wv", "Wq", "Wo"]):
                sp.dma_start([wk[1], wv[1], wq[1], wo][n][:, :], a[f"L1_xattn_{name}"]).then_inc(sem("attn_loaded1"), 16)
            for l in range(2):
                sp.dma_start(table[l][:, :, 0:F], w1_dram[l].rearrange("e d f -> d e f")).then_inc(sem(f"w1_loaded{l}"), 16)
                sp.dma_start(w2[l][:, :, :, :], w2_dram[l].rearrange("e (c p) d -> p e c d", p=P)).then_inc(sem(f"w2_loaded{l}"), 16)
                sp.dma_start(table[l][:, :, AT_B2:AT_NORM], b2_dram[l].rearrange("e d -> (e d)").partition_broadcast(P).rearrange("p (e d) -> p e d", e=E))\
                    .then_inc(sem(f"w2_loaded{l}"), 16)
            sp.dma_start(rw1[:, :], a["L1_ffn_rw1"]).then_inc(sem("router_loaded1"), 16)
            sp.dma_start(rw2[:, :], a["L1_ffn_rw2"]).then_inc(sem("router_loaded1"), 16)
            sp.dma_start(rb2[:, :], a["L1_ffn_rb2"].partition_broadcast(P)).then_inc(sem("router_loaded1"), 16)
            sp.wait_ge(sem("pad_tile_ready"), 2)
            for l in range(2):
                sp.dma_start(sent[l][PAD_ROW:PAD_ROW + P, :], pad_tile[:, :]).then_inc(sem("pad_written"), 16)

            for l in range(2):
                sp.wait_ge(sem("pad_known"), l + 1)
                for e in range(E):
                    r = sp.value_load(pad_at[0:1, e:e + 1], min_val=0, max_val=PAD_ROW - P)
                    sp.dma_start(sent[l][bass.ds(r, P), :], pad_tile[:, :]).then_inc(sem("pad_written"), 16)
                sp.wait_ge(sem("map_ready"), l + 1)
                first_row = sp.value_load(row_base[0:1, one(0)], min_val=0, max_val=PAD_ROW)
                sp.wait_ge(sem("pad_written"), 16 * (2 + E * (l + 1)))
                sp.wait_ge(sem("rows_sent"), 16 * TOP * NT * (l + 1))

                before = l * FFN_TILES

                def load(i, c):
                    j = UNROLL * i + c
                    if reached(j, UNROLL):
                        sp.wait_ge(sem("x_turned"), before + j - UNROLL + 1)
                        sp.wait_ge(sem("meta_ready"), before + j - UNROLL + 1)
                    r = first_row if isinstance(j, int) and j == 0 else \
                        sp.value_load(row_base[0:1, one(j)], min_val=0, max_val=PAD_ROW)
                    sp.dma_start(xs[:, c % UNROLL, :], sent[l][bass.ds(r, P), :]).then_inc(sem(f"xs_loaded_{c % UNROLL}"), 16)

                for c in range(UNROLL):
                    load(0, c)
                with sp.Fori(1, LOOPS) as i:
                    for c in range(UNROLL):
                        load(i, c)
                for j in range(UNROLL * LOOPS, FFN_TILES):
                    load(j // UNROLL, j % UNROLL)

                for u in range(UNROLL):
                    sp.wait_ge(sem(f"y_sent_{u}"), 16 * loads_before(l + 1, u))
                for b in range(BATCHES):
                    src = contrib[l][b * SEQ:(b + 1) * SEQ, :]
                    sp.dma_start(back[:, b, 0, :, :], src.rearrange("(t p) d -> p t d", p=P)).then_inc(sem(f"back_{b}"), 16)
            for b in range(BATCHES):
                sp.wait_ge(sem("added"), nth(1, b))
                sp.dma_start(out_dram[:, TB * b:TB * (b + 1), :], x_sb[:, TB * b:TB * (b + 1), :]).then_inc(sem("stored"), 16)
            sp.wait_ge(sem("stored"), 16 * BATCHES)

        @block.gpsimd
        def _(pool):
            g = nc.gpsimd

            def power_a(order, n0, n1):
                pool.wait_ge(sem("var_ready_a"), order)
                g.tensor_tensor(rstd[:, n0:n1], var_eps[:, n0:n1], minus_half[:, 0:n1 - n0], ALU.pow).then_inc(sem("rstd_ready_a"), 1)

            def power_r(l, b):
                k = TOP if l == 0 else 1
                pool.wait_ge(sem("var_ready_r"), nth(l, b))
                g.tensor_tensor(rstd_r[:, b, 0:k, :], var_r[:, b, 0:k, :], minus_half[:, 0:k * TB].rearrange("p (k t) -> p k t", k=k),
                                ALU.pow).then_inc(sem("rstd_ready_r"), 1)

            g.memset(ident[:, :], 0.0).then_inc(sem("const_step"), 1)
            pool.wait_ge(sem("const_step"), 1)
            g.affine_select(out=ident[:, :], in_=ident[:, :], compare_op=ALU.not_equal, fill=1.0, base=0,
                            pattern=[[-1, P]], channel_multiplier=1).then_inc(sem("ident_ready"), 1)
            g.memset(ones_f[:, :], 1.0)
            g.memset(v_wide[:, :, :, :], 0.0).then_inc(sem("v_cleared"), 1)
            g.memset(minus_half[:, :], -0.5).then_inc(sem("const_step"), 1)
            pool.wait_ge(sem("const_step"), 2)
            power_a(1, 0, TB)
            g.memset(ones_b[:, :], 1.0)
            g.memset(earlier[:, :], 1.0)
            g.memset(head_mask[:, :], 1.0)
            g.memset(zero_i[:, :], 0)
            g.memset(row[:, :, :, D:], 0.0)
            g.memset(v_head[:, :, :, :], 0.0).then_inc(sem("v_cleared"), 1)
            g.memset(pad_tile[:, :], 0.0).then_inc(sem("const_step"), 1)
            pool.wait_ge(sem("const_step"), 3)
            g.iota(desc[:, :], pattern=[[-1, E]], base=E, channel_multiplier=0, allow_small_or_imprecise_dtypes=True)
            g.iota(region_at[:, :], pattern=[[REGION, E]], base=0, channel_multiplier=0, allow_small_or_imprecise_dtypes=True)
            g.iota(tile_no[:, :], pattern=[[1, MAP]], base=0, channel_multiplier=0, allow_small_or_imprecise_dtypes=True)
            power_a(2, TB, NT)
            g.affine_select(out=earlier[:, :], in_=earlier[:, :], compare_op=ALU.is_gt, fill=0.0, base=0,
                            pattern=[[1, P]], channel_multiplier=-1).then_inc(sem("consts_ready"), 1)
            g.iota(pad_tile[:, AT_DEST:AT_DEST + 1].bitcast(I32), pattern=[[0, 1]], base=NOWHERE,
                   channel_multiplier=0).then_inc(sem("pad_tile_ready"), 2)
            for k in range(TOP):
                g.iota(row[:, :, k, AT_DEST:AT_DEST + 1].bitcast(I32), pattern=[[P, NT], [0, 1]], base=k * TOKENS,
                       channel_multiplier=1)
            g.affine_select(out=head_mask[:, :], in_=head_mask[:, :], compare_op=ALU.is_ge, fill=0.0, base=0,
                            pattern=[[-HD, HEADS]], channel_multiplier=1).then_inc(sem("const_step"), 1)
            pool.wait_ge(sem("const_step"), 4)
            g.affine_select(out=head_mask[:, :], in_=head_mask[:, :], compare_op=ALU.is_ge, fill=0.0, base=HD - 1,
                            pattern=[[HD, HEADS]], channel_multiplier=-1).then_inc(sem("const_step"), 1)
            pool.wait_ge(sem("const_step"), 5)
            power_r(0, 0)
            pool.wait_ge(sem("kT_ready"), 2)
            for b in range(BATCHES):
                m = g.tensor_tensor(k_wide[:, b, :, :], kT[:, 1, KEYS * b:KEYS * (b + 1)].unsqueeze(1).broadcast_to([P, HEADS, KEYS]),
                                    head_mask[:, :].unsqueeze(2).broadcast_to([P, HEADS, KEYS]), ALU.mult)
            m.then_inc(sem("k_wide_ready"), 1)

            last_place = pool.to_reg(TOP * TOKENS - 1)

            def scatter_ffn(l):
                before = l * FFN_TILES
                def copy_meta(i, c):
                    j, s = UNROLL * i + c, c % UNROLL
                    pool.wait_ge(sem(f"xs_loaded_{s}"), 16 * (loads_before(l, s) + i + c // UNROLL + 1))
                    if reached(j, UNROLL):
                        pool.wait_ge(sem("y_gated"), before + j - UNROLL + 1)
                        pool.wait_ge(sem(f"y_sent_{s}"), 16 * (loads_before(l, s) + i + c // UNROLL))
                    g.tensor_tensor(meta[:, s, :].bitcast(I32), xs[:, s, AT_DEST:AT_DEST + 2].bitcast(I32), zero_i[:, :], ALU.add)\
                        .then_inc(sem("meta_ready"), 1)

                def send(i, c):
                    j, s = UNROLL * i + c, c % UNROLL
                    pool.wait_ge(sem("meta_ready"), before + j + 1)
                    pool.wait_ge(sem("y_gated"), before + j + 1)
                    g.tensor_tensor(pool_carrier[:, s, :], zero_i[:, :], zero_i[:, :], ALU.add)
                    pool.indirect_dma_start(
                        out=contrib[l], out_offset=bass.IndirectOffsetOnAxis(ap=meta[:, s, 0:1].bitcast(I32), axis=0),
                        in_=y_out[:, s, :], in_offset=None, bounds_check=last_place, oob_is_err=False)\
                        .then_inc(sem(f"y_sent_{s}"), 16)

                def body(i, c):
                    j = UNROLL * i + c
                    if not isinstance(j, int) or j + 1 < FFN_TILES:
                        copy_meta(i, c + 1)
                    send(i, c - 1)

                copy_meta(0, 0)
                copy_meta(0, 1)
                for j in range(1, UNROLL + 1):
                    body(0, j)
                with pool.Fori(1, LOOPS) as i:
                    for c in range(1, UNROLL + 1):
                        body(i, c)
                for j in range(UNROLL * LOOPS + 1, FFN_TILES + 1):
                    body(LOOPS, j - UNROLL * LOOPS)

            def scatter_rows(l, b, t0, t1):
                pool.wait_ge(sem("slots_ready"), nth(l, b))
                pool.wait_ge(sem("rows_copied"), nth(l, b))
                pool.wait_ge(sem("rows_gated"), nth(l, b))
                for t in range(t0, t1):
                    for k in range(TOP):
                        pool.indirect_dma_start(
                            out=sent[l], out_offset=bass.IndirectOffsetOnAxis(ap=slot[:, b, k, t:t + 1], axis=0),
                            in_=row[:, TB * b + t, k, :], in_offset=None).then_inc(sem("rows_sent"), 16)

            def sum_back0(b):
                pool.wait_ge(sem(f"back_{b}"), 16 * TOP)
                g.tensor_tensor(back[:, b, 0, :, :], back[:, b, 0, :, :], back[:, b, 1, :, :], ALU.add).then_inc(sem("back_summed"), 1)

            SPLIT = (TB - 1, TB // 2)
            for l in range(2):
                if l == 1:
                    sum_back0(0)
                    for b in range(BATCHES):
                        if b + 1 < BATCHES:
                            sum_back0(b + 1)
                        power_a(2 + b + 1, TB * b, TB * (b + 1))
                    power_r(1, 0)
                power_r(l, 1)
                if l == 1:
                    power_r(l, 2)
                for b in range(BATCHES):
                    scatter_rows(l, b, 0, SPLIT[l])
                    if b + 2 + l < BATCHES:
                        power_r(l, b + 2 + l)
                    scatter_rows(l, b, SPLIT[l], TB)
                scatter_ffn(l)

        @block.tensor
        def _(pe):
            mm = nc.tensor.matmul

            def warm_up(n, dst):
                for _ in range(n):
                    mm(dst[:, :].rearrange("p (o q) -> p o q", o=4), nothing[:, :], nothing[:, :].unsqueeze(1).broadcast_to([P, 4, P]),
                       start=True, stop=True)

            def meanwhile(n, dst, lag):
                return (lambda b: warm_up(n, dst), lag)

            def keys(l, dst):
                mm(dst[:, 0:P], wk[l][:, :], ctxT[:, :], start=True, stop=True).then_inc(sem("k_ready"), 1)

            def values(l, dst):
                mm(dst[:, :].rearrange("p (b d) -> p b d", b=BATCHES), ones_f[0:1, :],
                   bias_row[0:1, l:l + 1, :].broadcast_to([1, BATCHES, D]), start=True, stop=False)
                for b in range(BATCHES):
                    m = mm(dst[:, D * b:D * (b + 1)], ctxT4[:, b, :, :].rearrange("c g k -> c (g k)"),
                           wv[l][:, :], start=False, stop=(b == BATCHES - 1))
                m.then_inc(sem("v_ready"), 1)

            def setup():
                pe.wait_ge(sem("nothing_ready"), 1)
                warm_up(6, bank[7])
                pe.wait_ge(sem("ident_ready"), 1)
                pe.wait_ge(sem("ctx_loaded"), 16)
                nc.tensor.transpose(bank[1][0:CTX, 0:P], ctx_sb[:, :], ident[:, :]).then_inc(sem("ctx_turned"), 1)
                warm_up(8, bank[7])
                pe.wait_ge(sem("first_loaded"), 16 * (N_FIRST + 1))
                nc.tensor.transpose(bank[0][:, 0:N_FIRST], first_rows[:, :], ident[0:N_FIRST, 0:N_FIRST]).then_inc(sem("cols_turned"), 1)
                pe.wait_ge(sem("ctxT_ready"), 2)
                pe.wait_ge(sem("v_cleared"), 1)
                pe.wait_ge(sem("attn_loaded0"), 16 * 3)
                keys(0, bank[2])
                values(0, bank[3])
                pe.wait_ge(sem("cols_ready"), 1)

            def turn(n, l, b, src, dst):
                pe.wait_ge(sem(f"z_ready_{n}"), nth(l, b))
                for t in range(TB):
                    m = nc.tensor.transpose(dst[:, P * t:P * (t + 1)], src[:, t, :], ident[:, :])
                m.then_inc(sem(f"z_turned_{n}"), 1)

            def turn_a0(b):
                turn("a", 0, b, z_a, bank[0])

            def project_q0(b):
                pe.wait_ge(sem("zT_copied_a"), nth(0, b))
                mm(bank[1][:, :], wq[0][:, :], zT_a[:, :], start=True, stop=True).then_inc(sem("q_done"), 1)

            def scores0(b):
                pe.wait_ge(sem("qT_copied"), nth(0, b))
                pe.wait_ge(sem("kT_ready"), 1)
                for t in range(TB):
                    m = mm(bank[2][:, KEYS * t:KEYS * (t + 1)], qT[:, b % 2, P * t:P * (t + 1)], kT[:, 0, KEYS * b:KEYS * (b + 1)],
                           start=True, stop=True)
                m.then_inc(sem("scores_done0"), 1)

            def turn_probs0(b):
                if b == 0:
                    pe.wait_ge(sem("v_wide_ready"), 1)
                pe.wait_ge(sem("probs_ready0"), b + 1)
                nc.tensor.transpose(bank[3][:, 0:P], shifted[:, :, :].rearrange("p t k -> p (t k)"), ident[:, :])\
                    .then_inc(sem("probs_turned0"), 1)

            def attend0(b):
                pe.wait_ge(sem("probsT_copied0"), b + 1)
                mm(bank[4][:, :], probsT[:, :], v_wide[:, b, :, :].rearrange("p t d -> p (t d)"), start=True, stop=True)\
                    .then_inc(sem("att_done"), 1)

            def turn_r(l, b):
                turn("r", l, b, z_r[:, b % 2, :, :], bank[5])

            def logits(l, b):
                pe.wait_ge(sem("zT_copied_r"), nth(l, b))
                if l == 0:
                    pe.wait_ge(sem("router_loaded0"), 16 * 2)
                feat, w = zT_r, wg
                if l == 1:
                    pe.wait_ge(sem("router_silu"), b + 1)
                    feat, w = hidT, rw2
                for t in range(TB):
                    m = mm(bank[LOGITS[l]][:, E * t:E * (t + 1)], feat[:, P * t:P * (t + 1)], w[:, :], start=True, stop=True)
                m.then_inc(sem("logits_done"), 1)

            def hidden1(b):
                pe.wait_ge(sem("zT_copied_r"), nth(1, b))
                mm(bank[0][:, :], rw1[:, :], zT_r[:, :], start=True, stop=True).then_inc(sem("router_hidden"), 1)

            def rank(l, b):
                pe.wait_ge(sem("picked_ready"), nth(l, b))
                pe.wait_ge(sem("consts_ready"), 1)
                rank = bank[6][:, 64:64 + TB * E]
                chosen = picked[:, :, :].rearrange("p t e -> p (t e)")
                mm(rank, earlier[:, :], chosen, start=True, stop=False)
                for s in range(1, TB):
                    mm(rank[:, E * s:], ones_b[:, :], chosen[:, 0:E * (TB - s)], start=False, stop=False)
                mm(rank.rearrange("p (t e) -> p t e", e=E), ones_b[:, :], picked_before[:, :].unsqueeze(1).broadcast_to([P, TB, E]),
                   start=False, stop=True).then_inc(sem("rank_done"), 1)

            def count_experts(l):
                pe.wait_ge(sem("picked_summed"), nth(l, BATCHES - 1))
                pe.wait_ge(sem("rank_read"), nth(l, BATCHES - 1))
                mm(bank[6][:, 0:E], ones_b[:, :], picked_before[:, :], start=True, stop=True).then_inc(sem("counts_done"), 1)

            def prepare(b):
                if b == 0:
                    pe.wait_ge(sem("attn_loaded1"), 16 * 4)
                    pe.wait_ge(sem("ctx_mean_ready"), 1)
                    pe.wait_ge(sem("small_loaded"), 16 * N_SMALL_DMAS)
                    mm(bank[5][:, P:P + BATCHES], wv[1][:, :], ctx_mean[:, :], start=True, stop=True)
                    keys(1, bank[5])
                    nc.tensor.transpose(bank[6][:, 0:N_SMALL], small_rows[:, :], ident[0:N_SMALL, 0:N_SMALL]).then_inc(sem("cols_turned"), 1)

            def finish_preparing():
                values(1, bank[0])
                for n in range(BATCHES):
                    m = mm(bank[1][0:1, D * n:D * (n + 1)], v_mean[:, n:n + 1], wo[:, :], start=True, stop=True)
                m.then_inc(sem("even_row_done"), 1)

            def ffn(l):
                before = l * FFN_TILES
                def turn_rows(i, c):
                    j, s = UNROLL * i + c, c % UNROLL
                    pe.wait_ge(sem(f"xs_loaded_{s}"), 16 * (loads_before(l, s) + i + c // UNROLL + 1))
                    if reached(j, 2):
                        pe.wait_ge(sem("xT_ready"), before + j - 1)
                    nc.tensor.transpose(bank[c % 2][:, 0:P], xs[:, s, 0:D], ident[:, :]).then_inc(sem("x_turned"), 1)

                def up(i, c):
                    j, h = UNROLL * i + c, c % 2
                    pe.wait_ge(sem("xT_ready"), before + j + 1)
                    pe.wait_ge(sem("staged"), before + j + 1)
                    if reached(j, 2):
                        pe.wait_ge(sem("hid_biased"), before + j - 1)
                    for f in range(FC):
                        m = mm(bank[2 + h][:, P * f:P * (f + 1)], staged[:, c % STAGED, P * f:P * (f + 1)], xT[:, h, :],
                               start=True, stop=True)
                    m.then_inc(sem("up_done"), 1)

                def down(i, c):
                    j, h = UNROLL * i + c, c % 2
                    e = pe.value_load(expert[0:1, one(j)], min_val=0, max_val=E - 1)
                    pe.wait_ge(sem("hid_ready"), before + j + 1)
                    if reached(j, 2):
                        pe.wait_ge(sem("y_biased"), before + j - 1)
                    for f in range(FC):
                        m = mm(bank[4 + h][:, 0:D], hid[:, h, P * f:P * (f + 1)],
                               w2[l][:, one(e), f, :].rearrange("p o d -> p (o d)"), start=(f == 0), stop=(f == FC - 1))
                    m.then_inc(sem("down_done"), 1)

                def body(i, c):
                    j = UNROLL * i + c
                    if not isinstance(j, int) or j + 1 < FFN_TILES:
                        turn_rows(i, c + 1)
                    if not isinstance(j, int) or j < FFN_TILES:
                        up(i, c)
                    if reached(j, 1):
                        down(i, c - 1)

                turn_rows(0, 0)
                for j in range(UNROLL + 1):
                    body(0, j)
                with pe.Fori(1, LOOPS) as i:
                    for c in range(1, UNROLL + 1):
                        body(i, c)
                for j in range(UNROLL * LOOPS + 1, FFN_TILES + 1):
                    body(LOOPS, j - UNROLL * LOOPS)

            def turn_a1(b):
                turn("a", 1, b, z_a, bank[0])

            def project_q1(b):
                pe.wait_ge(sem("zT_copied_a"), nth(1, b))
                mm(bank[0][:, :], wq[1][:, :], zT_a[:, :], start=True, stop=True).then_inc(sem("q_done"), 1)

            def scores1(n):
                b, t = divmod(n, TB)
                if n >= 2:
                    pe.wait_ge(sem("nan_seen"), n - 1)
                pe.wait_ge(sem("qT_copied"), nth(1, b))
                pe.wait_ge(sem("k_wide_ready"), 1)
                mm(bank[2 + n % 2][:, :], qT[:, b % 2, P * t:P * (t + 1)], k_wide[:, b, :, :].rearrange("p h k -> p (h k)"),
                   start=True, stop=True).then_inc(sem("scores_done1"), 1)

            def turn_probs1(n):
                pe.wait_ge(sem("exp_done1"), n + 1)
                for c in range(TB):
                    m = nc.tensor.transpose(bank[4 + n % 2][:, P * c:P * (c + 1)],
                                            sc[:, n % 2, GROUP * c:GROUP * (c + 1), :].rearrange("p h k -> p (h k)"), ident[:, :])
                m.then_inc(sem("p_turned1"), 1)

            def weigh(n):
                pe.wait_ge(sem("pT_copied1"), n + 1)
                if n >= 2:
                    pe.wait_ge(sem("att_ready1"), n - 1)
                w = GROUP * (HD + 1)
                for c in range(TB):
                    m = mm(bank[WEIGHED[n % 2]][:, w * c:w * (c + 1)], pT[:, n % 2, P * c:P * (c + 1)],
                           v_head[:, n // TB, GROUP * c:GROUP * (c + 1), :].rearrange("p h d -> p (h d)"), start=True, stop=True)
                m.then_inc(sem("weighed1"), 1)

            def turn_att1(b):
                pe.wait_ge(sem("att_ready1"), TB * (b + 1))
                if b >= 1:
                    pe.wait_ge(sem("attT_copied1"), b)
                for t in range(TB):
                    m = nc.tensor.transpose(bank[6][:, P * t:P * (t + 1)], att[:, b % 2, t, :], ident[:, :])
                m.then_inc(sem("att_turned1"), 1)

            def attention1():
                pe.wait_ge(sem("v_head_ready"), 2)
                turn_a1(0)
                warm_up(2, bank[2])
                project_q1(0)
                warm_up(2, bank[2])
                scores1(0)
                scores1(1)
                warm_up(8, bank[7])
                for n in range(NT):
                    b, t = divmod(n, TB)
                    if n + 2 < NT:
                        scores1(n + 2)
                    else:
                        pe.wait_ge(sem("nan_seen"), n + 1)
                        warm_up(6, bank[2 + n % 2])
                    if n >= 1:
                        weigh(n - 1)
                    if t == 0 and b + 1 < BATCHES:
                        turn_a1(b + 1)
                    if t == 1 and b + 1 < BATCHES:
                        project_q1(b + 1)
                    turn_probs1(n)
                    if t == 2 and b >= 1:
                        turn_att1(b - 1)
                pe.wait_ge(sem("nan_seen"), NT)
                mm(bank[0][:, 0:NT], ones_f[:, :], nan_seen[:, :], start=True, stop=True).then_inc(sem("nan_summed"), 1)
                weigh(NT - 1)
                warm_up(6, bank[2])
                output1(0)
                turn_att1(BATCHES - 1)

            def output1(b):
                pe.wait_ge(sem("out_bias_ready"), 1)
                pe.wait_ge(sem("att_kept1"), b + 1)
                out = bank[4 - b % 2]
                mm(out[:, :].rearrange("p (t d) -> p t d", t=TB), ones_f[0:1, :], out_bias[0:1, b:b + 1, :].broadcast_to([1, TB, D]),
                   start=True, stop=False)
                for t in range(TB):
                    m = mm(out[:, D * t:D * (t + 1)], attT[:, b, t, :], wo[:, :], start=False, stop=(t == TB - 1))
                m.then_inc(sem("att_done"), 1)

            setup()
            idle = bank[7]
            steps((turn_probs0, 1), meanwhile(2, idle, 1),
                  (attend0, 1),
                  (lambda b: turn_r(0, b), 2),
                  (lambda b: logits(0, b), 2), meanwhile(2, idle, 2),
                  (turn_a0, 0),
                  (project_q0, 0), meanwhile(5, idle, 2),
                  (lambda b: rank(0, b), 2), meanwhile(2, idle, 0),
                  (scores0, 0),
                  (prepare, 1), meanwhile(8, idle, 1))
            count_experts(0)
            finish_preparing()
            pe.wait_ge(sem("v_head_ready"), 2)
            pe.wait_ge(sem("even_row_ready"), 1)
            pe.wait_ge(sem("w2_loaded0"), 16 * 2)
            pe.wait_ge(sem("rows_sent"), 16 * TOP * NT)
            warm_up(6, bank[2])
            ffn(0)
            pe.wait_ge(sem("back_summed"), 1)
            warm_up(10, bank[2])
            attention1()
            pe.wait_ge(sem("router_loaded1"), 16 * 3)
            idle = bank[2]
            output1(1)
            warm_up(5, idle)
            output1(2)
            warm_up(2, idle)
            steps((lambda b: turn_r(1, b), 0), meanwhile(2, idle, 0),
                  (lambda b: rank(1, b), 1),
                  (lambda b: output1(3) if b == 1 else None, 0),
                  (hidden1, 0), meanwhile(3, idle, 0),
                  (lambda b: logits(1, b), 0), meanwhile(6, idle, 0))
            count_experts(1)
            pe.wait_ge(sem("w2_loaded1"), 16 * 2)
            pe.wait_ge(sem("rows_sent"), 16 * 2 * TOP * NT)
            warm_up(6, bank[2])
            ffn(1)

        @block.scalar
        def _(act):
            s = nc.scalar
            first = [(R_BK[0], 1, vec(a["L0_xattn_bk"])), (R_BQ[0], 1, vec(a["L0_xattn_bq"]))]
            for r, n, src in first:
                act.dma_start(first_rows[r - R_BK[0]:r - R_BK[0] + n, :], src).then_inc(sem("first_loaded"), 16)
            act.dma_start(bias_row[0:1, 0, :], vec(a["L0_xattn_bv"])).then_inc(sem("first_loaded"), 16)
            act.wait_ge(sem("ident_ready"), 1)
            s.activation(act_start[:, :], ident[:, 0:1], ACT.Exp)

            def normalise_a0(b):
                act.wait_ge(sem("shift_ready_a"), 1 if b == 0 else 2)
                for t in range(TB):
                    n = TB * b + t
                    m = s.activation(z_a[:, t, :], x_sb[:, n, :], ACT.Identity, scale=rstd[:, n:n + 1], bias=shift_a[:, n:n + 1])
                m.then_inc(sem("z_ready_a"), 1)

            def spread_v_wide(b):
                if b > 0:
                    return
                act.wait_ge(sem("v_cleared"), 1)
                act.wait_ge(sem("v_ready"), 1)
                for r in range(GROUP):
                    p = slice(KEYS * r, KEYS * (r + 1))
                    m = s.copy(v_wide[p, :, r, :], bank[3][p, :].rearrange("p (b d) -> p b d", b=BATCHES))
                m.then_inc(sem("v_wide_ready"), 1)

            def spread_v_head():
                act.wait_ge(sem("v_cleared"), 2)
                act.wait_ge(sem("v_ready"), 2)
                for r in range(GROUP):
                    p = slice(KEYS * r, KEYS * (r + 1))
                    m = s.copy(v_head[p, :, r::GROUP, 0:HD], bank[0][p, :].rearrange("p (b h d) -> p b h d", b=BATCHES, d=HD)[:, :, r::GROUP, :])
                m.then_inc(sem("v_head_ready"), 1)

            def copy_zT(n, l, b, dst, src):
                act.wait_ge(sem(f"z_turned_{n}"), nth(l, b))
                s.copy(dst[:, :], src[:, :]).then_inc(sem(f"zT_copied_{n}"), 1)

            def add_bq(l, b):
                act.wait_ge(sem("q_done"), nth(l, b))
                s.activation(qT[:, b % 2, :], bank[1 - l][:, :], ACT.Identity, bias=col[:, R_BQ[l]:R_BQ[l] + 1]).then_inc(sem("qT_copied"), 1)

            def exp0(b):
                act.wait_ge(sem("shifted0"), b + 1)
                s.activation(shifted[:, :, :], shifted[:, :, :], ACT.Exp).then_inc(sem("exp_done0"), 1)

            def copy_probsT0(b):
                act.wait_ge(sem("probs_turned0"), b + 1)
                s.copy(probsT[:, :], bank[3][:, 0:P]).then_inc(sem("probsT_copied0"), 1)

            def copy_rows(l, b):
                act.wait_ge(sem("z_ready_r"), nth(l, b))
                for t in range(TB):
                    n = TB * b + t
                    if l == 0:
                        m = s.activation(row[:, n, :, 0:D], x_sb[:, n:n + 1, :].broadcast_to([P, TOP, D]), ACT.Identity,
                                         bias=shift_r[:, b, t:t + 1], scale=rstd_r[:, b, 1, t:t + 1])
                    else:
                        m = s.copy(row[:, n, :, 0:D], z_r[:, b % 2, t:t + 1, :].broadcast_to([P, TOP, D]))
                m.then_inc(sem("rows_copied"), 1)

            def silu1(b):
                act.wait_ge(sem("router_hidden"), b + 1)
                s.activation(hidT[:, :], bank[0][:, :], ACT.Silu, bias=col[:, R_RB1:R_RB1 + 1]).then_inc(sem("router_silu"), 1)

            def ratio_of(l, b):
                act.wait_ge(sem("gap_ready"), nth(l, b))
                s.activation(ratio[:, :], gap[:, :], ACT.Exp).then_inc(sem("ratio_ready"), 1)

            def ffn(l):
                before = l * FFN_TILES
                func = [ACT.Gelu_apprx_tanh, ACT.Silu][l]

                def copy_xT(i, c):
                    j, h = UNROLL * i + c, c % 2
                    act.wait_ge(sem("x_turned"), before + j + 1)
                    if reached(j, 2):
                        act.wait_ge(sem("up_done"), before + j - 1)
                    if l == 0:
                        act.wait_ge(sem("staged"), before + j + 1)
                        m = s.activation(xT[:, h, :], bank[h][:, 0:P], ACT.Identity, scale=staged[:, c % STAGED, AT_NORM:AT_NORM + 1],
                                         bias=staged[:, c % STAGED, AT_NORM + 1:AT_NORM + 2])
                    else:
                        m = s.copy(xT[:, h, :], bank[h][:, 0:P])
                    m.then_inc(sem("xT_ready"), 1)

                def activate(i, c):
                    j, h = UNROLL * i + c, c % 2
                    act.wait_ge(sem("hid_biased"), before + j + 1)
                    s.activation(hid[:, h, :], hid[:, h, :], func).then_inc(sem("hid_ready"), 1)

                def apply_gate(i, c):
                    j, q = UNROLL * i + c, c % UNROLL
                    act.wait_ge(sem("y_biased"), before + j + 1)
                    act.wait_ge(sem("meta_ready"), before + j + 1)
                    if reached(j, UNROLL):
                        act.wait_ge(sem(f"y_sent_{q}"), 16 * (loads_before(l, q) + i + c // UNROLL))
                    s.activation(y_out[:, q, :], y_raw[:, c % 2, :], ACT.Copy, scale=meta[:, q, 1:2]).then_inc(sem("y_gated"), 1)

                def body(i, c):
                    j = UNROLL * i + c
                    if not isinstance(j, int) or j + 1 < FFN_TILES:
                        copy_xT(i, c + 1)
                    if not isinstance(j, int) or j < FFN_TILES:
                        activate(i, c)
                    if reached(j, 1):
                        apply_gate(i, c - 1)

                copy_xT(0, 0)
                for j in range(UNROLL + 1):
                    body(0, j)
                with act.Fori(1, LOOPS) as i:
                    for c in range(1, UNROLL + 1):
                        body(i, c)
                for j in range(UNROLL * LOOPS + 1, FFN_TILES + 1):
                    body(LOOPS, j - UNROLL * LOOPS)

            def load_back(l):
                for u in range(UNROLL):
                    act.wait_ge(sem(f"y_sent_{u}"), 16 * loads_before(l + 1, u))
                for b in range(BATCHES):
                    src = contrib[l][TOKENS + b * SEQ:TOKENS + (b + 1) * SEQ, :]
                    act.dma_start(back[:, b, 1, :, :], src.rearrange("(t p) d -> p t d", p=P)).then_inc(sem(f"back_{b}"), 16)

            def find_nan(n):
                act.wait_ge(sem("clipped1"), n + 1)
                if n >= 2:
                    act.wait_ge(sem("nan_seen"), n - 1)
                s.activation(nan_junk[:, n % 2, :], bank[2 + n % 2][:, :], ACT.Tanh, accum_out=nan_seen[:, n:n + 1])\
                    .then_inc(sem("nan_seen"), 1)

            def copy_pT(n):
                act.wait_ge(sem("p_turned1"), n + 1)
                s.copy(pT[:, n % 2, :], bank[4 + n % 2][:, :]).then_inc(sem("pT_copied1"), 1)

            def copy_attT(b):
                act.wait_ge(sem("att_turned1"), b + 1)
                s.copy(attT[:, b, :, :].rearrange("p t q -> p (t q)"), bank[6][:, :]).then_inc(sem("attT_copied1"), 1)

            def attention1():
                s.activation(act_start[:, :], ident[:, 0:1], ACT.Exp)
                copy_zT("a", 1, 0, zT_a, bank[0])
                add_bq(1, 0)
                for n in range(NT):
                    b, t = divmod(n, TB)
                    find_nan(n)
                    if n >= 1:
                        copy_pT(n - 1)
                    act.wait_ge(sem("shift_done1"), n + 1)
                    s.activation(sc[:, n % 2, :, :], sc[:, n % 2, :, :], ACT.Exp).then_inc(sem("exp_done1"), 1)
                    if t == 0 and b + 1 < BATCHES:
                        copy_zT("a", 1, b + 1, zT_a, bank[0])
                    if t == 1 and b + 1 < BATCHES:
                        add_bq(1, b + 1)
                    if t == 3 and b >= 1:
                        copy_attT(b - 1)
                copy_pT(NT - 1)
                copy_attT(BATCHES - 1)

            act.wait_ge(sem("cols_ready"), 1)
            normalise_a0(0)
            steps((copy_probsT0, 1),
                  (lambda b: copy_zT("r", 0, b, zT_r, bank[5]), 2),
                  (lambda b: copy_zT("a", 0, b, zT_a, bank[0]), 0),
                  (lambda b: copy_rows(0, b), 2),
                  (lambda b: add_bq(0, b), 0),
                  (spread_v_wide, 0),
                  (lambda b: ratio_of(0, b), 2),
                  (exp0, 0),
                  (lambda b: normalise_a0(b + 1) if b + 1 < BATCHES else None, 0))
            spread_v_head()
            ffn(0)
            load_back(0)
            attention1()
            steps((lambda b: copy_zT("r", 1, b, zT_r, bank[5]), 0), (lambda b: ratio_of(1, b), 1), (silu1, 0),
                  (lambda b: copy_rows(1, b), 0))
            ffn(1)
            load_back(1)

        @block.vector
        def _(dve):
            v = nc.vector

            dve_steps = [0]

            def then_wait(m):
                dve_steps[0] += 1
                m.then_inc(sem("dve_step"), 1)
                dve.wait_ge(sem("dve_step"), dve_steps[0])

            def per_tile(ap, n):
                return ap.unsqueeze(2).broadcast_to([P, TB, n])

            def stats_a(l, n0, n1):
                for n in range(n0, n1):
                    m = v.bn_stats(bn[:, n, :], x_sb[:, n, :])
                then_wait(m)
                for n in range(n0, n1):
                    m = v.bn_aggr(mv[:, n, :], bn[:, n, :])
                then_wait(m)
                v.tensor_scalar(var_eps[:, n0:n1], mv[:, n0:n1, 1], EPS, None, ALU.add).then_inc(sem("var_ready_a"), 1)

            def normalise_a(l, b, powers):
                dve.wait_ge(sem("rstd_ready_a"), powers)
                for t in range(TB):
                    n = TB * b + t
                    m = v.tensor_scalar(z_a[:, t, :], x_sb[:, n, :], mv[:, n, 0:1], rstd[:, n:n + 1], ALU.subtract, ALU.mult)
                m.then_inc(sem("z_ready_a"), 1)

            def setup():
                v.memset(nothing[:, :], 0.0).then_inc(sem("nothing_ready"), 1)
                dve.wait_ge(sem("ctx_turned"), 1)
                v.tensor_copy(ctxT[:, :], bank[1][0:CTX, 0:P]).then_inc(sem("ctxT_ready"), 1)
                v.tensor_copy(ctxT4[:, :, :, :], bank[1][0:CTX, 0:P].rearrange("c (b k) -> c b k", b=BATCHES)
                              .unsqueeze(2).broadcast_to([CTX, BATCHES, GROUP, KEYS])).then_inc(sem("ctxT_ready"), 1)
                dve.wait_ge(sem("x_first"), 16)
                stats_a(0, 0, TB)
                dve.wait_ge(sem("ctxT_ready"), 2)
                then_wait(v.tensor_reduce(ctx_mean[:, :], ctxT[:, :].rearrange("c (b k) -> c b k", b=BATCHES), AX.X, ALU.add))
                v.tensor_scalar(ctx_mean[:, :], ctx_mean[:, :], 1.0 / KEYS, None, ALU.mult).then_inc(sem("ctx_mean_ready"), 1)
                dve.wait_ge(sem("cols_turned"), 1)
                v.tensor_copy(col[:, N_SMALL:], bank[0][:, 0:N_FIRST]).then_inc(sem("cols_ready"), 1)
                shift_a0(0, TB, 1)
                dve.wait_ge(sem("k_ready"), 1)
                dve.wait_ge(sem("cols_ready"), 1)
                v.tensor_scalar(kT[:, 0, :], bank[2][:, 0:P], col[:, R_BK[0]:R_BK[0] + 1], SCALE[0], ALU.add, ALU.mult)\
                    .then_inc(sem("kT_ready"), 1)

            def prepare(b):
                if b == 0:
                    dve.wait_ge(sem("cols_turned"), 2)
                    v.tensor_copy(col[:, 0:N_SMALL], bank[6][:, 0:N_SMALL]).then_inc(sem("cols_ready"), 1)
                    dve.wait_ge(sem("cols_ready"), 2)
                    v.tensor_scalar(kT[:, 1, :], bank[5][:, 0:P], col[:, R_BK[1]:R_BK[1] + 1], SCALE[1], ALU.add, ALU.mult)\
                        .then_inc(sem("kT_ready"), 1)
                    v.tensor_scalar(v_mean[:, :], bank[5][:, P:P + BATCHES], col[:, R_BV:R_BV + 1], None, ALU.add)\
                        .then_inc(sem("v_mean_ready"), 1)
                    dve.wait_ge(sem("v_cleared"), 2)
                    for r in range(GROUP):
                        m = v.memset(v_head[KEYS * r:KEYS * (r + 1), :, r::GROUP, HD:HD + 1].rearrange("p b h o -> p b (h o)"), 1.0)
                    m.then_inc(sem("v_head_ready"), 1)
                    for l in range(2):
                        v.tensor_copy(table[l][:, :, AT_B1:AT_B2], col[:, R_B1[l]:R_B1[l] + E * FC].rearrange("p (e c) -> p e c", e=E))
                    v.tensor_copy(table[0][:, :, AT_NORM:], col[:, R_LNW:R_LNW + 2 * E].rearrange("p (k e) -> p e k", k=2))\
                        .then_inc(sem("table_filled"), 1)

            def finish_preparing():
                dve.wait_ge(sem("even_row_done"), 1)
                v.tensor_copy(even_row[:, :, :], bank[1][0:1, :].rearrange("o (b d) -> o b d", b=BATCHES)).then_inc(sem("even_row_ready"), 1)

            def stats_rest(b):
                if b == 0:
                    dve.wait_ge(sem("x_rest"), 16)
                    stats_a(0, TB, NT)

            def shift_a0(n0, n1, powers):
                dve.wait_ge(sem("rstd_ready_a"), powers)
                v.scalar_tensor_tensor(out=shift_a[:, n0:n1], in0=mv[:, n0:n1, 0], scalar=-1.0, in1=rstd[:, n0:n1],
                                       op0=ALU.mult, op1=ALU.mult).then_inc(sem("shift_ready_a"), 1)

            def shift_scores0(b):
                dve.wait_ge(sem("scores_done0"), b + 1)
                scores = bank[2][:, 0:TB * KEYS].rearrange("p (t k) -> p t k", k=KEYS)
                then_wait(v.tensor_reduce(top_score[:, :], scores, AX.X, ALU.max))
                v.tensor_tensor(shifted[:, :, :], scores, per_tile(top_score[:, :], KEYS), ALU.subtract).then_inc(sem("shifted0"), 1)

            def normalise_probs0(b):
                dve.wait_ge(sem("exp_done0"), b + 1)
                then_wait(v.tensor_reduce(prob_sum[:, :], shifted[:, :, :], AX.X, ALU.add))
                then_wait(v.reciprocal(prob_scale[:, :], prob_sum[:, :]))
                v.tensor_tensor(shifted[:, :, :], shifted[:, :, :], per_tile(prob_scale[:, :], KEYS), ALU.mult).then_inc(sem("probs_ready0"), 1)

            def add_attention(l, b):
                mine = x_sb[:, TB * b:TB * (b + 1), :]
                dve.wait_ge(sem("att_done"), nth(l, b))
                src = bank[4] if l == 0 else bank[4 - b % 2]
                then_wait(v.tensor_tensor(mine, mine, src[:, :].rearrange("p (t d) -> p t d", t=TB), ALU.add))
                for t in range(TB):
                    m = v.bn_stats(bn_r[:, t, :], x_sb[:, TB * b + t, :])
                then_wait(m)
                for t in range(TB):
                    m = v.bn_aggr(mv_r[:, b, t, :], bn_r[:, t, :])
                then_wait(m)
                m = v.tensor_scalar(var_r[:, b, 0, :], mv_r[:, b, :, 1], EPS, None, ALU.add)
                if l == 0:
                    m = v.tensor_scalar(var_r[:, b, 1, :], mv_r[:, b, :, 1], 1.0 + EPS, EPS * EPS, ALU.mult, ALU.add)
                m.then_inc(sem("var_ready_r"), 1)

            def normalise_r(l, b):
                dve.wait_ge(sem("rstd_ready_r"), nth(l, b))
                if l == 0:
                    v.scalar_tensor_tensor(out=shift_r[:, b, :], in0=mv_r[:, b, :, 0], scalar=-1.0, in1=rstd_r[:, b, 1, :],
                                           op0=ALU.mult, op1=ALU.mult)
                elif b >= 2:
                    dve.wait_ge(sem("rows_copied"), nth(1, b - 2))
                for t in range(TB):
                    m = v.tensor_scalar(z_r[:, b % 2, t, :], x_sb[:, TB * b + t, :], mv_r[:, b, t, 0:1], rstd_r[:, b, 0, t:t + 1],
                                        ALU.subtract, ALU.mult)
                m.then_inc(sem("z_ready_r"), 1)

            def add_normalised1(b):
                mine = x_sb[:, TB * b:TB * (b + 1), :]
                dve.wait_ge(sem("rows_copied"), nth(1, b))
                v.tensor_tensor(mine, mine, row[:, TB * b:TB * (b + 1), 0, 0:D], ALU.add).then_inc(sem("z_added1"), 1)

            def pick(l, b):
                bc_e = [P, TB, E]
                dve.wait_ge(sem("logits_done"), nth(l, b))
                lg = bank[LOGITS[l]][:, 0:TB * E].rearrange("p (t e) -> p t e", e=E)
                if l == 0:
                    then_wait(v.tensor_copy(logit[:, :, :], lg))
                else:
                    then_wait(v.tensor_tensor(logit[:, :, :], lg, rb2[:, :].unsqueeze(1).broadcast_to(bc_e), ALU.add))
                by_e = desc[:, :].unsqueeze(1).broadcast_to(bc_e)
                src = logit
                for k in range(TOP):
                    then_wait(v.tensor_reduce(best[:, k, :], src[:, :, :], AX.X, ALU.max))
                    then_wait(v.tensor_tensor(tied[:, :, :], src[:, :, :], per_tile(best[:, k, :], E), ALU.is_equal))
                    then_wait(v.tensor_tensor(tied[:, :, :], tied[:, :, :], by_e, ALU.mult))
                    then_wait(v.tensor_reduce(key[:, k, :], tied[:, :, :], AX.X, ALU.max))
                    then_wait(v.tensor_tensor(hot[:, k, :, :], by_e, per_tile(key[:, k, :], E), ALU.is_equal))
                    if k == 0:
                        then_wait(v.scalar_tensor_tensor(out=rest[:, :, :], in0=hot[:, 0, :, :], scalar=-BIG, in1=logit[:, :, :],
                                                         op0=ALU.mult, op1=ALU.add))
                        src = rest
                v.tensor_tensor(picked[:, :, :], hot[:, 0, :, :], hot[:, 1, :, :], ALU.add).then_inc(sem("picked_ready"), 1)
                v.tensor_tensor(gap[:, :], best[:, 1, :], best[:, 0, :], ALU.subtract).then_inc(sem("gap_ready"), 1)

            def place(l, b):
                alphas = alpha[:, :].unsqueeze(1).broadcast_to([P, TOP * TB, E])
                if l == 0:
                    v.tensor_tensor(alpha_hot[:, :, :, :].rearrange("p k t e -> p (k t) e"), hot[:, :, :, :].rearrange("p k t e -> p (k t) e"),
                                    alphas, ALU.mult).then_inc(sem("alpha_step"), 1)
                dve.wait_ge(sem("picked_ready"), nth(l, b))
                then_wait(v.tensor_reduce(picked_now[:, :], picked[:, :, :].rearrange("p t e -> p e t"), AX.X, ALU.add))
                dve.wait_ge(sem("rank_done"), nth(l, b))
                v.tensor_tensor(row_of[:, :, :], bank[6][:, 64:64 + TB * E].rearrange("p (t e) -> p t e", e=E),
                                region_at[:, :].unsqueeze(1).broadcast_to([P, TB, E]), ALU.add).then_inc(sem("rank_read"), 1)
                v.tensor_tensor(picked_before[:, :], picked_before[:, :], picked_now[:, :], ALU.add).then_inc(sem("picked_summed"), 1)
                dve.wait_ge(sem("rank_read"), nth(l, b))
                m = v.tensor_tensor(spread[:, :, :, :], hot[:, :, :, :], row_of[:, :, :].unsqueeze(1).broadcast_to([P, TOP, TB, E]), ALU.mult)
                dve.wait_ge(sem("ratio_ready"), nth(l, b))
                then_wait(v.tensor_scalar(total[:, :], ratio[:, :], 1.0, None, ALU.add))
                v.reciprocal(gate[:, 0, :], total[:, :]).then_inc(sem("gates"), 1)
                then_wait(v.tensor_reduce(slot_f[:, :, :], spread[:, :, :, :], AX.X, ALU.add))
                v.tensor_copy(slot[:, b, :, :], slot_f[:, :, :]).then_inc(sem("slots_ready"), 1)
                dve.wait_ge(sem("gates"), 2 * nth(l, b) - 2 + 1)
                v.tensor_tensor(gate[:, 1, :], gate[:, 0, :], ratio[:, :], ALU.mult).then_inc(sem("gates"), 1)
                out = row[:, TB * b:TB * (b + 1), :, AT_GATE]
                if l == 0:
                    dve.wait_ge(sem("alpha_step"), 2 * b + 1)
                    v.tensor_reduce(alpha_of[:, :, :], alpha_hot[:, :, :, :], AX.X, ALU.add).then_inc(sem("alpha_step"), 1)
                    dve.wait_ge(sem("alpha_step"), 2 * b + 2)
                dve.wait_ge(sem("gates"), 2 * nth(l, b) - 2 + 2)
                if l == 0:
                    v.tensor_tensor(out, gate[:, :, :].rearrange("p k t -> p t k"), alpha_of[:, :, :].rearrange("p k t -> p t k"), ALU.mult)\
                        .then_inc(sem("rows_gated"), 1)
                else:
                    v.tensor_copy(out, gate[:, :, :].rearrange("p k t -> p t k")).then_inc(sem("rows_gated"), 1)

            def map_tiles(l):
                by_tile = [P, MAP, E]
                dve.wait_ge(sem("counts_done"), l + 1)
                then_wait(v.tensor_copy(count[:, :], bank[6][:, 0:E]))
                v.tensor_tensor(pad_at[:, :], count[:, :], region_at[:, :], ALU.add).then_inc(sem("pad_known"), 1)
                then_wait(v.tensor_scalar(count_up[:, :], count[:, :], float(P - 1), None, ALU.add))
                then_wait(v.tensor_scalar(tiles_i[:, :], count_up[:, :], 7, None, ALU.arith_shift_right))
                then_wait(v.tensor_copy(tiles_f[:, :], tiles_i[:, :]))
                then_wait(v.tensor_tensor_scan(tiles_end[:, :], ones_f[:, 0:E], tiles_f[:, :], 0.0, ALU.mult, ALU.add))
                then_wait(v.tensor_tensor(passed[:, :, :], tiles_end[:, :].unsqueeze(1).broadcast_to(by_tile),
                                          tile_no[:, :].unsqueeze(2).broadcast_to(by_tile), ALU.is_le))
                then_wait(v.tensor_reduce(expert_f[:, :], passed[:, :, :], AX.X, ALU.add))
                then_wait(v.tensor_tensor(passed[:, :, :], passed[:, :, :], tiles_f[:, :].unsqueeze(1).broadcast_to(by_tile), ALU.mult))
                then_wait(v.tensor_reduce(first_f[:, :], passed[:, :, :], AX.X, ALU.add))
                then_wait(v.tensor_tensor(first_f[:, :], tile_no[:, :], first_f[:, :], ALU.subtract))
                then_wait(v.scalar_tensor_tensor(out=first_f[:, :], in0=expert_f[:, :], scalar=float(REGION // P), in1=first_f[:, :],
                                                 op0=ALU.mult, op1=ALU.add))
                v.tensor_scalar(row_base[:, :], first_f[:, :], float(P), float(PAD_ROW), ALU.mult, ALU.min)
                v.tensor_scalar(expert[:, :], expert_f[:, :], float(E - 1), None, ALU.min).then_inc(sem("map_ready"), 1)
                dve.wait_ge(sem("map_ready"), l + 1)

            def ffn(l):
                before = l * FFN_TILES
                def stage(i, c):
                    j = UNROLL * i + c
                    e = dve.value_load(expert[0:1, one(UNROLL * i + c)], min_val=0, max_val=E - 1)
                    if reached(j, STAGED):
                        dve.wait_ge(sem("y_biased"), before + j - STAGED + 1)
                    v.tensor_copy(staged[:, c % STAGED, 0:W_TABLE[l]], table[l][:, one(e), :].rearrange("p o f -> p (o f)")).then_inc(sem("staged"), 1)

                def add_b1(i, c):
                    j, h = UNROLL * i + c, c % 2
                    dve.wait_ge(sem("up_done"), before + j + 1)
                    dve.wait_ge(sem("staged"), before + j + 1)
                    if reached(j, 2):
                        dve.wait_ge(sem("down_done"), before + j - 1)
                    v.tensor_tensor(hid[:, h, :].rearrange("p (f q) -> p f q", f=FC), bank[2 + h][:, :].rearrange("p (f q) -> p f q", f=FC),
                                    staged[:, c % STAGED, AT_B1:AT_B2].unsqueeze(2).broadcast_to([P, FC, P]), ALU.add)\
                        .then_inc(sem("hid_biased"), 1)

                def add_b2(i, c):
                    j, h = UNROLL * i + c, c % 2
                    dve.wait_ge(sem("down_done"), before + j + 1)
                    if reached(j, 2):
                        dve.wait_ge(sem("y_gated"), before + j - 1)
                    v.tensor_tensor(y_raw[:, h, :], bank[4 + h][:, 0:D], staged[:, c % STAGED, AT_B2:AT_NORM], ALU.add)\
                        .then_inc(sem("y_biased"), 1)

                def body(i, c):
                    j = UNROLL * i + c
                    if not isinstance(j, int) or j < FFN_TILES:
                        add_b1(i, c)
                    if not isinstance(j, int) or j + 2 < FFN_TILES:
                        stage(i, c + 2)
                    if reached(j, 1):
                        add_b2(i, c - 1)

                stage(0, 0)
                stage(0, 1)
                for j in range(UNROLL + 1):
                    body(0, j)
                with dve.Fori(1, LOOPS) as i:
                    for c in range(1, UNROLL + 1):
                        body(i, c)
                for j in range(UNROLL * LOOPS + 1, FFN_TILES + 1):
                    body(LOOPS, j - UNROLL * LOOPS)

            def add_back(l, b):
                mine = x_sb[:, TB * b:TB * (b + 1), :]
                if l == 1:
                    dve.wait_ge(sem("z_added1"), b + 1)
                if l == 1:
                    dve.wait_ge(sem(f"back_{b}"), 16 * TOP * 2)
                    then_wait(v.tensor_tensor(mine, mine, back[:, b, 1, :, :], ALU.add))
                else:
                    dve.wait_ge(sem("back_summed"), b + 1)
                v.tensor_tensor(mine, mine, back[:, b, 0, :, :], ALU.add).then_inc(sem("added"), 1)

            def residual1(b):
                add_back(0, b)
                dve.wait_ge(sem("added"), nth(0, b))
                stats_a(1, TB * b, TB * (b + 1))

            def attention1():
                for n in range(NT + 3):
                    h = n % 2
                    b, t = divmod(n, TB)
                    if n >= 3:
                        divide(n - 3)
                    if n < NT:
                        scores = bank[2 + h][:, :].rearrange("p (h k) -> p h k", k=KEYS)
                        dve.wait_ge(sem("scores_done1"), n + 1)
                        if n == 0:
                            normalise_a(1, 1, 2 + 2)
                        if t == TB - 1 and b + 2 < BATCHES:
                            normalise_a(1, b + 2, 2 + b + 3)
                        then_wait(v.tensor_reduce(max_all[:, n, :], scores, AX.X, ALU.max))
                        then_wait(v.tensor_scalar(max_clip[:, n, :], max_all[:, n, :], -CLAMP, CLAMP, ALU.max, ALU.min))
                        if n >= 2:
                            dve.wait_ge(sem("p_turned1"), n - 1)
                        v.scalar_tensor_tensor(out=sc[:, h, :, :], in0=scores, scalar=-CLAMP,
                                               in1=max_clip[:, n, :].unsqueeze(2).broadcast_to([P, HEADS, KEYS]), op0=ALU.max, op1=ALU.subtract)\
                            .then_inc(sem("clipped1"), 1)
                        dve.wait_ge(sem("clipped1"), n + 1)
                        v.tensor_scalar(sc[:, h, :, :], sc[:, h, :, :], 0.0, None, ALU.min).then_inc(sem("shift_done1"), 1)
                        if n < BATCHES - 2:
                            residual1(n + 2)
                    if n == NT:
                        guard_against_nan()
                        keep_att1(0)

            def divide(n):
                dve.wait_ge(sem("weighed1"), n + 1)
                got = bank[WEIGHED[n % 2]][:, 0:HEADS * (HD + 1)].rearrange("p (h d) -> p h d", d=HD + 1)
                then_wait(v.reciprocal(head_scale[:, n % 2, :], got[:, :, HD]))
                v.tensor_tensor(att[:, n // TB % 2, n % TB, :].rearrange("p (h d) -> p h d", d=HD), got[:, :, 0:HD],
                                head_scale[:, n % 2, :].unsqueeze(2).broadcast_to([P, HEADS, HD]), ALU.mult).then_inc(sem("att_ready1"), 1)

            def guard_against_nan():
                dve.wait_ge(sem("nan_summed"), 1)
                then_wait(v.tensor_reduce(nan_sum[:, :], bank[0][:, 0:NT], AX.X, ALU.add))
                then_wait(v.tensor_tensor(all_numbers[:, :], nan_sum[:, :], nan_sum[:, :], ALU.is_equal))
                v.tensor_scalar(keep_bits[:, :], all_numbers[:, :], -1.0, None, ALU.mult)
                then_wait(v.tensor_scalar(guard[:, :], all_numbers[:, :], -1.0, 1.0, ALU.mult, ALU.add))
                dve.wait_ge(sem("even_row_ready"), 1)
                v.scalar_tensor_tensor(out=out_bias[:, :, :], in0=even_row[:, :, :], scalar=guard[0:1, 0:1],
                                       in1=bias_row[0:1, 2:3, :].broadcast_to([1, BATCHES, D]), op0=ALU.mult, op1=ALU.add)\
                    .then_inc(sem("out_bias_ready"), 1)

            def keep_att1(b):
                dve.wait_ge(sem("attT_copied1"), b + 1)
                mine = attT[:, b, :, :].rearrange("p t q -> p (t q)").bitcast(I32)
                v.tensor_tensor(mine, mine, keep_bits[:, :].broadcast_to([P, SEQ]), ALU.bitwise_and).then_inc(sem("att_kept1"), 1)

            setup()
            v.memset(picked_before[:, :], 0.0)
            dve.wait_ge(sem("router_loaded0"), 16 * 2)
            steps((normalise_probs0, 1),
                  (lambda b: normalise_r(0, b), 2),
                  (stats_rest, 0),
                  (lambda b: shift_a0(TB, NT, 2) if b == 0 else None, 0),
                  (lambda b: add_attention(0, b), 1),
                  (lambda b: pick(0, b), 2),
                  (lambda b: place(0, b), 2),
                  (shift_scores0, 0),
                  (prepare, 1))
            map_tiles(0)
            finish_preparing()
            dve.wait_ge(sem("table_filled"), 1)
            dve.wait_ge(sem("w1_loaded0"), 16)
            dve.wait_ge(sem("w2_loaded0"), 16 * 2)
            ffn(0)
            residual1(0)
            residual1(1)
            normalise_a(1, 0, 2 + 1)
            v.memset(picked_before[:, :], 0.0)
            attention1()
            dve.wait_ge(sem("router_loaded1"), 16 * 3)
            keep_att1(1)
            add_attention(1, 0)
            keep_att1(2)
            add_attention(1, 1)
            normalise_r(1, 0)
            keep_att1(3)
            add_attention(1, 2)
            steps((lambda b: normalise_r(1, b) if b > 0 else None, 0),
                  (lambda b: pick(1, b), 1), (lambda b: place(1, b), 1),
                  (lambda b: add_attention(1, 3) if b == 1 else None, 0))
            map_tiles(1)
            dve.wait_ge(sem("w1_loaded1"), 16)
            dve.wait_ge(sem("w2_loaded1"), 16 * 2)
            ffn(1)
            for b in range(BATCHES):
                add_normalised1(b)
            for b in range(BATCHES):
                add_back(1, b)



_INS = ['x', 'ctx_768', 'L0_xattn_Wq', 'L0_xattn_bq', 'L0_xattn_Wk', 'L0_xattn_bk', 'L0_xattn_Wv', 'L0_xattn_bv',
        'L0_ffn_Wg', 'L0_ffn_alpha', 'L0_ffn_ln_w', 'L0_ffn_ln_b', 'L0_ffn_fc1_w', 'L0_ffn_fc1_b', 'L0_ffn_fc2_w',
        'L0_ffn_fc2_b', 'L1_xattn_Wq', 'L1_xattn_bq', 'L1_xattn_Wk', 'L1_xattn_bk', 'L1_xattn_Wv', 'L1_xattn_bv',
        'L1_xattn_Wo', 'L1_xattn_bo', 'L1_ffn_rw1', 'L1_ffn_rb1', 'L1_ffn_rw2', 'L1_ffn_rb2', 'L1_ffn_we1',
        'L1_ffn_be1', 'L1_ffn_we2', 'L1_ffn_be2']


def kernel(**inputs):
    import numpy as _np
    import concourse.bacc as _bacc
    from concourse import mybir as _mybir
    from concourse.bass_utils import run_bass_kernel_spmd as _run

    nc = _bacc.Bacc("TRN2", target_bir_lowering=False, num_devices=1)
    arrays, aps = {}, {}
    for name in _INS:
        arr = _np.ascontiguousarray(inputs[name])
        arrays[f"in_{name}"] = arr
        aps[name] = nc.dram_tensor(f"in_{name}", arr.shape, _mybir.dt.from_np(arr.dtype), kind="ExternalInput").ap()
    out = nc.dram_tensor("out_0", (BATCHES, SEQ, D), F32, kind="ExternalOutput").ap()
    sent = [nc.dram_tensor(f"sent{l}", (PAD_ROW + P, W_ROW), F32, kind="Internal").ap() for l in range(2)]
    contrib = [nc.dram_tensor(f"contrib{l}", (TOP * TOKENS, D), F32, kind="Internal").ap() for l in range(2)]
    build(nc, aps, out, sent, contrib)
    r = _run(nc, [arrays], core_ids=[0])
    return r.results[0]["out_0"]
```
